# Optimizing a Trainium2 kernel written in Bass

```python
import numpy as np
import jax
import jax.numpy as jnp

def _softmax(x, axis=-1):
    return jax.nn.softmax(x, axis=axis)

def _gelu(x):
    return jax.nn.gelu(x, approximate=True)

def _silu(x):
    return jax.nn.silu(x)

def _sigmoid(x):
    return jax.nn.sigmoid(x)

def _layernorm(x, axis=-1, eps=1e-05):
    m = jnp.mean(x, axis=axis, keepdims=True)
    v = jnp.var(x, axis=axis, keepdims=True)
    return (x - m) / jnp.sqrt(v + eps)

def _scatter_add(tgt, idx, src, axis=0):
    return tgt.at[idx].add(src)

def _segment_sum(src, seg, n):
    return jax.ops.segment_sum(src, seg, n)
kernel_name = 'mk_xattn_ffn_d2_seqx_r8_6b7fc3'

def setup_inputs(seed: int=0):
    np.random.seed(seed)
    _w = jnp.asarray

    def _rec_inputs():
        import jax
        import jax.numpy as jnp
        _rk = jax.random.key(seed)
        x = -0.0002928 + 1 * jax.random.normal(jax.random.fold_in(_rk, 1), (8, 128, 256), jnp.float32)
        _lenS = 128 - jax.random.randint(jax.random.fold_in(_rk, 7), (8,), 0, max(1, 128 // 4) + 1, jnp.int32)
        _lenS2 = 128 - jax.random.randint(jax.random.fold_in(_rk, 8), (8,), 0, max(1, 128 // 4) + 1, jnp.int32)
        _ctx_2048P = jax.random.normal(jax.random.fold_in(_rk, 11), (8, 16, 256), jnp.float32)
        _ctx_2048c = jax.random.dirichlet(jax.random.fold_in(_rk, 511), 0.3 * jnp.ones((16,), jnp.float32), (8, 128))
        _ctx_2048t = jnp.einsum('bsk,bkd->bsd', _ctx_2048c, _ctx_2048P)
        _ctx_2048t = _ctx_2048t * jax.lax.rsqrt(jnp.mean(jnp.square(_ctx_2048t)) + 1e-12) * 0.953939
        ctx_2048 = -1.39393e-06 + 0.999914 * (_ctx_2048t + 0.3 * jax.random.normal(jax.random.fold_in(_rk, 611), (8, 128, 256), jnp.float32))
        _validS = jnp.arange(128)[None, :] < _lenS[:, None]
        _validS2 = jnp.arange(128)[None, :] < _lenS2[:, None]
        _causal = jnp.tril(jnp.ones((128, 128), dtype=bool))
        mask_Bx1x2048_fk1 = jnp.where(jnp.ones((8, 1, 256), dtype=bool), 1.0, 0.0).astype(jnp.float32)
        mask_Bx1xSxS_fk0 = jnp.where(jnp.broadcast_to(_validS[:, None, None, :], (8, 1, 128, 128)), -1000000000.0, 0.0).astype(jnp.float32)
        return (x, ctx_2048, mask_Bx1x2048_fk1, mask_Bx1xSxS_fk0)
    x, ctx_2048, mask_Bx1x2048_fk1, mask_Bx1xSxS_fk0 = _rec_inputs()

    def _L0_xattn_setup():
        import math
        import jax, jax.numpy as jnp
        import numpy as np
        SIZE = 128
        HEADS = 16
        HEAD_DIM = SIZE // HEADS
        B, T, S = (2, 256, 256)
        NEG = 1000000.0
        key = jax.random.key(seed)
        ks = jax.random.split(key, 10)
        target = jax.random.normal(ks[0], (B, SIZE, T), dtype=jnp.float32)
        source = jax.random.normal(ks[1], (B, SIZE, S), dtype=jnp.float32)
        target_mask = (jax.random.uniform(ks[2], (B, 1, T)) > 0.1).astype(jnp.float32)
        source_mask = (jax.random.uniform(ks[3], (B, 1, S)) > 0.1).astype(jnp.float32)
        scale = 1.0 / math.sqrt(SIZE)
        Wq = jax.random.normal(ks[4], (SIZE, SIZE), dtype=jnp.float32) * scale
        Wk = jax.random.normal(ks[5], (SIZE, SIZE), dtype=jnp.float32) * scale
        Wv = jax.random.normal(ks[6], (SIZE, SIZE), dtype=jnp.float32) * scale
        bq = jax.random.normal(ks[7], (SIZE,), dtype=jnp.float32) * 0.01
        bk = jax.random.normal(ks[8], (SIZE,), dtype=jnp.float32) * 0.01
        bv = jax.random.normal(ks[9], (SIZE,), dtype=jnp.float32) * 0.01
        return {'target': target, 'source': source, 'target_mask': target_mask, 'source_mask': source_mask, 'Wq': Wq, 'bq': bq, 'Wk': Wk, 'bk': bk, 'Wv': Wv, 'bv': bv}
    _L0_xattn_all = _L0_xattn_setup()
    _L0_xattn_in = {k: v for k, v in _L0_xattn_all.items() if k in ('Wq', 'bq', 'Wk', 'bk', 'Wv', 'bv')}
    del _L0_xattn_all

    def _L0_ffn_setup():
        import jax, jax.numpy as jnp
        import numpy as np
        B, S, H, E, I, TOPK = (1, 128, 256, 16, 128, 2)
        SCALE = 1.0
        key = jax.random.key(seed)
        k0, k1, k2, k3 = jax.random.split(key, 4)
        hidden_states = jax.random.normal(k0, (B, S, H), dtype=jnp.float32)
        gate_w = jax.random.normal(k1, (E, H), dtype=jnp.float32) * 0.02
        gate_up_proj = jax.random.normal(k2, (E, H, 2 * I), dtype=jnp.float32) / np.sqrt(H)
        down_proj = jax.random.normal(k3, (E, I, H), dtype=jnp.float32) / np.sqrt(I)
        return {'hidden_states': hidden_states, 'gate_w': gate_w, 'gate_up_proj': gate_up_proj, 'down_proj': down_proj}
    _L0_ffn_all = _L0_ffn_setup()
    _L0_ffn_in = {k: v for k, v in _L0_ffn_all.items() if k in ('gate_w', 'gate_up_proj', 'down_proj')}
    del _L0_ffn_all

    def _L1_xattn_setup():
        import jax, jax.numpy as jnp
        import numpy as np
        import math
        B, S, HID, H = (2, 256, 256, 32)
        D = HID // H
        AL = 10

        def _rope_tables(seq_len, dim, dtype):
            inv_freq = 1.0 / 10000.0 ** (np.arange(0, dim, 2, dtype=np.float32) / dim)
            t = np.arange(seq_len, dtype=np.float32)
            freqs = np.outer(t, inv_freq)
            emb = np.concatenate([freqs, freqs], -1)
            return (jnp.asarray(np.cos(emb), dtype), jnp.asarray(np.sin(emb), dtype))

        def _rotate_half(x):
            x1, x2 = jnp.split(x, 2, axis=-1)
            return jnp.concatenate([-x2, x1], axis=-1)
        key = jax.random.key(seed)
        ks = jax.random.split(key, 8)
        hidden_states = jax.random.normal(ks[0], (B, S, HID), dtype=jnp.float32)
        adapter = jax.random.normal(ks[1], (B, AL, HID), dtype=jnp.float32)
        causal = jnp.tril(jnp.ones((S, S), dtype=bool))
        attention_mask = jnp.broadcast_to(jnp.where(causal, 0.0, -1000000000.0).astype(jnp.float32)[None, None], (B, 1, S, S))
        scale = 0.02
        Wq = jax.random.normal(ks[2], (HID, HID), dtype=jnp.float32) * scale
        Wk = jax.random.normal(ks[3], (HID, HID), dtype=jnp.float32) * scale
        Wv = jax.random.normal(ks[4], (HID, HID), dtype=jnp.float32) * scale
        Wo = jax.random.normal(ks[5], (HID, HID), dtype=jnp.float32) * scale
        gate = jax.random.normal(ks[6], (1, H, 1, 1), dtype=jnp.float32) * 0.1
        return {'hidden_states': hidden_states, 'attention_mask': attention_mask, 'adapter': adapter, 'Wq': Wq, 'Wk': Wk, 'Wv': Wv, 'Wo': Wo, 'gate': gate}
    _L1_xattn_all = _L1_xattn_setup()
    _L1_xattn_in = {k: v for k, v in _L1_xattn_all.items() if k in ('Wq', 'Wk', 'Wv', 'Wo', 'gate')}
    del _L1_xattn_all

    def _L1_ffn_setup():
        import math
        import jax, jax.numpy as jnp
        import numpy as np
        NUM_EXPERTS = 8
        HIDDEN = 256
        INTER = 1024
        CAP_FACTOR = 1.25
        MIN_CAP = 4
        B, S = (4, 256)

        def _capacity(num_tokens: int, num_experts: int) -> int:
            cap = math.floor(CAP_FACTOR * num_tokens / num_experts)
            cap += cap % 2
            return max(cap, MIN_CAP)
        key = jax.random.key(seed)
        k1, k2, k3, k4 = jax.random.split(key, 4)
        std_h = math.sqrt(0.1 / HIDDEN)
        std_i = math.sqrt(0.1 / INTER)
        inputs = jax.random.normal(k1, (B, S, HIDDEN), dtype=jnp.float32)
        gate_weight = jax.random.normal(k2, (NUM_EXPERTS, HIDDEN), dtype=jnp.float32) * std_h
        wi = jax.random.normal(k3, (NUM_EXPERTS, HIDDEN, INTER), dtype=jnp.float32) * std_h
        wo = jax.random.normal(k4, (NUM_EXPERTS, INTER, HIDDEN), dtype=jnp.float32) * std_i
        return {'inputs': inputs, 'gate_weight': gate_weight, 'wi': wi, 'wo': wo}
    _L1_ffn_all = _L1_ffn_setup()
    _L1_ffn_in = {k: v for k, v in _L1_ffn_all.items() if k in ('gate_weight', 'wi', 'wo')}
    del _L1_ffn_all
    return {'x': x, 'ctx_2048': ctx_2048, 'mask_Bx1x2048_fk1': mask_Bx1x2048_fk1, 'mask_Bx1xSxS_fk0': mask_Bx1xSxS_fk0, 'L0_xattn_Wq': _L0_xattn_in['Wq'], 'L0_xattn_bq': _L0_xattn_in['bq'], 'L0_xattn_Wk': _L0_xattn_in['Wk'], 'L0_xattn_bk': _L0_xattn_in['bk'], 'L0_xattn_Wv': _L0_xattn_in['Wv'], 'L0_xattn_bv': _L0_xattn_in['bv'], 'L0_ffn_gate_w': _L0_ffn_in['gate_w'], 'L0_ffn_gate_up_proj': _L0_ffn_in['gate_up_proj'], 'L0_ffn_down_proj': _L0_ffn_in['down_proj'], 'L1_xattn_Wq': _L1_xattn_in['Wq'], 'L1_xattn_Wk': _L1_xattn_in['Wk'], 'L1_xattn_Wv': _L1_xattn_in['Wv'], 'L1_xattn_Wo': _L1_xattn_in['Wo'], 'L1_xattn_gate': _L1_xattn_in['gate'], 'L1_ffn_gate_weight': _L1_ffn_in['gate_weight'], 'L1_ffn_wi': _L1_ffn_in['wi'], 'L1_ffn_wo': _L1_ffn_in['wo']}

def reference(x, ctx_2048, mask_Bx1x2048_fk1, mask_Bx1xSxS_fk0, L0_xattn_Wq, L0_xattn_bq, L0_xattn_Wk, L0_xattn_bk, L0_xattn_Wv, L0_xattn_bv, L0_ffn_gate_w, L0_ffn_gate_up_proj, L0_ffn_down_proj, L1_xattn_Wq, L1_xattn_Wk, L1_xattn_Wv, L1_xattn_Wo, L1_xattn_gate, L1_ffn_gate_weight, L1_ffn_wi, L1_ffn_wo):
    import jax
    import jax.numpy as jnp

    def _L0_xattn_ref(target, source, target_mask, source_mask, Wq, bq, Wk, bk, Wv, bv):
        import math
        import jax, jax.numpy as jnp
        import numpy as np
        SIZE = 128
        HEADS = 16
        HEAD_DIM = SIZE // HEADS
        B, T, S = (2, 256, 256)
        NEG = 1000000.0
        b, _, t = target.shape
        s = source.shape[-1]
        q = jnp.einsum('oc,bct->bot', Wq, target) + bq[None, :, None]
        k = jnp.einsum('oc,bcs->bos', Wk, source) + bk[None, :, None]
        v = jnp.einsum('oc,bcs->bos', Wv, source) + bv[None, :, None]
        q = q.reshape(b, HEADS, HEAD_DIM, t)
        k = k.reshape(b, HEADS, HEAD_DIM, s)
        v = v.reshape(b, HEADS, HEAD_DIM, s)
        dot = jnp.einsum('bhdt,bhds->bhts', q, k) / math.sqrt(HEAD_DIM)
        mask = target_mask[:, :, :, None] * source_mask[:, :, None, :]
        dot = mask * dot - (1.0 - mask) * NEG
        amap = jax.nn.softmax(dot, axis=-1) * mask
        out = jnp.einsum('bhts,bhds->bhdt', amap, v)
        return out.reshape(b, HEADS * HEAD_DIM, t)

    def _L0_ffn_ref(hidden_states, gate_w, gate_up_proj, down_proj):
        import jax, jax.numpy as jnp
        import numpy as np
        B, S, H, E, I, TOPK = (1, 128, 256, 16, 128, 2)
        SCALE = 1.0
        b, s, h = hidden_states.shape
        e = gate_w.shape[0]
        x = hidden_states.reshape(-1, h)
        logits = jnp.matmul(x.astype(jnp.float32), gate_w.T.astype(jnp.float32))
        p = jax.nn.sigmoid(logits)
        p = p / jnp.sum(p, axis=-1, keepdims=True)
        w, idx = jax.lax.top_k(p, TOPK)
        w = w / jnp.sum(w, axis=-1, keepdims=True)
        w = w * SCALE
        combine = jnp.sum(jax.nn.one_hot(idx, e, dtype=w.dtype) * w[..., None], axis=1)
        gu = jnp.einsum('th,ehf->etf', x, gate_up_proj)
        gate, up = jnp.split(gu, 2, axis=-1)
        inter = jax.nn.silu(gate) * up
        y = jnp.einsum('eti,eih->eth', inter, down_proj)
        out = jnp.einsum('eth,te->th', y, combine.astype(y.dtype))
        return out.reshape(b, s, h)

    def _L1_xattn_ref(hidden_states, attention_mask, adapter, Wq, Wk, Wv, Wo, gate):
        import jax, jax.numpy as jnp
        import numpy as np
        import math
        B, S, HID, H = (2, 256, 256, 32)
        D = HID // H
        AL = 10

        def _rope_tables(seq_len, dim, dtype):
            inv_freq = 1.0 / 10000.0 ** (np.arange(0, dim, 2, dtype=np.float32) / dim)
            t = np.arange(seq_len, dtype=np.float32)
            freqs = np.outer(t, inv_freq)
            emb = np.concatenate([freqs, freqs], -1)
            return (jnp.asarray(np.cos(emb), dtype), jnp.asarray(np.sin(emb), dtype))

        def _rotate_half(x):
            x1, x2 = jnp.split(x, 2, axis=-1)
            return jnp.concatenate([-x2, x1], axis=-1)
        bsz, q_len, hid = hidden_states.shape
        n_heads = gate.shape[1]
        head_dim = hid // n_heads
        inv_sqrt_d = 1.0 / math.sqrt(head_dim)

        def split_heads(x, length):
            return x.reshape(bsz, length, n_heads, head_dim).transpose(0, 2, 1, 3)
        q = split_heads(hidden_states @ Wq, q_len)
        k = split_heads(hidden_states @ Wk, q_len)
        v = split_heads(hidden_states @ Wv, q_len)
        cos, sin = _rope_tables(q_len, head_dim, q.dtype)
        q = q * cos + _rotate_half(q) * sin
        k = k * cos + _rotate_half(k) * sin
        scores = jnp.einsum('bhqd,bhkd->bhqk', q, k) * inv_sqrt_d
        scores = scores + attention_mask
        scores = jnp.maximum(scores, jnp.finfo(scores.dtype).min)
        w = jax.nn.softmax(scores.astype(jnp.float32), axis=-1).astype(q.dtype)
        attn_output = jnp.einsum('bhqk,bhkd->bhqd', w, v)
        adapter_len = adapter.shape[1]
        a_k = split_heads(adapter @ Wk, adapter_len)
        a_v = split_heads(adapter @ Wv, adapter_len)
        a_scores = jnp.einsum('bhqd,bhkd->bhqk', q, a_k) * inv_sqrt_d
        a_scores = jnp.tanh(gate) * jax.nn.softmax(a_scores.astype(jnp.float32), axis=-1).astype(q.dtype)
        attn_output = attn_output + jnp.einsum('bhqk,bhkd->bhqd', a_scores, a_v)
        attn_output = attn_output.transpose(0, 2, 1, 3).reshape(bsz, q_len, hid)
        return attn_output @ Wo

    def _L1_ffn_ref(inputs, gate_weight, wi, wo):
        import math
        import jax, jax.numpy as jnp
        import numpy as np
        NUM_EXPERTS = 8
        HIDDEN = 256
        INTER = 1024
        CAP_FACTOR = 1.25
        MIN_CAP = 4
        B, S = (4, 256)

        def _capacity(num_tokens: int, num_experts: int) -> int:
            cap = math.floor(CAP_FACTOR * num_tokens / num_experts)
            cap += cap % 2
            return max(cap, MIN_CAP)
        b, s, h = inputs.shape
        tokens = inputs.reshape(-1, h)
        T = tokens.shape[0]
        E = gate_weight.shape[0]
        C = _capacity(T, E)
        logits = tokens.astype(jnp.float32) @ gate_weight.astype(jnp.float32).T
        probs = jax.nn.softmax(logits, axis=-1)
        top1 = jnp.argmax(logits, axis=-1)
        mask = jax.nn.one_hot(top1, E, dtype=jnp.int32)
        ranks = jnp.cumsum(mask, axis=0) - 1
        mask = mask * (ranks < C).astype(jnp.int32)
        ranks_tok = jnp.sum(mask * ranks, axis=-1)
        ranks_oh = jax.nn.one_hot(ranks_tok, C, dtype=jnp.float32)
        weight = mask.astype(probs.dtype) * probs
        combine_weights = weight[:, :, None] * ranks_oh[:, None, :]
        sec_mask = jax.lax.stop_gradient(combine_weights != 0).astype(inputs.dtype)
        dispatch = jnp.einsum('tec,th->ech', sec_mask, tokens)
        hmid = jnp.einsum('ech,ehi->eci', dispatch, wi)
        hmid = jax.nn.gelu(hmid, approximate=False)
        eout = jnp.einsum('eci,eih->ech', hmid, wo)
        out = jnp.einsum('tec,ech->th', combine_weights.astype(inputs.dtype), eout)
        return out.reshape(b, s, h)
    x = x + _L0_xattn_ref(_layernorm(x, axis=-1), ctx_2048, mask_Bx1x2048_fk1, mask_Bx1x2048_fk1, L0_xattn_Wq, L0_xattn_bq, L0_xattn_Wk, L0_xattn_bk, L0_xattn_Wv, L0_xattn_bv)
    x = x + _L0_ffn_ref(_layernorm(x, axis=-1), L0_ffn_gate_w, L0_ffn_gate_up_proj, L0_ffn_down_proj)
    x = x + _L1_xattn_ref(_layernorm(x, axis=-1), mask_Bx1xSxS_fk0, ctx_2048, L1_xattn_Wq, L1_xattn_Wk, L1_xattn_Wv, L1_xattn_Wo, L1_xattn_gate)
    x = x + _L1_ffn_ref(_layernorm(x, axis=-1), L1_ffn_gate_weight, L1_ffn_wi, L1_ffn_wo)
    return x

_drawn_inputs = setup_inputs


def setup_inputs(seed=0):
    import zlib

    import numpy as np

    out = dict(_drawn_inputs(seed))
    spreads = {}
    factors = {'L0_xattn_bq': 3.924,
     'L0_xattn_bk': 8.0,
     'L0_xattn_bv': 5.752,
     'L1_xattn_Wq': 8.0,
     'L1_xattn_Wk': 8.0,
     'L1_xattn_gate': 8.0,
     'L1_ffn_gate_weight': 6.227,
     'L1_ffn_wi': 5.831,
     'L1_ffn_wo': 5.669}
    for name, (base, spread) in spreads.items():
        noise = np.random.default_rng([zlib.crc32(name.encode()), seed]).standard_normal(out[name].shape)
        drawn = base * np.exp(spread * noise) if base else spread * noise
        out[name] = jnp.asarray(drawn.astype(out[name].dtype))
    for name, factor in factors.items():
        out[name] = (out[name] * factor).astype(out[name].dtype)
    return out
```

```python
import concourse.bass as bass
from concourse import mybir
from contextlib import ExitStack

import numpy as np


ORDER = ("A1", "C1", "F", "A2", "C2", "A3", "C3")

USES = {
    "slot0": {"A1": 1, "C1": 0, "F": 2, "A2": 4, "C2": 4, "A3": 4, "C3": 4},
    "slot1": {"A1": 0, "C1": 1, "F": 2, "A2": 4, "C2": 4, "A3": 4, "C3": 4},
    "misc": {"A1": 0, "C1": 2, "F": 6, "A2": 1, "C2": 1, "A3": 1, "C3": 4},
}


def uses_before(region, stage, at, batches):
    count = 0
    for kind, lag in (("A", 0), ("F", 1), ("C", 2)):
        if isinstance(at, int):
            done = min(max(at - lag, 0), batches)
            active = 0 <= at - lag < batches
        else:
            done, active = at - lag, True
        ahead = 0
        for s in ORDER:
            if s[0] == kind:
                count = done * USES[region][s] + count
                if active and ORDER.index(s) < ORDER.index(stage):
                    ahead += USES[region][s]
        count = count + ahead
    return count


def two_layer_kernel(nc, x, ctx_in, mask01, mask01_cols, addmask, addmaskT, wq0T, bq0, wk0T, bk0, wv0T, bv0, gate0T, gate_up, down,
                     wq1, wk1, wv1, wo1, gate1, gate1wT, wi, wo, rope, out):
    F32 = mybir.dt.float32
    F32R = mybir.dt.float32r
    BF16 = mybir.dt.bfloat16
    U32 = mybir.dt.uint32
    ALU = mybir.AluOpType
    ACT = mybir.ActivationFunctionType
    AX = mybir.AxisListType

    NB, P, D = x.shape
    H0, H1, HD = 16, 32, 8
    E0, I0 = down.shape[0], down.shape[1]
    E1, I1 = wo.shape[0], wo.shape[1]
    CAP = 160
    SLOTS = E1 * CAP
    NEG = 1000000.0
    EPS = 1e-5
    KT = D // P
    ROWS_MAX = 122
    IT1 = I1 // P

    dram = lambda name, shape, dt=F32: nc.dram_tensor(name, shape, dt, kind="Internal").ap()
    qk0_dram = dram("qk0_dram", [5, P, D])
    m0_dram = dram("m0_dram", [2, 32, P])
    mq_dram = dram("mq_dram", [NB, 6, D])
    mk_dram = dram("mk_dram", [NB, 6, D])
    c_dram = dram("c_dram", [13, 2, P, P], BF16)
    m1_dram = dram("m1_dram", [2, 3, H1, P], BF16)
    disp_dram = dram("disp_dram", [SLOTS + P, D])
    x3_dram = dram("x3_dram", [NB, P, D])
    eout_dram = dram("eout_dram", [SLOTS + P, D])

    with ExitStack() as stack:
        def sb(name, shape, dt=F32):
            return stack.enter_context(nc.sbuf_tensor(name, shape, dt))

        def pb(name, shape, dt=F32):
            return stack.enter_context(nc.psum_tensor(name, shape, dt))

        def sem(name):
            return stack.enter_context(nc.semaphore(name))

        ident = sb("ident", [P, P])
        ident_r = sb("ident_r", [P, P], F32R)
        tri = sb("tri", [P, P])
        ones = sb("ones", [P, P])
        minus_half = sb("minus_half", [P, 1])
        sel = sb("sel", [P, 2, P])
        iota16 = sb("iota16", [P, 16])
        dump_row = sb("dump_row", [P, 1])
        ebase = sb("ebase", [P, E1])
        wq0_sb = sb("wq0_sb", [P, P])
        wk0_sb = sb("wk0_sb", [P, P])
        wv0_sb = sb("wv0_sb", [P, P])
        bq0_sb = sb("bq0_sb", [P, 1])
        bk0_sb = sb("bk0_sb", [P, 1])
        bv0_sb = sb("bv0_sb", [1, P])
        gate0_sb = sb("gate0_sb", [P, KT, E0])
        gu_sb = sb("gu_sb", [P, KT, E0, 2 * I0])
        dn_sb = sb("dn_sb", [P, E0, D])
        wq1_sb = sb("wq1_sb", [P, KT, D])
        wk1_sb = sb("wk1_sb", [P, KT, D])
        wv1_sb = sb("wv1_sb", [P, KT, D])
        wo1_sb = sb("wo1_sb", [P, 4, D])
        gate1_sb = sb("gate1_sb", [P, D])
        gate1w_sb = sb("gate1w_sb", [P, KT, E1])
        rope_sb = sb("rope_sb", [P, 8, P])
        gu_flat = gu_sb[:].rearrange("p k e f -> p (k e f)")
        half = KT * I1
        wi_sb = gu_flat[:, 0:2 * half].rearrange("p (s k i) -> p s k i", s=2, k=KT)
        wo_sb = gu_flat[:, 2 * half:2 * half + 2 * IT1 * D].rearrange("p (s k h) -> p s k h", s=2, k=IT1)
        dn_flat = dn_sb[:].rearrange("p e h -> p (e h)")
        dispT = dn_flat[:, 0:KT * SLOTS].rearrange("p (k c) -> p k c", k=KT)
        mask_rows = dn_flat[0:NB, 0:12 * D].rearrange("b (r t) -> b r t", r=12)
        mask_tmp = dn_flat[0:NB, 12 * D:15 * D].rearrange("b (r t) -> b r t", r=3)

        x_in = sb("x_in", [P, D])
        x_res = sb("x_res", [P, D])
        ctx_a = sb("ctx_a", [P, D])
        tm_b = sb("tm_b", [P, D])
        sm_col = sb("sm_col", [P, 2])
        tms_b = sb("tms_b", [P, D])
        qk0 = sb("qk0", [P, 2, D])
        qk0_p = sb("qk0_p", [P, 2, 2, D], F32R)
        QS0 = sb("QS0", [P, H0, D], F32R)
        KS0 = sb("KS0", [P, H0, D], F32R)
        vst0 = sb("vst0", [P, 2, H0 // 2, 64])
        mx0 = sb("mx0", [P, H0, 2])
        m0_p = sb("m0_p", [32, 2, P], F32R)
        p = sb("p", [P, 2, 1024])
        den = sb("den", [P, 2, 2 * D])
        den_a, rec_a = den[:, 0, :], den[:, 1, :]
        o_a = sb("o_a", [P, 2, D])
        x1 = sb("x1", [P, D])

        n1T = sb("n1T", [P, KT, P])
        route = sb("route", [P, 8, E0])
        rsmall = sb("rsmall", [P, 8])
        top8 = sb("top8", [P, 8])
        top8i = sb("top8i", [P, 8], U32)
        tanh_g = sb("tanh_g", [P, 2, 4, P])
        inter = sb("inter", [P, 2, 4, P])
        interT = sb("interT", [P, 2, 4, P])
        x2 = sb("x2", [P, D])

        x2_res = sb("x2_res", [P, D])
        ctx_c = sb("ctx_c", [P, D])
        amask = sb("amask", [P, 2, P])
        amask_p = sb("amask_p", [P, 2, 2, P], F32R)
        nT = sb("nT", [P, 4, P])
        qka = sb("qka", [P, 6, P])
        qka_r = sb("qka_r", [P, 6, P])
        qka_p = sb("qka_p", [P, 3, 3, D], BF16)
        QS1 = sb("QS1", [P, H1, P], BF16)
        KS1 = sb("KS1", [P, H1, P], BF16)
        AS1 = sb("AS1", [P, H1, P], BF16)
        vst_s = sb("vst_s", [P, H1 // 2, 64])
        vst_x = sb("vst_x", [P, H1 // 2, 64])
        mx1 = sb("mx1", [P, 2, H1])
        m1_f = sb("m1_f", [64, 2, P])
        m1_p = sb("m1_p", [64, 3, P], BF16)
        hT = [t[:].rearrange("p h t -> p (h t)").bitcast(F32)[:, 0:IT1 * CAP].rearrange("p (i c) -> p i c", i=IT1)
              for t in (QS1, KS1)]
        o_c = sb("o_c", [P, 4, P])

        bn = {k: sb(f"bn_{k}", [P, 6]) for k in "afce"}
        mv = {k: sb(f"mv_{k}", [P, 2]) for k in "afce"}
        rstd = {k: sb(f"rstd_{k}", [P, 1]) for k in "afce"}
        normed = {k: sb(f"normed_{k}", [P, D]) for k in "afce"}

        x3 = AS1[:].rearrange("p h t -> p (h t)").bitcast(F32).rearrange("p (b h) -> p b h", b=NB)
        x3_now = sb("x3_now", [P, D])
        slot_now = sb("slot_now", [P, 1], U32)
        n3T = sb("n3T", [P, KT, P])
        top1 = sb("top1", [P, 8])
        top1i = sb("top1i", [P, 8], U32)
        lg1 = sb("lg1", [P, 6, E1])
        one_hot1 = sb("one_hot1", [P, E1])
        seen = sb("seen", [P, E1])
        small1 = sb("small1", [P, 8])
        wgt = sb("wgt", [P, NB])
        slot_u = sb("slot_u", [P, NB], U32)

        slot = [pb(f"slot{k}", [P, 1024]) for k in range(2)]
        misc = pb("misc", [P, 512])
        pv0 = pb("pv0", [P, 512])
        pvs = pb("pvs", [P, 512])
        pvx = pb("pvx", [P, 512])

        names = """
        passed_SP passed_Pool passed_DVE passed_PE x3_ld gate1_s qka_a dn_chunk bn_a bn_f bn_c bn_e tms_s x3_copy load_w0 load_a load_c load_gu load_w1
        load_we0 load_we1 maskrow_st ones_row const_pool const_step const_dve mask_rows_done zeros_st slot0_full
        slot0_free slot1_full slot1_free misc_full misc_free bn_step rstd_ready_a rstd_ready_f rstd_ready_c
        rstd_ready_e var_a var_f var_c var_e norm_a xres_a qk0_ready qk0_h qk0_l v0_ready qk0_st qk0_ld
        mask0_ld m0_h m0_st m0_ld pvdone_a den_a_s rec_a_s o_a_s x1_ready norm_f route_s comb_ready tanh_s
        actg_s inter_s x2_ready norm_c x2res_s amask_h amask_l qka_step qka_p2 qka_done vs_ready vx_ready
        c_st c_ld m1_step m1_st m1_ld pvdone_c den_c_s o_c_s norm_e exp_e route1_s onehot_s seen_s
        slot_ready scat_s disp_ld0 disp_ld1 eo_full eo_sb eo_st0 eo_st1 gath0 gath1 comb_s out_st
        """.split()
        S = {n: sem(n) for n in names}

        def full(k):
            return S[f"slot{k}_full"]

        def free(k):
            return S[f"slot{k}_free"]

        qk_flat = QS0[:].rearrange("p h t -> p (h t)")

        def flat(tile):
            return tile[:].rearrange("p h t -> p (h t)")

        def apart(eng, semaphore, value):
            after(eng, semaphore, value)
            if not isinstance(value, int):
                eng.sem_inc(S[f"passed_{eng.engine.name}"], 1)

        def by_x(tile):
            return tile[:].rearrange("p (x m) t -> p x (m t)", x=3)

        block = stack.enter_context(nc.Block())

        LAST = NB + 1
        LOOP = (3, NB - 1)

        def iterations(eng, stages):
            def one(i):
                for s in ORDER:
                    lag = {"A": 0, "F": 1, "C": 2}[s[0]]
                    if isinstance(i, int) and not 0 <= i - lag < NB:
                        continue
                    if s in stages:
                        stages[s](i - lag if lag else i, i)
            for i in range(LOOP[0]):
                one(i)
            with eng.Fori(*LOOP) as i:
                one(i)
            for i in range(LOOP[1], LAST + 1):
                one(i)

        def after(eng, semaphore, value):
            if not isinstance(value, int) or value > 0:
                eng.wait_ge(semaphore, value)

        @block.sync
        def _(sp):
            def wait(semaphore, value):
                if isinstance(value, int):
                    after(sp, semaphore, value)
                else:
                    apart(sp, semaphore, value)

            def load_a(b):
                sp.dma_start(x_in[:], x[b, :, :]).then_inc(S["load_a"], 16)
                sp.dma_start(ctx_a[:], ctx_in[b, :, :]).then_inc(S["load_a"], 16)
                sp.dma_start(tm_b[:], mask01[b, :, :].broadcast_to([P, D])).then_inc(S["load_a"], 16)
                sp.dma_start(sm_col[:], mask01_cols[b, :, :]).then_inc(S["load_a"], 16)

            def load_c(b):
                sp.dma_start(ctx_c[:], ctx_in[b, :, :]).then_inc(S["load_c"], 16)
                sp.dma_start(amask[:, 0, :], addmask[b, :, :]).then_inc(S["load_c"], 16)
                sp.dma_start(amask[:, 1, :], addmaskT[b, :, :]).then_inc(S["load_c"], 16)

            load_a(0)
            for dst, src in ((mask_tmp[:, 0, :], mask01.rearrange("b o t -> (b o) t")), (wq0_sb[:], wq0T),
                             (wk0_sb[:], wk0T), (wv0_sb[:], wv0T), (bq0_sb[:], bq0), (bk0_sb[:], bk0),
                             (bv0_sb[:], bv0)):
                sp.dma_start(dst, src).then_inc(S["load_w0"], 16)
            load_c(0)
            sp.dma_start(gate0_sb[:], gate0T.rearrange("(k p) e -> p k e", p=P)).then_inc(S["load_gu"], 16)
            for k in range(KT):
                sp.dma_start(gu_sb[:, k, :, :],
                             gate_up[:, k * P:(k + 1) * P, :].rearrange("e p f -> p e f")).then_inc(S["load_gu"], 16)
            for dst, src in ((wq1_sb, wq1), (wk1_sb, wk1), (wv1_sb, wv1), (gate1w_sb, gate1wT)):
                sp.dma_start(dst[:], src.rearrange("(k p) o -> p k o", p=P)).then_inc(S["load_w1"], 16)
            sp.dma_start(wo1_sb[:], wo1.rearrange("r p o -> p r o")).then_inc(S["load_w1"], 16)
            sp.dma_start(gate1_sb[:], gate1.broadcast_to([P, D])).then_inc(S["load_w1"], 16)
            sp.dma_start(rope_sb[:], rope).then_inc(S["load_w1"], 16)
            wait(S["const_pool"], 1)
            for n in range(4):
                sp.dma_start(flat(KS0)[126:128, 1024 * n:1024 * n + 1024].bitcast(F32), p[0:2, 0, :]).then_inc(S["ones_row"], 16)
            ones_bf = p[:, 1, :].bitcast(BF16)
            for n in range(2):
                sp.dma_start(flat(KS1)[122:125, 2048 * n:2048 * n + 2048], ones_bf[0:3, :]).then_inc(S["ones_row"], 16)
                sp.dma_start(flat(AS1)[125:128, 2048 * n:2048 * n + 2048], ones_bf[0:3, :]).then_inc(S["ones_row"], 16)
            for n in range((SLOTS + P) // P):
                sp.dma_start(disp_dram[n * P:(n + 1) * P, :], x1[:]).then_inc(S["zeros_st"], 16)
            sp.dma_start(eout_dram[SLOTS:SLOTS + P, :], x1[:]).then_inc(S["zeros_st"], 16)
            wait(S["mask_rows_done"], 1)
            sp.dma_start(mq_dram.rearrange("b r t -> b (r t)"),
                         mask_rows[:, 0:6, :].rearrange("b r t -> b (r t)")).then_inc(S["maskrow_st"], 16)
            sp.dma_start(mk_dram.rearrange("b r t -> b (r t)"),
                         mask_rows[:, 6:12, :].rearrange("b r t -> b (r t)")).then_inc(S["maskrow_st"], 16)
            wait(S["maskrow_st"], 32)
            sp.dma_start(dn_sb[:], down.rearrange("e i h -> i e h")).then_inc(S["load_gu"], 16)

            def load_expert(e):
                sp.dma_start(wi_sb[:, e % 2, :, :], wi[e, :, :].rearrange("(k p) i -> p k i", p=P)).then_inc(S[f"load_we{e % 2}"], 16)
                sp.dma_start(wo_sb[:, e % 2, :, :], wo[e, :, :].rearrange("(k p) h -> p k h", p=P)).then_inc(S[f"load_we{e % 2}"], 16)

            def a1(b, i):
                wait(S["qk0_h"], b + 1)
                wait(S["qk0_l"], b + 1)
                flat4 = qk0_dram.rearrange("s p t -> p s t")
                src = qk0_p[:].rearrange("p l q t -> p q l t").bitcast(F32)
                wait(S["qk0_ld"], 64 * b)
                sp.dma_start(flat4[:, 0:2, :], src[:, 0, :, :]).then_inc(S["qk0_st"], 16)
                sp.dma_start(flat4[:, 2:4, :], src[:, 1, :, :]).then_inc(S["qk0_st"], 16)
                sp.dma_start(flat4[:, 4, :], src[:, 1, 0, :]).then_inc(S["qk0_st"], 16)
                wait(S["pvdone_a"], 8 * b)
                if isinstance(b, int) and b == 0:
                    wait(S["const_pool"], 2)
                wait(S["qk0_st"], 48 * b + 48)
                rows = qk0_dram.rearrange("s (d h) t -> (s d) (h t)", h=H0)
                sp.dma_start(flat(QS0)[0:16, :].bitcast(F32), rows[0:16, :]).then_inc(S["qk0_ld"], 16)
                sp.dma_start(flat(QS0)[16:32, :].bitcast(F32), rows[0:16, :]).then_inc(S["qk0_ld"], 16)
                sp.dma_start(flat(KS0)[0:16, :].bitcast(F32), rows[16:32, :]).then_inc(S["qk0_ld"], 16)
                sp.dma_start(flat(KS0)[16:32, :].bitcast(F32), rows[24:40, :]).then_inc(S["qk0_ld"], 16)
                mq = mq_dram[b, :, :].unsqueeze(1).broadcast_to([6, H0, D])
                mk = mk_dram[b, :, :].unsqueeze(1).broadcast_to([6, H0, D])
                sp.dma_start(QS0[32:38, :, :].bitcast(F32), mq).then_inc(S["mask0_ld"], 16)
                sp.dma_start(KS0[32:38, :, :].bitcast(F32), mk).then_inc(S["mask0_ld"], 16)

            def c1(b, i):
                wait(S["qka_done"], b + 1)
                wait(S["c_ld"], 144 * b)
                dst = c_dram.rearrange("s m p t -> p s m t")
                for x_, (at, n) in enumerate(((0, 3), (3, 3), (8, 3))):
                    sp.dma_start(dst[:, at:at + n, :, :].rearrange("p s m t -> p (s m) t"),
                                 qka_p[:, x_, :, :].rearrange("p s (m t) -> p (s m) t", m=2)).then_inc(S["c_st"], 16)
                for x_, at in ((1, 6), (2, 11)):
                    sp.dma_start(dst[:, at:at + 2, :, :].rearrange("p s m t -> p (s m) t"),
                                 qka_p[:, x_, 0:2, :].rearrange("p s (m t) -> p (s m) t", m=2)).then_inc(S["c_st"], 16)
                wait(S["pvdone_c"], 8 * b)
                wait(S["c_st"], 80 * b + 80)
                rows = c_dram.rearrange("s m (d h) t -> (s m d) (h t)", h=H1)
                for w in range(3):
                    sp.dma_start(flat(QS1)[24 * w:24 * w + 24, :], rows[0:24, :]).then_inc(S["c_ld"], 16)
                    sp.dma_start(flat(KS1)[24 * w:24 * w + 24, :], rows[24 + 8 * w:48 + 8 * w, :]).then_inc(S["c_ld"], 16)
                    sp.dma_start(flat(AS1)[24 * w:24 * w + 24, :], rows[64 + 8 * w:88 + 8 * w, :]).then_inc(S["c_ld"], 16)

            def a2(b, i):
                wait(S["misc_free"], uses_before("misc", "A2", i, NB) + 1)
                wait(S["m0_ld"], 16 * b)
                sp.dma_start(m0_dram.rearrange("s r t -> r s t"), m0_p[:].bitcast(F32)).then_inc(S["m0_st"], 16)
                wait(S["m0_st"], 16 * b + 16)
                sp.dma_start(flat(QS0)[126:128, :].bitcast(F32),
                             m0_dram.rearrange("s r t -> s (r t)")).then_inc(S["m0_ld"], 16)

            def c2(b, i):
                wait(S["m1_step"], 3 * b + 3)
                wait(S["m1_ld"], 16 * b)
                for kind in range(2):
                    sp.dma_start(m1_dram[kind, :, :, :].rearrange("s h t -> h s t"),
                                 m1_p[32 * kind:32 * kind + 32, :, :]).then_inc(S["m1_st"], 16)
                wait(S["m1_st"], 32 * b + 32)
                sp.dma_start(flat(QS1)[122:128, :], m1_dram.rearrange("k s h t -> (k s) (h t)")).then_inc(S["m1_ld"], 16)

            def a3(b, i):
                if isinstance(b, int) and b == NB - 1:
                    return
                wait(S["xres_a"], b + 1)
                wait(S["norm_a"], b + 1)
                wait(S["v0_ready"], 4 * b + 4)
                wait(S["misc_free"], uses_before("misc", "A3", i, NB) + 1)
                load_a(b + 1)

            def c3(b, i):
                wait(S["misc_free"], uses_before("misc", "C3", i, NB) + 1)
                sp.dma_start(x3_dram[b, :, :], x3_now[:]).then_inc(S["x3_copy"], 16)
                if isinstance(b, int) and b == NB - 2:
                    wait(S["x2_ready"], NB)
                    load_expert(0)
                    load_expert(1)
                if isinstance(b, int) and b == NB - 1:
                    return
                wait(S["misc_free"], uses_before("misc", "C1", i, NB) + 1)
                wait(S["amask_l"], b + 1)
                load_c(b + 1)

            iterations(sp, {"A1": a1, "C1": c1, "A2": a2, "C2": c2, "A3": a3, "C3": c3})

            wait(S["x3_copy"], 16 * NB)
            wait(S["pvdone_c"], 8 * NB)
            sp.dma_start(x3, x3_dram.rearrange("b p h -> p b h")).then_inc(S["x3_ld"], 16)
            wait(S["scat_s"], 16 * NB)
            for n in range(SLOTS // P):
                if n >= 2:
                    wait(free(n % 2), uses_before(f"slot{n % 2}", "A1", NB + 2, NB) + n // 2)
                sp.dma_start(p[:, n % 2, 0:D], disp_dram[n * P:(n + 1) * P, :]).then_inc(S[f"disp_ld{n % 2}"], 16)
            for e in range(E1):
                if e + 2 < E1:
                    wait(S["eo_full"], 2 * e + 2)
                    load_expert(e + 2)
                for c in range(2):
                    rows = P if c == 0 else CAP - P
                    wait(S["eo_sb"], 2 * e + c + 1)
                    sp.dma_start(eout_dram[e * CAP + c * P:e * CAP + c * P + rows, :],
                                 p[0:rows, c, (e % 2) * D:(e % 2) * D + D]).then_inc(S[f"eo_st{e % 2}"], 16)
            for b in range(NB):
                wait(S["comb_s"], b + 1)
                sp.dma_start(out[b, :, :], x3[:, b, :]).then_inc(S["out_st"], 16)
            wait(S["out_st"], 16 * NB)

        @block.gpsimd
        def _(pool):
            g = nc.gpsimd
            setup = [0]

            def step(ins):
                setup[0] += 1
                ins.then_inc(S["const_step"], 1)
                return setup[0]

            step(g.memset(minus_half[:], -0.5))
            step(g.memset(ident[:], 0.0))
            step(g.memset(tri[:], 1.0))
            step(g.memset(sel[:], 0.0))
            step(g.memset(x1[:], 0.0))
            step(g.memset(p[:, 0, :], 1.0))
            step(g.memset(p[:, 1, :].bitcast(BF16), 1.0))
            step(g.memset(seen[:], 0.0))
            step(g.memset(KS0[:].bitcast(F32), 0.0))
            step(g.memset(KS1[:], 0.0))
            n = step(g.memset(AS1[:], 0.0))
            pool.wait_ge(S["const_step"], n)
            g.affine_select(out=ident[:], in_=ident[:], compare_op=ALU.not_equal, fill=1.0, base=0,
                            pattern=[[-1, P]], channel_multiplier=1).then_inc(S["const_pool"], 1)
            step(g.memset(QS0[:].bitcast(F32), 0.0))
            step(g.memset(QS1[:], 0.0))
            step(g.iota(iota16[:], pattern=[[1, 16]], base=0, channel_multiplier=0,
                        allow_small_or_imprecise_dtypes=True))
            step(g.iota(dump_row[:], pattern=[[0, 1]], base=SLOTS, channel_multiplier=1,
                        allow_small_or_imprecise_dtypes=True))
            step(g.iota(ebase[:], pattern=[[CAP, E1]], base=0, channel_multiplier=0,
                        allow_small_or_imprecise_dtypes=True))
            n = step(g.affine_select(out=tri[:], in_=tri[:], compare_op=ALU.is_ge, fill=0.0, base=0,
                                 pattern=[[1, P]], channel_multiplier=-1))
            for j in range(4):
                for r in range(2):
                    pool.wait_ge(S["const_step"], n)
                    v = sel[32 * j:32 * j + 32, r, 64 * r + 16 * j:64 * r + 16 * j + 16]
                    n = step(g.affine_select(out=v, in_=v, compare_op=ALU.not_equal, fill=1.0, base=0,
                                             pattern=[[-1, 16]], channel_multiplier=1))
            pool.wait_ge(S["const_step"], n)
            for t in (vst0[:].rearrange("p s k c -> p (s k) c"), vst_s[:], vst_x[:]):
                n = step(g.memset(t, 0.0))
            pool.wait_ge(S["const_step"], n)
            for t in (vst0[:].rearrange("p s k c -> p (s k) c"), vst_s[:], vst_x[:]):
                step(g.memset(t[:, :, 16:24], 1.0))
                n = step(g.memset(t[:, :, 56:64], 1.0))
            pool.wait_ge(S["const_step"], n)
            g.memset(ones[:], 1.0).then_inc(S["const_pool"], 1)

            def rsqrt(k, b):
                pool.wait_ge(S[f"var_{k}"], b + 1)
                g.tensor_tensor(rstd[k][:], mv[k][:, 1:2], minus_half[:], ALU.pow).then_inc(S[f"rstd_ready_{k}"], 1)

            def a1(b, i):
                rsqrt("a", b)
                after(pool, S["x1_ready"], b)
                apart(pool, S["load_a"], 64 * b + 64)
                g.tensor_copy(x_res[:], x_in[:]).then_inc(S["xres_a"], 1)
                apart(pool, S["qk0_h"], b)
                g.tensor_scalar(tms_b[:], tm_b[:], float(HD) ** -0.5, 1.0, ALU.mult, ALU.mult).then_inc(S["tms_s"], 1)

            def c1(b, i):
                after(pool, S["bn_e"], 2 * b)
                apart(pool, S["x2_ready"], b + 1)
                g.tensor_copy(x2_res[:], x2[:]).then_inc(S["x2res_s"], 1)
                rsqrt("c", b)

            def f(b, i):
                rsqrt("f", b)
                for c in range(4):
                    pool.wait_ge(S["comb_ready"], b + 1)
                    pool.wait_ge(free(c % 2), uses_before(f"slot{c % 2}", "F", i, NB) + c // 2 + 1)
                    share = route[:, 7, 4 * c:4 * c + 4].unsqueeze(2).broadcast_to([P, 4, P])
                    g.tensor_tensor(inter[:, c % 2, :, :], inter[:, c % 2, :, :], share,
                                    ALU.mult).then_inc(S["inter_s"], 1)

            def c3(b, i):
                rsqrt("e", b)
                pool.wait_ge(S["norm_e"], b + 1)
                apart(pool, S["slot_ready"], b + 1)
                if isinstance(b, int) and b == 0:
                    pool.wait_ge(S["zeros_st"], 16 * (SLOTS // P + 2))
                g.indirect_dma_start(disp_dram, bass.IndirectOffsetOnAxis(ap=slot_now[:], axis=0),
                                     normed["e"][:], None).then_inc(S["scat_s"], 16)

            iterations(pool, {"A1": a1, "C1": c1, "F": f, "C3": c3})

            for k in range(2):
                pool.wait_ge(S[f"eo_st{k}"], 32 * E1 // 2)
            for b in range(NB):
                if b >= 2:
                    pool.wait_ge(S["comb_s"], b - 1)
                g.indirect_dma_start(p[:, b % 2, 2 * D:3 * D], None, eout_dram,
                                     bass.IndirectOffsetOnAxis(ap=slot_u[:, b:b + 1], axis=0)).then_inc(S[f"gath{b % 2}"], 16)

        @block.vector
        def _(dve):
            v = nc.vector

            def norm_stats(k, src, b):
                v.bn_stats(bn[k][:], src).then_inc(S[f"bn_{k}"], 1)
                apart(dve, S[f"bn_{k}"], 2 * b + 1)
                v.bn_aggr(mv[k][:], bn[k][:]).then_inc(S[f"bn_{k}"], 1)
                dve.wait_ge(S[f"bn_{k}"], 2 * b + 2)
                v.tensor_scalar_add(mv[k][:, 1:2], mv[k][:, 1:2], EPS).then_inc(S[f"var_{k}"], 1)

            def norm_apply(k, src, b):
                dve.wait_ge(S[f"rstd_ready_{k}"], b + 1)
                v.tensor_scalar(normed[k][:], src, mv[k][:, 0:1], rstd[k][:], ALU.subtract,
                                ALU.mult).then_inc(S[f"norm_{k}"], 1)

            dve.wait_ge(S["load_w0"], 16 * 7)
            steps = [0]

            def link(ins):
                steps[0] += 1
                ins.then_inc(S["const_dve"], 1)
                dve.wait_ge(S["const_dve"], steps[0])

            mh = qk0_p[0:NB, 0, 0, :]
            mask, w_, low = mask_tmp[:, 0, :], mask_tmp[:, 1, :], mask_tmp[:, 2, :]
            link(v.tensor_scalar(w_, mask, 1.0, NEG, ALU.subtract, ALU.mult))
            link(v.tensor_copy(mh, mask))
            link(v.tensor_tensor(low, mask, mh.bitcast(F32), ALU.subtract))
            for r in (0, 1):
                v.tensor_copy(mask_rows[:, r, :], mh.bitcast(F32))
                link(v.tensor_copy(mask_rows[:, 2 + r, :], low))
            link(v.tensor_copy(mh, w_))
            link(v.tensor_tensor(low, w_, mh.bitcast(F32), ALU.subtract))
            for r in (4, 6, 8):
                v.tensor_copy(mask_rows[:, r, :], mh.bitcast(F32))
                link(v.tensor_copy(mask_rows[:, r + 1, :], low))
            link(v.memset(mask_rows[:, 10, :], 1.0))
            v.memset(mask_rows[:, 11, :], 1.0).then_inc(S["mask_rows_done"], 1)
            dve.wait_ge(S["const_pool"], 1)
            v.tensor_copy(ident_r[:], ident[:]).then_inc(S["const_dve"], 1)
            identr_step = steps[0] + 1
            dve.wait_ge(S["const_pool"], 2)

            def a1(b, i):
                dve.wait_ge(S["load_a"], 64 * b + 64)
                norm_stats("a", x_in[:], b)
                norm_apply("a", x_in[:], b)
                n = uses_before("slot0", "A1", i, NB)
                dve.wait_ge(full(0), n + 1)
                dve.wait_ge(S["tms_s"], b + 1)
                v.scalar_tensor_tensor(qk0[:, 0, :], slot[0][:, 0:D], bq0_sb[:], tms_b[:], ALU.add,
                                       ALU.mult).then_inc(S["qk0_ready"], 1)
                v.scalar_tensor_tensor(qk0[:, 1, :], slot[0][:, D:2 * D], bk0_sb[:], tm_b[:], ALU.add,
                                       ALU.mult).then_inc(S["qk0_ready"], 1)
                after(dve, S["qk0_st"], 48 * b)
                dve.wait_ge(S["qk0_ready"], 2 * b + 2)
                v.tensor_copy(qk0_p[:, 0, :, :], qk0[:]).then_inc(S["qk0_h"], 1)
                dve.wait_ge(S["qk0_h"], b + 1)
                v.tensor_tensor(qk0_p[:, 1, :, :], qk0[:], qk0_p[:, 0, :, :].bitcast(F32),
                                ALU.subtract).then_inc(S["qk0_l"], 1)

            def c1(b, i):
                dve.wait_ge(S["x2_ready"], b + 1)
                norm_stats("c", x2[:], b)
                dve.wait_ge(S["load_c"], 48 * b + 48)
                after(dve, S["pvdone_c"], 8 * b)
                v.tensor_copy(amask_p[:, 0, :, :], amask[:]).then_inc(S["amask_h"], 1)
                norm_apply("c", x2[:], b)
                dve.wait_ge(S["amask_h"], b + 1)
                v.tensor_tensor(amask_p[:, 1, :, :], amask[:], amask_p[:, 0, :, :].bitcast(F32),
                                ALU.subtract).then_inc(S["amask_l"], 1)
                n = uses_before("slot1", "C1", i, NB)
                dve.wait_ge(full(1), n + 1)
                ps = slot[1][:, 0:512].rearrange("p (x m t) -> p x m t", x=2, m=2)
                cos = rope_sb[:, 0:4, :].rearrange("p (x m) t -> p x m t", x=2)
                sin = rope_sb[:, 4:8, :].rearrange("p (x m) t -> p x m t", x=2)
                r = qka_r[:, 0:4, :].rearrange("p (x m) t -> p x m t", x=2)
                s_ = qka[:, 0:4, :].rearrange("p (x m) t -> p x m t", x=2)
                after(dve, S["qka_p2"], b)
                v.tensor_tensor(r, ps, cos, ALU.mult).then_inc(S["qka_step"], 1)
                v.tensor_tensor(s_[:, :, 0, :], ps[:, :, 1, :], sin[:, :, 0, :], ALU.mult).then_inc(S["qka_step"], 1)
                v.tensor_tensor(s_[:, :, 1, :], ps[:, :, 0, :], sin[:, :, 1, :], ALU.mult).then_inc(S["qka_step"], 1)
                dve.wait_ge(S["qka_step"], 5 * b + 3)
                v.tensor_tensor(qka_r[:, 0:4, :], qka_r[:, 0:4, :], qka[:, 0:4, :], ALU.add).then_inc(S["qka_step"], 1)
                n = uses_before("misc", "C1", i, NB) + 1
                dve.wait_ge(S["misc_full"], n + 1)
                dve.wait_ge(S["vs_ready"], 2 * b + 2)
                for hh in range(2):
                    src = misc[:, D:2 * D].rearrange("p (k x) -> p k x", x=16)[:, :, 8 * hh:8 * hh + 8]
                    gt = gate1_sb[:].rearrange("p (k x) -> p k x", x=16)[:, :, 8 * hh:8 * hh + 8]
                    last = v.tensor_tensor(vst_x[:, :, 40 * hh:40 * hh + 8], src, gt, ALU.mult)
                    last.then_inc(S["vx_ready" if hh == 0 else "misc_free"], 1)
                dve.wait_ge(free(1), uses_before("slot1", "C1", i, NB) + 1)
                v.tensor_tensor(by_x(qka), by_x(qka_r), qka_p[:, :, 0, :], ALU.subtract).then_inc(S["qka_step"], 1)
                dve.wait_ge(S["qka_p2"], b + 1)
                v.tensor_tensor(qka_p[:, :, 2, :], by_x(qka), qka_p[:, :, 1, :], ALU.subtract).then_inc(S["qka_done"], 1)

            ROUTE0 = 12

            def f(b, i):
                count = [0]

                def rs(ins, wait=True):
                    count[0] += 1
                    ins.then_inc(S["route_s"], 1)
                    if wait:
                        apart(dve, S["route_s"], ROUTE0 * b + count[0])

                dve.wait_ge(S["x1_ready"], b + 1)
                norm_stats("f", x1[:], b)
                norm_apply("f", x1[:], b)
                dve.wait_ge(S["misc_free"], uses_before("misc", "F", i, NB) + 2)
                after(dve, S["inter_s"], 4 * b)
                rs(v.tensor_scalar_add(route[:, 1, :], route[:, 0, :], 1.0))
                rs(v.reciprocal(route[:, 2, :], route[:, 1, :]))
                rs(v.reduce_sum(rsmall[:, 0:1], route[:, 2, :], AX.X))
                rs(v.reciprocal(rsmall[:, 1:2], rsmall[:, 0:1]))
                rs(v.tensor_scalar(route[:, 3, :], route[:, 2, :], rsmall[:, 1:2], None, ALU.mult))
                rs(v.max(top8[:], route[:, 3, :]))
                rs(v.max_index(top8i[:], top8[:], route[:, 3, :]))
                rs(v.tensor_copy(rsmall[:, 2:4], top8i[:, 0:2]))
                rs(v.tensor_tensor(rsmall[:, 4:5], top8[:, 0:1], top8[:, 1:2], ALU.add))
                rs(v.reciprocal(rsmall[:, 5:6], rsmall[:, 4:5]))
                rs(v.tensor_scalar(rsmall[:, 6:8], top8[:, 0:2], rsmall[:, 5:6], 0.5, ALU.mult, ALU.mult))
                v.tensor_scalar(route[:, 4, :], iota16[:], rsmall[:, 2:3], rsmall[:, 6:7], ALU.is_equal, ALU.mult)
                rs(v.tensor_scalar(route[:, 5, :], iota16[:], rsmall[:, 3:4], rsmall[:, 7:8], ALU.is_equal, ALU.mult))
                v.tensor_tensor(route[:, 7, :], route[:, 4, :], route[:, 5, :], ALU.add).then_inc(S["comb_ready"], 1)
                assert count[0] == ROUTE0
                for c in range(4):
                    k = c % 2
                    n = uses_before(f"slot{k}", "F", i, NB) + c // 2
                    ps = slot[k][:].rearrange("p (e g i) -> p e g i", e=4, g=2)
                    dve.wait_ge(S["tanh_s"], 4 * b + c + 1)
                    v.scalar_tensor_tensor(tanh_g[:, k, :, :], tanh_g[:, k, :, :], 1.0, ps[:, :, 0, :], ALU.add,
                                           ALU.mult).then_inc(S["actg_s"], 1)
                    dve.wait_ge(S["actg_s"], 4 * b + c + 1)
                    if c >= 2:
                        dve.wait_ge(S["misc_free"], uses_before("misc", "F", i, NB) + 2 + c - 1)
                    v.tensor_tensor(inter[:, k, :, :], tanh_g[:, k, :, :], ps[:, :, 1, :],
                                    ALU.mult).then_inc(free(k), 1)
                dve.wait_ge(S["dn_chunk"], 4 * b + 4)
                after(dve, S["x2res_s"], b)
                v.tensor_tensor(x2[:], x1[:], pv0[:, 0:D], ALU.add).then_inc(S["x2_ready"], 1)

            def a2(b, i):
                for g_ in range(8):
                    k = g_ % 2
                    n = uses_before(f"slot{k}", "A2", i, NB) + g_ // 2
                    dve.wait_ge(full(k), n + 1)
                    hg, tt = g_ % 4, g_ // 4
                    v.reduce_max(mx0[:, 4 * hg:4 * hg + 4, tt], slot[k][:].rearrange("p (h s) -> p h s", h=4),
                                 AX.X).then_inc(free(k), 1)
                n = uses_before("misc", "A2", i, NB)
                dve.wait_ge(S["misc_full"], n + 1)
                after(dve, S["m0_st"], 16 * b)
                v.tensor_scalar(m0_p[:, 0, :], misc[0:32, 0:P], -1.0, None, ALU.mult).then_inc(S["m0_h"], 1)
                dve.wait_ge(S["m0_h"], b + 1)
                v.scalar_tensor_tensor(m0_p[:, 1, :], misc[0:32, 0:P], -1.0, m0_p[:, 0, :].bitcast(F32), ALU.mult,
                                       ALU.subtract).then_inc(S["misc_free"], 1)

            def c2(b, i):
                for g_ in range(8):
                    k = g_ % 2
                    n = uses_before(f"slot{k}", "C2", i, NB) + g_ // 2
                    dve.wait_ge(full(k), n + 1)
                    kind, r = g_ // 4, g_ % 4
                    v.reduce_max(mx1[:, kind, 8 * r:8 * r + 8], slot[k][:].rearrange("p (h s) -> p h s", h=8),
                                 AX.X).then_inc(free(k), 1)
                n = uses_before("misc", "C2", i, NB)
                dve.wait_ge(S["misc_full"], n + 1)
                after(dve, S["m1_st"], 32 * b)
                v.tensor_scalar(m1_p[:, 0, :], misc[0:64, 0:P], -1.0, None, ALU.mult).then_inc(S["m1_step"], 1)
                dve.wait_ge(S["m1_step"], 3 * b + 1)
                v.scalar_tensor_tensor(m1_f[:, 0, :], misc[0:64, 0:P], -1.0, m1_p[:, 0, :], ALU.mult,
                                       ALU.subtract).then_inc(S["misc_free"], 1)
                dve.wait_ge(S["misc_free"], n + 1)
                v.tensor_copy(m1_p[:, 1, :], m1_f[:, 0, :]).then_inc(S["m1_step"], 1)
                dve.wait_ge(S["m1_step"], 3 * b + 2)
                v.tensor_tensor(m1_p[:, 2, :], m1_f[:, 0, :], m1_p[:, 1, :], ALU.subtract).then_inc(S["m1_step"], 1)

            to_sums = [16 + j % 16 for j in range(32)]

            def a3(b, i):
                apart(dve, S["pvdone_a"], 8 * b + 8)
                v.stream_shuffle(den_a, pv0[:], to_sums).then_inc(S["den_a_s"], 1)
                dve.wait_ge(S["den_a_s"], b + 1)
                v.reciprocal(rec_a, den_a).then_inc(S["rec_a_s"], 1)
                dve.wait_ge(S["rec_a_s"], b + 1)
                v.tensor_tensor(o_a[:].rearrange("p r t -> p (r t)"), pv0[:], rec_a, ALU.mult).then_inc(S["o_a_s"], 1)
                n = uses_before("misc", "A3", i, NB)
                dve.wait_ge(S["misc_full"], n + 1)
                v.tensor_tensor(rec_a[:, 0:D], misc[:, 0:D], tm_b[:],
                                ALU.mult).then_inc(S["misc_free"], 1)
                dve.wait_ge(S["misc_free"], n + 1)
                dve.wait_ge(S["xres_a"], b + 1)
                if isinstance(b, int) and b == 0:
                    dve.wait_ge(S["zeros_st"], 16 * (SLOTS // P + 2))
                v.tensor_tensor(x1[:], rec_a[:, 0:D], x_res[:], ALU.add).then_inc(S["x1_ready"], 1)

            ROUTE1 = 17

            def c3(b, i):
                for kind, pv in ((0, pvs), (1, pvx)):
                    apart(dve, S["pvdone_c"], 8 * b + 4 * kind + 4)
                    v.stream_shuffle(den[:, 0, :], pv[:], to_sums).then_inc(S["den_c_s"], 1)
                    dve.wait_ge(S["den_c_s"], 4 * b + 2 * kind + 1)
                    v.reciprocal(den[:, 1, :], den[:, 0, :]).then_inc(S["den_c_s"], 1)
                    dve.wait_ge(S["den_c_s"], 4 * b + 2 * kind + 2)
                    o = o_c[:].rearrange("p r t -> p (r t)")
                    if kind == 0:
                        v.tensor_tensor(o, pv[:], den[:, 1, :], ALU.mult).then_inc(S["o_c_s"], 1)
                    else:
                        v.tensor_tensor(den[:, 0, :], pv[:], den[:, 1, :], ALU.mult).then_inc(S["o_c_s"], 1)
                        dve.wait_ge(S["o_c_s"], 3 * b + 2)
                        v.tensor_tensor(o, o, den[:, 0, :], ALU.add).then_inc(S["o_c_s"], 1)
                n = uses_before("misc", "C3", i, NB)
                dve.wait_ge(S["misc_full"], n + 1)
                dve.wait_ge(S["x2res_s"], b + 1)
                after(dve, S["x3_copy"], 16 * b)
                v.tensor_tensor(x3_now[:], misc[:, 0:D], x2_res[:],
                                ALU.add).then_inc(S["misc_free"], 1)
                dve.wait_ge(S["misc_free"], n + 1)
                norm_stats("e", x3_now[:], b)
                after(dve, S["scat_s"], 16 * b)
                norm_apply("e", x3_now[:], b)

                count = [0]

                def rs(ins, wait=True):
                    count[0] += 1
                    ins.then_inc(S["route1_s"], 1)
                    if wait:
                        apart(dve, S["route1_s"], ROUTE1 * b + count[0])

                dve.wait_ge(S["misc_full"], n + 3)
                after(dve, S["exp_e"], b)
                v.tensor_copy(lg1[:, 0, :], misc[:, 0:E1]).then_inc(S["misc_free"], 1)
                apart(dve, S["misc_free"], n + 3)
                rs(v.max(top1[:], lg1[:, 0, :]))
                rs(v.max_index(top1i[:], top1[:], lg1[:, 0, :]))
                rs(v.tensor_scalar(small1[:, 0:1], top1[:, 0:1], -1.0, None, ALU.mult))
                rs(v.tensor_copy(small1[:, 1:2], top1i[:, 0:1]))
                v.tensor_scalar(one_hot1[:], iota16[:, 0:E1], small1[:, 1:2], None,
                                ALU.is_equal).then_inc(S["onehot_s"], 1)
                dve.wait_ge(S["exp_e"], b + 1)
                rs(v.reciprocal(small1[:, 3:4], small1[:, 2:3]))
                dve.wait_ge(S["onehot_s"], b + 1)
                dve.wait_ge(S["misc_full"], n + 4)
                rs(v.scalar_tensor_tensor(lg1[:, 1, :], misc[:, 0:E1], -1.0, one_hot1[:], ALU.add, ALU.mult))
                v.scalar_tensor_tensor(lg1[:, 2, :], misc[:, 0:E1], -1.0, ebase[:], ALU.add,
                                       ALU.add).then_inc(S["misc_free"], 1)
                dve.wait_ge(S["misc_free"], n + 4)
                rs(v.tensor_tensor(lg1[:, 3, :], lg1[:, 2, :], one_hot1[:], ALU.mult))
                rs(v.reduce_sum(small1[:, 4:5], lg1[:, 1, :], AX.X))
                rs(v.reduce_sum(small1[:, 5:6], lg1[:, 3, :], AX.X))
                v.tensor_tensor(seen[:], seen[:], one_hot1[:], ALU.add).then_inc(S["seen_s"], 1)
                rs(v.tensor_scalar(small1[:, 6:7], small1[:, 4:5], float(CAP), None, ALU.is_lt))
                rs(v.tensor_tensor(small1[:, 7:8], small1[:, 5:6], dump_row[:], ALU.subtract))
                rs(v.tensor_scalar(lg1[:, 4, 0:1], small1[:, 7:8], small1[:, 6:7], dump_row[:], ALU.mult, ALU.add))
                rs(v.tensor_tensor(wgt[:, bass.ds(b, 1)], small1[:, 3:4], small1[:, 6:7], ALU.mult))
                rs(v.tensor_copy(slot_u[:, bass.ds(b, 1)], lg1[:, 4, 0:1]))
                v.tensor_copy(slot_now[:], lg1[:, 4, 0:1]).then_inc(S["slot_ready"], 1)
                while count[0] < ROUTE1:
                    rs(v.tensor_copy(lg1[:, 5, 0:1], lg1[:, 4, 0:1]))
                assert count[0] == ROUTE1

            iterations(dve, {"A1": a1, "C1": c1, "F": f, "A2": a2, "C2": c2, "A3": a3, "C3": c3})

            for e in range(E1):
                for c, ps in ((0, pv0), (1, pvs)):
                    rows = P if c == 0 else CAP - P
                    dve.wait_ge(S["eo_full"], 2 * e + c + 1)
                    if e >= 2:
                        dve.wait_ge(S[f"eo_st{e % 2}"], 32 * (e // 2))
                    v.tensor_copy(p[0:rows, c, (e % 2) * D:(e % 2) * D + D], ps[0:rows, 0:D]).then_inc(S["eo_sb"], 1)
            for b in range(NB):
                dve.wait_ge(S[f"gath{b % 2}"], 16 * (b // 2) + 16)
                dve.wait_ge(S["x3_ld"], 16)
                v.scalar_tensor_tensor(x3[:, b, :], p[:, b % 2, 2 * D:3 * D], wgt[:, b:b + 1], x3[:, b, :], ALU.mult,
                                       ALU.add).then_inc(S["comb_s"], 1)

        @block.scalar
        def _(act):
            a = nc.scalar
            act.wait_ge(S["load_w1"], 16 * 7)
            a.activation(gate1_sb[:], gate1_sb[:], ACT.Tanh).then_inc(S["gate1_s"], 1)

            def copy_misc(dst, cols, use):
                act.wait_ge(S["misc_full"], use + 1)
                a.activation(dst, misc[:, 0:cols], ACT.Copy).then_inc(S["misc_free"], 1)

            def a1(b, i):
                n = uses_before("slot0", "A1", i, NB)
                act.wait_ge(full(0), n + 1)
                after(act, S["pvdone_a"], 8 * b)
                if isinstance(b, int) and b == 0:
                    act.wait_ge(S["const_pool"], 2)
                act.wait_ge(S["load_a"], 64 * b + 64)
                for st in range(2):
                    for hh in range(2):
                        src = slot[0][:, 2 * D + st * P:2 * D + st * P + P].rearrange("p (k x) -> p k x", x=16)
                        ins = a.activation(vst0[:, st, :, 40 * hh:40 * hh + 8], src[:, :, 8 * hh:8 * hh + 8], ACT.Copy,
                                           scale=sm_col[:, st:st + 1])
                        ins.then_inc(S["v0_ready"], 1)
                act.wait_ge(S["qk0_ready"], 2 * b + 2)
                act.wait_ge(S["v0_ready"], 4 * b + 4)
                act.sem_inc(free(0), 1)

            def c1(b, i):
                n = uses_before("misc", "C1", i, NB)
                copy_misc(nT[:].rearrange("p k t -> p (k t)"), 512, n)
                m = uses_before("slot1", "C1", i, NB)
                act.wait_ge(full(1), m + 1)
                after(act, S["qka_step"], 5 * b)
                a.activation(qka_r[:, 4:6, :].rearrange("p k t -> p (k t)"), slot[1][:, 512:768],
                             ACT.Copy).then_inc(S["qka_a"], 1)
                act.wait_ge(S["misc_full"], n + 2)
                after(act, S["pvdone_c"], 8 * b)
                for hh in range(2):
                    src = misc[:, 0:D].rearrange("p (k x) -> p k x", x=16)[:, :, 8 * hh:8 * hh + 8]
                    a.activation(vst_s[:, :, 40 * hh:40 * hh + 8], src, ACT.Copy).then_inc(S["vs_ready"], 1)
                act.wait_ge(S["qka_step"], 5 * b + 4)
                act.wait_ge(S["qka_a"], b + 1)
                after(act, S["c_st"], 80 * b)
                a.activation(qka_p[:, :, 0, :], by_x(qka_r), ACT.Copy).then_inc(free(1), 1)
                act.wait_ge(S["qka_step"], 5 * b + 5)
                a.activation(qka_p[:, :, 1, :], by_x(qka), ACT.Copy).then_inc(S["qka_p2"], 1)

            def f(b, i):
                n = uses_before("misc", "F", i, NB)
                after(act, S["dn_chunk"], 4 * b)
                copy_misc(n1T[:].rearrange("p k t -> p (k t)"), KT * P, n)
                act.wait_ge(S["misc_full"], n + 2)
                after(act, S["comb_ready"], b)
                a.activation(route[:, 0, :], misc[:, 0:E0], ACT.Exp,
                             scale=-1.0).then_inc(S["misc_free"], 1)

                def tanh(c):
                    k = c % 2
                    m = uses_before(f"slot{k}", "F", i, NB) + c // 2
                    act.wait_ge(full(k), m + 1)
                    after(act, S["actg_s"], 4 * b + c - 1)
                    ps = slot[k][:].rearrange("p (e g i) -> p e g i", e=4, g=2)
                    a.activation(tanh_g[:, k, :, :], ps[:, :, 0, :], ACT.Tanh, scale=0.5).then_inc(S["tanh_s"], 1)

                def copy_inter(c):
                    after(act, S["dn_chunk"], 4 * b + c - 1)
                    copy_misc(interT[:, c % 2, :, :].rearrange("p e t -> p (e t)"), 512, n + 2 + c)

                tanh(0)
                for c in range(1, 4):
                    tanh(c)
                    copy_inter(c - 1)
                copy_inter(3)

            def a3(b, i):
                for g_ in range(8):
                    k = g_ % 2
                    n = uses_before(f"slot{k}", "A3", i, NB) + g_ // 2
                    act.wait_ge(full(k), n + 1)
                    ran_c = max(min(i - 2, NB), 0) if isinstance(i, int) else i - 2
                    if g_ >= 2 or (isinstance(ran_c, int) and ran_c == 0):
                        after(act, S["pvdone_a"], 8 * b + g_ - 1)
                    else:
                        act.wait_ge(S["pvdone_c"], 8 * ran_c + g_ - 1)
                    a.activation(p[:, k, :], slot[k][:], ACT.Exp).then_inc(free(k), 1)

            def c3(b, i):
                for g_ in range(8):
                    k = g_ % 2
                    n = uses_before(f"slot{k}", "C3", i, NB) + g_ // 2
                    act.wait_ge(full(k), n + 1)
                    if g_ >= 2 or (isinstance(i, int) and i >= NB):
                        after(act, S["pvdone_c"], 8 * b + g_ - 1)
                    else:
                        act.wait_ge(S["pvdone_a"], 8 * i + g_ + 7)
                    a.activation(p[:, k, :], slot[k][:], ACT.Exp).then_inc(free(k), 1)
                n = uses_before("misc", "C3", i, NB)
                after(act, S["route1_s"], 17 * b)
                copy_misc(n3T[:].rearrange("p k t -> p (k t)"), KT * P, n + 1)
                act.wait_ge(S["route1_s"], 17 * b + 3)
                a.activation(lg1[:, 5, :], lg1[:, 0, :], ACT.Exp, bias=small1[:, 0:1],
                             accum_out=small1[:, 2:3]).then_inc(S["exp_e"], 1)

            iterations(act, {"A1": a1, "C1": c1, "F": f, "A3": a3, "C3": c3})

            end = NB + 2
            for n in range(SLOTS // P):
                k = n % 2
                m = uses_before(f"slot{k}", "A1", end, NB) + n // 2
                act.wait_ge(full(k), m + 1)
                a.activation(dispT[:, :, n * P:(n + 1) * P], slot[k][:, 0:KT * P].rearrange("p (k t) -> p k t", k=KT),
                             ACT.Copy).then_inc(free(k), 1)
            for e in range(E1):
                for u in range(2):
                    m = uses_before(f"slot{u}", "A1", end, NB) + SLOTS // P // 2 + e
                    act.wait_ge(full(u), m + 1)
                    if e >= 2:
                        act.wait_ge(S["eo_full"], 2 * (e - 1))
                    src = slot[u][:].rearrange("p (k n) -> p k n", k=2)[:, :, 0:2 * CAP]
                    dst = hT[e % 2][:, 4 * u:4 * u + 4, :].rearrange("p (k i) c -> p k (i c)", k=2)
                    a.activation(dst, src, ACT.Gelu).then_inc(free(u), 1)

        @block.tensor
        def _(pe):
            t = nc.tensor

            def take(region, use):
                after(pe, S[f"{region}_free"], use)

            def a1(b, i):
                take("slot0", uses_before("slot0", "A1", i, NB))
                if isinstance(b, int) and b == 0:
                    pe.wait_ge(S["load_w0"], 16 * 7)
                    pe.wait_ge(S["const_pool"], 2)
                pe.wait_ge(S["load_a"], 64 * b + 64)
                ps = slot[0]
                for st in range(2):
                    o = ps[:, 2 * D + st * P:2 * D + (st + 1) * P]
                    t.matmul(o, ctx_a[:, st * P:(st + 1) * P], wv0_sb[:], start=True, stop=False)
                    t.matmul(o, ones[0:1, :], bv0_sb[:], start=False, stop=True)
                t.matmul(ps[:, D:2 * D], wk0_sb[:], ctx_a[:], start=True, stop=True)
                pe.wait_ge(S["norm_a"], b + 1)
                t.matmul(ps[:, 0:D], wq0_sb[:], normed["a"][:], start=True, stop=True).then_inc(full(0), 1)

            def c1(b, i):
                n = uses_before("misc", "C1", i, NB)
                take("misc", n)
                pe.wait_ge(S["load_c"], 48 * b + 48)
                for k in range(KT):
                    t.transpose(misc[:, (2 + k) * P:(3 + k) * P], ctx_c[:, k * P:(k + 1) * P], ident[:])
                pe.wait_ge(S["norm_c"], b + 1)
                for k in range(KT):
                    last = t.transpose(misc[:, k * P:(k + 1) * P], normed["c"][:, k * P:(k + 1) * P], ident[:])
                last.then_inc(S["misc_full"], 1)
                m = uses_before("slot1", "C1", i, NB)
                take("slot1", m)
                pe.wait_ge(S["misc_free"], n + 1)
                if isinstance(b, int) and b == 0:
                    pe.wait_ge(S["load_w1"], 16 * 7)
                for x_, w, src in ((0, wq1_sb, 0), (1, wk1_sb, 0), (2, wk1_sb, 2)):
                    for mt in range(2):
                        at = (2 * x_ + mt) * P
                        for k in range(KT):
                            last = t.matmul(slot[1][:, at:at + P], w[:, k, mt * P:(mt + 1) * P], nT[:, src + k, :],
                                            start=(k == 0), stop=(k == KT - 1))
                last.then_inc(full(1), 1)
                take("misc", n + 1)
                for x_, src in ((0, 0), (1, 2)):
                    for k in range(KT):
                        last = t.matmul(misc[:, x_ * D:(x_ + 1) * D], nT[:, src + k, :], wv1_sb[:, k, :],
                                        start=(k == 0), stop=(k == KT - 1))
                last.then_inc(S["misc_full"], 1)

            def f(b, i):
                n = uses_before("misc", "F", i, NB)
                take("misc", n)
                pe.wait_ge(S["norm_f"], b + 1)
                for k in range(KT):
                    last = t.transpose(misc[:, k * P:(k + 1) * P], normed["f"][:, k * P:(k + 1) * P], ident[:])
                last.then_inc(S["misc_full"], 1)
                take("misc", n + 1)
                if isinstance(b, int) and b == 0:
                    pe.wait_ge(S["load_gu"], 16 * 4)
                for k in range(KT):
                    last = t.matmul(misc[:, 0:E0], n1T[:, k, :], gate0_sb[:, k, :], start=(k == 0), stop=(k == KT - 1))
                last.then_inc(S["misc_full"], 1)

                def gate_and_up(c):
                    s_ = c % 2
                    take(f"slot{s_}", uses_before(f"slot{s_}", "F", i, NB) + c // 2)
                    for half_ in range(2):
                        for k in range(KT):
                            rhs = gu_sb[:, k, 4 * c + 2 * half_:4 * c + 2 * half_ + 2, :].rearrange("p e f -> p (e f)")
                            last = t.matmul(slot[s_][:, 512 * half_:512 * half_ + 512], n1T[:, k, :], rhs,
                                            start=(k == 0), stop=(k == KT - 1))
                    last.then_inc(full(s_), 1)

                def transposes(c):
                    take("misc", n + 2 + c)
                    pe.wait_ge(S["inter_s"], 4 * b + c + 1)
                    for e in range(4):
                        last = t.transpose(misc[:, e * P:(e + 1) * P], inter[:, c % 2, e, :], ident[:])
                    last.then_inc(S["misc_full"], 1)

                def down_products(c):
                    pe.wait_ge(S["misc_free"], n + 2 + c + 1)
                    for e in range(4):
                        last = t.matmul(pv0[:, 0:D], interT[:, c % 2, e, :], dn_sb[:, 4 * c + e, :],
                                        start=(c == 0 and e == 0), stop=(c == 3 and e == 3))
                    last.then_inc(S["dn_chunk"], 1)

                for c in range(4):
                    gate_and_up(c)
                    if c >= 1:
                        transposes(c - 1)
                    if c >= 2:
                        down_products(c - 2)
                transposes(3)
                down_products(2)
                down_products(3)

            def a2(b, i):
                pe.wait_ge(S["qk0_ld"], 64 * b + 64)
                pe.wait_ge(S["mask0_ld"], 32 * b + 32)
                if isinstance(b, int) and b == 0:
                    pe.wait_ge(S["ones_row"], 16 * 8)
                for g_ in range(8):
                    s_ = g_ % 2
                    hg, tt = g_ % 4, g_ // 4
                    take(f"slot{s_}", uses_before(f"slot{s_}", "A2", i, NB) + g_ // 2)
                    for u in range(4):
                        h = 4 * hg + u
                        last = t.matmul(slot[s_][:, u * D:(u + 1) * D], QS0[0:ROWS_MAX, h, tt * P:(tt + 1) * P],
                                        KS0[0:ROWS_MAX, h, :], start=True, stop=True)
                    last.then_inc(full(s_), 1)
                take("misc", uses_before("misc", "A2", i, NB))
                for s_ in range(2):
                    apart(pe, free(s_), uses_before(f"slot{s_}", "A2", i, NB) + 4)
                t.transpose(misc[0:32, 0:P], mx0[:].rearrange("p h s -> p (h s)"), ident[:]).then_inc(S["misc_full"], 1)

            def scores_with_mask(region, g_, which, lhs, rhs, rows):
                kind, r = g_ // 4, g_ % 4
                for hb in range(2):
                    if kind == 0:
                        for lo in range(2):
                            m = amask_p[:, lo, which, :].unsqueeze(1).broadcast_to([P, 4, P])
                            t.matmul(region[:, 512 * hb:512 * hb + 512], ident_r[:], m, start=(lo == 0), stop=(lo == 1))
                    for u in range(4):
                        h = 8 * r + 4 * hb + u
                        at = (4 * hb + u) * P
                        last = t.matmul(region[:, at:at + P], lhs[0:rows, h, :], rhs[0:rows, h, :], start=(kind == 1),
                                        stop=True, skip_group_check=True)
                return last

            def c2(b, i):
                pe.wait_ge(S["c_ld"], 144 * b + 144)
                pe.wait_ge(S["amask_l"], b + 1)
                for g_ in range(8):
                    s_ = g_ % 2
                    take(f"slot{s_}", uses_before(f"slot{s_}", "C2", i, NB) + g_ // 2)
                    scores_with_mask(slot[s_], g_, 0, QS1, KS1 if g_ < 4 else AS1, ROWS_MAX).then_inc(full(s_), 1)
                take("misc", uses_before("misc", "C2", i, NB))
                for s_ in range(2):
                    apart(pe, free(s_), uses_before(f"slot{s_}", "C2", i, NB) + 4)
                t.transpose(misc[0:64, 0:P], mx1[:].rearrange("p k h -> p (k h)"), ident[:]).then_inc(S["misc_full"], 1)

            def a3(b, i):
                pe.wait_ge(S["m0_ld"], 16 * b + 16)
                pe.wait_ge(S["v0_ready"], 4 * b + 4)

                def values(g_):
                    r, hh, st = g_ // 4, (g_ // 2) % 2, g_ % 2
                    take(f"slot{g_ % 2}", uses_before(f"slot{g_ % 2}", "A3", i, NB) + g_ // 2 + 1)
                    if g_ == 0:
                        after(pe, S["x2_ready"], b)
                    for j in range(4):
                        last = t.matmul(pv0[32 * j:32 * j + 32, r * D:(r + 1) * D],
                                        vst0[:, st, 4 * r + j, 32 * hh:32 * hh + 32],
                                        p[:, g_ % 2, j * D:(j + 1) * D],
                                        start=(hh == 0 and st == 0), stop=(hh == 1 and st == 1))
                    last.then_inc(S["pvdone_a"], 1)

                for g_ in range(8):
                    s_ = g_ % 2
                    r, hh, st = g_ // 4, (g_ // 2) % 2, g_ % 2
                    take(f"slot{s_}", uses_before(f"slot{s_}", "A3", i, NB) + g_ // 2)
                    for j in range(4):
                        h = 8 * r + 2 * j + hh
                        last = t.matmul(slot[s_][:, j * D:(j + 1) * D], KS0[:, h, st * P:(st + 1) * P], QS0[:, h, :],
                                        start=True, stop=True)
                    last.then_inc(full(s_), 1)
                    if g_ >= 1:
                        values(g_ - 1)
                values(7)
                take("misc", uses_before("misc", "A3", i, NB))
                pe.wait_ge(S["o_a_s"], b + 1)
                for r in range(2):
                    last = t.matmul(misc[:, 0:D], sel[:, r, :], o_a[:, r, :], start=(r == 0), stop=(r == 1))
                last.then_inc(S["misc_full"], 1)

            def c3(b, i):
                pe.wait_ge(S["m1_ld"], 16 * b + 16)
                pe.wait_ge(S["vs_ready"], 2 * b + 2)
                pe.wait_ge(S["vx_ready"], b + 1)

                def values(g_):
                    kind, r = g_ // 4, g_ % 4
                    take(f"slot{g_ % 2}", uses_before(f"slot{g_ % 2}", "C3", i, NB) + g_ // 2 + 1)
                    if g_ == 0:
                        after(pe, S["o_c_s"], 3 * b)
                    vst, pv = (vst_s, pvs) if kind == 0 else (vst_x, pvx)
                    for hh in range(2):
                        for j in range(4):
                            last = t.matmul(pv[32 * j:32 * j + 32, r * P:(r + 1) * P],
                                            vst[:, 4 * r + j, 32 * hh:32 * hh + 32],
                                            p[:, g_ % 2, (2 * j + hh) * P:(2 * j + hh + 1) * P],
                                            start=(hh == 0), stop=(hh == 1))
                    last.then_inc(S["pvdone_c"], 1)

                for g_ in range(8):
                    s_ = g_ % 2
                    take(f"slot{s_}", uses_before(f"slot{s_}", "C3", i, NB) + g_ // 2)
                    scores_with_mask(slot[s_], g_, 1, KS1 if g_ < 4 else AS1, QS1, P).then_inc(full(s_), 1)
                    if g_ >= 1:
                        values(g_ - 1)
                values(7)
                n = uses_before("misc", "C3", i, NB)
                take("misc", n)
                pe.wait_ge(S["o_c_s"], 3 * b + 3)
                for r in range(4):
                    last = t.matmul(misc[:, 0:D], o_c[:, r, :], wo1_sb[:, r, :], start=(r == 0), stop=(r == 3))
                last.then_inc(S["misc_full"], 1)
                take("misc", n + 1)
                pe.wait_ge(S["norm_e"], b + 1)
                for k in range(KT):
                    last = t.transpose(misc[:, k * P:(k + 1) * P], normed["e"][:, k * P:(k + 1) * P], ident[:])
                last.then_inc(S["misc_full"], 1)
                take("misc", n + 2)
                for k in range(KT):
                    last = t.matmul(misc[:, 0:E1], n3T[:, k, :], gate1w_sb[:, k, :], start=(k == 0), stop=(k == KT - 1))
                last.then_inc(S["misc_full"], 1)
                take("misc", n + 3)
                pe.wait_ge(S["onehot_s"], b + 1)
                after(pe, S["seen_s"], b)
                t.matmul(misc[:, 0:E1], tri[:], one_hot1[:], start=True, stop=False)
                t.matmul(misc[:, 0:E1], ones[:], seen[:], start=False, stop=True).then_inc(S["misc_full"], 1)

            iterations(pe, {"A1": a1, "C1": c1, "F": f, "A2": a2, "C2": c2, "A3": a3, "C3": c3})

            end = NB + 2
            for n in range(SLOTS // P):
                s_ = n % 2
                take(f"slot{s_}", uses_before(f"slot{s_}", "A1", end, NB) + n // 2)
                pe.wait_ge(S[f"disp_ld{n % 2}"], 16 * (n // 2) + 16)
                for k in range(KT):
                    last = t.transpose(slot[s_][:, k * P:(k + 1) * P], p[:, n % 2, k * P:(k + 1) * P], ident[:])
                last.then_inc(full(s_), 1)

            def hidden(e):
                pe.wait_ge(S[f"load_we{e % 2}"], 32 * (e // 2) + 32)
                for u in range(2):
                    take(f"slot{u}", uses_before(f"slot{u}", "A1", end, NB) + SLOTS // P // 2 + e)
                    for q in range(4):
                        at = 512 * (q // 2) + CAP * (q % 2)
                        for k in range(KT):
                            last = t.matmul(slot[u][:, at:at + CAP],
                                            wi_sb[:, e % 2, k, (4 * u + q) * P:(4 * u + q + 1) * P],
                                            dispT[:, k, e * CAP:(e + 1) * CAP], start=(k == 0), stop=(k == KT - 1))
                    last.then_inc(full(u), 1)

            def outputs(e):
                for u in range(2):
                    take(f"slot{u}", uses_before(f"slot{u}", "A1", end, NB) + SLOTS // P // 2 + e + 1)
                if e >= 1:
                    pe.wait_ge(S["eo_sb"], 2 * e)
                for c, ps in ((0, pv0), (1, pvs)):
                    rows = P if c == 0 else CAP - P
                    for k in range(IT1):
                        last = t.matmul(ps[0:rows, 0:D], hT[e % 2][:, k, c * P:c * P + rows], wo_sb[:, e % 2, k, :],
                                        start=(k == 0), stop=(k == IT1 - 1))
                    last.then_inc(S["eo_full"], 1)

            for s_ in range(2):
                take(f"slot{s_}", uses_before(f"slot{s_}", "A1", end, NB) + SLOTS // P // 2)
            hidden(0)
            for e in range(E1):
                if e + 1 < E1:
                    hidden(e + 1)
                outputs(e)


def kernel(**inputs):
    import concourse.bacc as bacc
    from concourse.bass_utils import run_bass_kernel_spmd

    arr = {k: np.ascontiguousarray(v) for k, v in inputs.items()}
    nb, p, d = arr["x"].shape
    hd = 8

    def by_width(w):
        heads = w.shape[-1] // hd
        return np.ascontiguousarray(w.reshape(w.shape[:-1] + (heads, hd)).swapaxes(-1, -2).reshape(w.shape))

    wo_rows = np.zeros((4, 4, 32, d), np.float32)
    wo_rows[:, :, 0:16, :] = arr["L1_xattn_Wo"].reshape(4, 4, 16, d)

    inv = 1.0 / 10000.0 ** (np.arange(0, hd, 2, dtype=np.float32) / hd)
    ang = np.outer(np.arange(p, dtype=np.float32), inv)
    cos, sin = (np.repeat(f(ang).astype(np.float32).T, p // (hd // 2), axis=0) for f in (np.cos, np.sin))
    s = np.float32(1.0 / np.sqrt(hd))
    rope = np.stack([cos * s, cos * s, cos, cos, -sin * s, sin * s, -sin, sin], axis=1).astype(np.float32)

    mask = arr["mask_Bx1xSxS_fk0"][:, 0]
    feed = {
        "x": arr["x"], "ctx": arr["ctx_2048"], "mask01": arr["mask_Bx1x2048_fk1"],
        "mask01_cols": arr["mask_Bx1x2048_fk1"].reshape(nb, d // p, p).transpose(0, 2, 1),
        "addmask": mask, "addmaskT": mask.transpose(0, 2, 1),
        "wq0T": by_width(arr["L0_xattn_Wq"].T), "bq0": by_width(arr["L0_xattn_bq"]).reshape(-1, 1),
        "wk0T": by_width(arr["L0_xattn_Wk"].T), "bk0": by_width(arr["L0_xattn_bk"]).reshape(-1, 1),
        "wv0T": arr["L0_xattn_Wv"].T, "bv0": arr["L0_xattn_bv"].reshape(1, -1),
        "gate0T": arr["L0_ffn_gate_w"].T, "gate_up": arr["L0_ffn_gate_up_proj"], "down": arr["L0_ffn_down_proj"],
        "wq1": by_width(arr["L1_xattn_Wq"]), "wk1": by_width(arr["L1_xattn_Wk"]), "wv1": arr["L1_xattn_Wv"],
        "wo1": wo_rows.reshape(4, 128, d), "gate1": np.repeat(arr["L1_xattn_gate"].reshape(1, -1), hd, axis=1),
        "gate1wT": arr["L1_ffn_gate_weight"].T, "wi": arr["L1_ffn_wi"], "wo": arr["L1_ffn_wo"], "rope": rope,
    }
    nc = bacc.Bacc("TRN2", target_bir_lowering=False, num_devices=1)
    arrays, args = {}, []
    for name, a in feed.items():
        a = np.ascontiguousarray(a)
        arrays[f"in_{name}"] = a
        args.append(nc.dram_tensor(f"in_{name}", a.shape, mybir.dt.from_np(a.dtype), kind="ExternalInput").ap())
    args.append(nc.dram_tensor("out_x", (nb, p, d), mybir.dt.float32, kind="ExternalOutput").ap())
    two_layer_kernel(nc, *args)
    r = run_bass_kernel_spmd(nc, [arrays], core_ids=[0])
    return r.results[0]["out_x"]
```

```python
import concourse.bass as bass
from concourse import mybir
from contextlib import ExitStack

import numpy as np


LAG = {"LA": -1, "A1": -1, "VA": -1, "AR": -1, "LS": -1, "M": 0, "MA": 0, "A3": 0, "ON": 0, "A4": 0,
       "LF": 0, "F0": 0, "F1": 0, "RT": 0, "G": 1, "X": 1, "T": 1, "D": 1, "X2": 1,
       "LC": 1, "C0": 1, "C1": 1, "CR": 1, "CP": 1, "VC": 1, "AM": 1, "CS": 1,
       "N": 2, "NC": 2, "C3": 2, "OS": 2, "OX": 2, "XR": 2, "W": 3, "R0": 3, "R1": 3, "R2": 3, "IN": -1, "INC": 1}
ORDER = [tuple(s.split(".")) for s in """
    IN INC G.0 G.1 M.0 X.0 G.2 W M.1 XR G.3 M.2 X.1 T.0 M.3 D.0 M.4 G.4 R0 M.5 G.5 M.6 X.2 T.1 R1 M.7 D.1 MA
    G.6 LA N.0 G.7 N.1 X.3 T.2 R2 N.2 D.2 N.3 N.4 T.3 N.5 D.3 X2 N.6 A1 N.7
    A3.0 A3.1 NC LC A3.2 A3.3 A3.4 A3.5 A3.6 A3.7 C0 A3.8 LS C1 CR ON CP
    C3.0 C3.1 C3.2 C3.3 A4 AR LF C3.4 C3.5 OS F0 C3.6 C3.7 F1 C3.8 CS OX AM VA VC RT
""".split()]
ORDER = [(s[0], int(s[1])) if len(s) > 1 else (s[0], 0) for s in ORDER]


def uses(region, kind, k):
    if region == "misc":
        return int(kind in ("W", "R0", "R1", "R2", "T", "MA", "NC", "C0", "A4", "F0", "F1", "VA", "VC"))
    if region == "slot2":
        return int(kind in ("M", "N", "C1"))
    at = int(region[-1])
    return int(kind in ("A3", "C3") and k < 8 and k % 2 == at or kind == "G" and k % 4 == 2 * at
               or kind == "A1" and at == 0)


def uses_before(region, step, at, batches):
    total, count = 0, 0
    for n, (kind, k) in enumerate(ORDER):
        u, lag = uses(region, kind, k), LAG[kind]
        if isinstance(at, int):
            count += u * min(max(at - lag, 0), batches)
            active = 0 <= at - lag < batches
        else:
            total += u
            count -= u * lag
            active = True
        if active and n < ORDER.index(step):
            count += u
    return count if isinstance(at, int) else at * total + count


def all_uses(region, batches):
    return batches * sum(uses(region, *s) for s in ORDER)


def two_layer_kernel(nc, x, ctx_in, mask01, mask01_cols, addmask, addmaskT, wq0T, bq0, wk0T, bk0, wv0T, bv0, gate0T, gate_up, down,
                     wq1, wk1, wv1, wo1, gate1, gate1wT, wi, wo, rope, out):
    F32 = mybir.dt.float32
    F32R = mybir.dt.float32r
    BF16 = mybir.dt.bfloat16
    U32 = mybir.dt.uint32
    ALU = mybir.AluOpType
    ACT = mybir.ActivationFunctionType
    AX = mybir.AxisListType

    NB, P, D = x.shape
    H0, H1, HD = 16, 32, 8
    E0, I0 = down.shape[0], down.shape[1]
    E1, I1 = wo.shape[0], wo.shape[1]
    CAP = 160
    SLOTS = E1 * CAP
    NEG = 1000000.0
    EPS = 1e-5
    KT = D // P
    ROWS_MAX = 122
    IT1 = I1 // P

    dram = lambda name, shape, dt=F32: nc.dram_tensor(name, shape, dt, kind="Internal").ap()
    qk0_dram = dram("qk0_dram", [5, P, D])
    m0_dram = dram("m0_dram", [2, 32, P])
    mq_dram = dram("mq_dram", [NB, 6, D])
    mk_dram = dram("mk_dram", [NB, 6, D])
    c_dram = dram("c_dram", [13, 2, P, P], BF16)
    m1_dram = dram("m1_dram", [2, 3, H1, P], BF16)
    disp_dram = dram("disp_dram", [SLOTS + P, D])
    x3_dram = dram("x3_dram", [NB, P, D])
    eout_dram = dram("eout_dram", [SLOTS + P, D])

    with ExitStack() as stack:
        def sb(name, shape, dt=F32):
            return stack.enter_context(nc.sbuf_tensor(name, shape, dt))

        def pb(name, shape, dt=F32):
            return stack.enter_context(nc.psum_tensor(name, shape, dt))

        def sem(name):
            return stack.enter_context(nc.semaphore(name))

        ident = sb("ident", [P, P])
        ident_r = sb("ident_r", [P, P], F32R)
        tri = sb("tri", [P, P])
        ones = sb("ones", [P, P])
        minus_half = sb("minus_half", [P, 1])
        sel = sb("sel", [P, 2, P])
        iota16 = sb("iota16", [P, 16])
        dump_row = sb("dump_row", [P, 1])
        ebase = sb("ebase", [P, E1])
        wq0_sb = sb("wq0_sb", [P, P])
        wk0_sb = sb("wk0_sb", [P, P])
        wv0_sb = sb("wv0_sb", [P, P])
        bq0_sb = sb("bq0_sb", [P, 1])
        bk0_sb = sb("bk0_sb", [P, 1])
        bv0_sb = sb("bv0_sb", [1, P])
        gate0_sb = sb("gate0_sb", [P, KT, E0])
        gu_sb = sb("gu_sb", [P, KT, E0, 2 * I0])
        dn_sb = sb("dn_sb", [P, E0, D])
        room_f = sb("room_f", [P, KT * I1 + IT1 * D])
        room_c = sb("room_c", [P, KT * I1 + IT1 * D])
        used = {"f": 0, "c": 0}

        def cut(which, shape):
            n = int(np.prod(shape))
            room = {"f": room_f, "c": room_c}[which]
            v = room[:, used[which]:used[which] + n]
            used[which] += n
            axes = "abcd"[:len(shape)]
            return v.rearrange(f"p ({' '.join(axes)}) -> p {' '.join(axes)}", **dict(zip(axes, shape)))

        wq1_sb = cut("c", (KT, D))
        wk1_sb = cut("c", (KT, D))
        wv1_sb = sb("wv1_sb", [P, KT, D])
        wo1_sb = sb("wo1_sb", [P, 4, D])
        gate1_sb = sb("gate1_sb", [P, D])
        gate1w_sb = sb("gate1w_sb", [P, KT, E1])
        rope_sb = cut("c", (8, P))
        gu_flat = gu_sb[:].rearrange("p k e f -> p (k e f)")
        dn_flat = dn_sb[:].rearrange("p e h -> p (e h)")
        dispT = dn_flat[:, 0:KT * SLOTS].rearrange("p (k c) -> p k c", k=KT)
        rows_8 = dn_flat[:, KT * SLOTS:KT * SLOTS + 2 * D].rearrange("p (n h) -> p n h", n=2)
        mask_rows = dn_flat[0:NB, 0:12 * D].rearrange("b (r t) -> b r t", r=12)
        mask_tmp = dn_flat[0:NB, 12 * D:15 * D].rearrange("b (r t) -> b r t", r=3)

        x_in = cut("c", (D,))
        x_res = sb("x_res", [P, D])
        ctx_a = cut("c", (D,))
        tm_b = sb("tm_b", [P, D])
        sm_col = sb("sm_col", [P, 2])
        tms_b = sb("tms_b", [P, D])
        qk0 = sb("qk0", [P, 2, D])
        qk0_p = sb("qk0_p", [P, 2, 2, D], F32R)
        QS0 = sb("QS0", [P, H0, D], F32R)
        KS0 = sb("KS0", [P, H0, D], F32R)
        tm_keep = sb("tm_keep", [P, D])
        half = KT * I1
        rings = [gu_flat[:, 0:2 * half], gu_flat[:, 2 * half:4 * half], room_f[:], room_c[:]]
        wi_sb = [r[:, 0:half].rearrange("p (k i) -> p k i", k=KT) for r in rings]
        wo_sb = [r[:, half:2 * half].rearrange("p (k h) -> p k h", k=IT1) for r in rings]
        vst0 = cut("f", (2, H0 // 2, 64))
        mx0 = sb("mx0", [P, H0, 2])
        m0_p = sb("m0_p", [32, 2, P], F32R)
        p = sb("p", [P, 2, 1024])
        den = sb("den", [P, 2, 2 * D])
        den_a, rec_a = den[:, 0, :], den[:, 1, :]
        o_a = sb("o_a", [P, 2, D])
        x1 = sb("x1", [P, D])

        n1T = sb("n1T", [P, KT, P])
        route = sb("route", [P, 8, E0])
        rsmall = sb("rsmall", [P, 8])
        top8 = sb("top8", [P, 8])
        top8i = sb("top8i", [P, 8], U32)
        tanh_g = cut("f", (2, 4, P))
        inter = cut("f", (2, 4, P))
        interT = cut("f", (2, 4, P))
        x2 = sb("x2", [P, D])

        x2_res = sb("x2_res", [P, D])
        ctx_c = sb("ctx_c", [P, D])
        amask = sb("amask", [P, 2, P])
        amask_p = sb("amask_p", [P, 2, 2, P], F32R)
        nT = sb("nT", [P, 4, P])
        qka = cut("c", (6, P))
        qka_r = cut("c", (6, P))
        qka_p = sb("qka_p", [P, 3, 3, D], BF16)
        QS1 = sb("QS1", [P, H1, P], BF16)
        KS1 = sb("KS1", [P, H1, P], BF16)
        AS1 = sb("AS1", [P, H1, P], BF16)
        vst_s = sb("vst_s", [P, H1 // 2, 64])
        vst_x = sb("vst_x", [P, H1 // 2, 64])
        mx1 = sb("mx1", [P, 2, H1])
        m1_f = sb("m1_f", [64, 2, P])
        m1_p = sb("m1_p", [64, 3, P], BF16)
        hT = [t[:].rearrange("p h t -> p (h t)").bitcast(F32)[:, 0:IT1 * CAP].rearrange("p (i c) -> p i c", i=IT1)
              for t in (QS1, KS1)]
        o_c = sb("o_c", [P, 4, P])

        oT = [o_a[:].rearrange("p r t -> p (r t)")[:, 0:KT * CAP].rearrange("p (m c) -> p m c", m=KT),
              o_c[:].rearrange("p r t -> p (r t)")[:, 0:KT * CAP].rearrange("p (m c) -> p m c", m=KT)]

        bn = {k: sb(f"bn_{k}", [P, 6]) for k in "afce"}
        mv = {k: sb(f"mv_{k}", [P, 2]) for k in "afce"}
        rstd = {k: sb(f"rstd_{k}", [P, 1]) for k in "afce"}
        normed = {k: sb(f"normed_{k}", [P, D]) for k in "afce"}

        x3 = AS1[:].rearrange("p h t -> p (h t)").bitcast(F32).rearrange("p (b h) -> p b h", b=NB)
        x3_now = sb("x3_now", [P, D])
        slot_now = sb("slot_now", [P, 1], U32)
        n3T = sb("n3T", [P, KT, P])
        top1 = sb("top1", [P, 8])
        top1i = sb("top1i", [P, 8], U32)
        lg1 = sb("lg1", [P, 6, E1])
        one_hot1 = sb("one_hot1", [P, E1])
        seen = sb("seen", [P, E1])
        small1 = sb("small1", [P, 8])
        wgt = sb("wgt", [P, NB])
        slot_u = sb("slot_u", [P, NB], U32)

        slot = [pb(f"slot{k}", [P, 1024]) for k in range(3)]
        misc = pb("misc", [P, 512])
        pv0 = pb("pv0", [P, 512])
        pvs, pvx = slot[2][:, 0:512], slot[2][:, 512:1024]

        names = """
        passed_SP passed_Pool passed_DVE passed_PE x3_ld gate1_s qka_a dn_chunk bn_a bn_f bn_c bn_e tms_s x3_copy load_w0 load_a load_c load_gu load_w1
        load_wi0 load_wi1 load_wi2 load_wi3 load_wo0 load_wo1 load_wo2 load_wo3 qka_p1 oT_ready eoT_full maskrow_st ones_row const_pool const_step const_dve mask_rows_done zeros_st slot0_full
        slot0_free slot1_full slot1_free slot2_full slot2_free misc_full misc_free bn_step rstd_ready_a rstd_ready_f rstd_ready_c
        rstd_ready_e var_a var_f var_c var_e norm_a xres_a qk0_ready qk0_h qk0_l v0_ready qk0_st qk0_ld
        mask0_ld m0_h m0_st m0_ld pvdone_a den_a_s rec_a_s o_a_s x1_ready norm_f route_s comb_ready tanh_s
        actg_s inter_s x2_ready norm_c x2res_s amask_h amask_l qka_step qka_p2 qka_done vs_ready vx_ready
        c_st c_ld m1_step m1_st m1_ld pvdone_c den_c_s o_c_s norm_e exp_e route1_s onehot_s seen_s
        slot_ready scat_s disp_ld0 disp_ld1 disp_ld2 eo_full eo_sb eo_st0 eo_st1 gath0 gath1 gath2 gath3 gath4 gath5 gath6 gath7 comb_s out_st
        """.split()
        S = {n: sem(n) for n in names}

        def full(k):
            return S[f"slot{k}_full"]

        def free(k):
            return S[f"slot{k}_free"]

        qk_flat = QS0[:].rearrange("p h t -> p (h t)")

        def flat(tile):
            return tile[:].rearrange("p h t -> p (h t)")

        def apart(eng, semaphore, value):
            after(eng, semaphore, value)
            if not isinstance(value, int):
                eng.sem_inc(S[f"passed_{eng.engine.name}"], 1)

        def by_x(tile):
            return tile[:].rearrange("p (x m) t -> p x (m t)", x=3)

        block = stack.enter_context(nc.Block())

        LAST = NB + 2
        LOOP = (3, NB - 1)

        def iterations(eng, steps):
            def one(i):
                for kind, k in ORDER:
                    lag = LAG[kind]
                    if kind in steps and (not isinstance(i, int) or 0 <= i - lag < NB):
                        steps[kind](i - lag if lag else i, i, k)
            for i in range(-1, LOOP[0]):
                one(i)
            with eng.Fori(*LOOP) as i:
                one(i)
            for i in range(LOOP[1], LAST + 1):
                one(i)

        def before(region, step, i):
            return uses_before(region, step, i, NB)

        def attentions_done(lag, i):
            return min(max(i - lag, 0), NB) if isinstance(i, int) else i - lag

        def after(eng, semaphore, value):
            if not isinstance(value, int) or value > 0:
                eng.wait_ge(semaphore, value)

        @block.sync
        def _(sp):
            def wait(semaphore, value):
                if isinstance(value, int):
                    after(sp, semaphore, value)
                else:
                    apart(sp, semaphore, value)

            def load_a(b):
                sp.dma_start(x_in[:], x[b, :, :]).then_inc(S["load_a"], 16)
                sp.dma_start(ctx_a[:], ctx_in[b, :, :]).then_inc(S["load_a"], 16)
                sp.dma_start(tm_b[:], mask01[b, :, :].broadcast_to([P, D])).then_inc(S["load_a"], 16)
                sp.dma_start(sm_col[:], mask01_cols[b, :, :]).then_inc(S["load_a"], 16)

            def load_c(b):
                sp.dma_start(ctx_c[:], ctx_in[b, :, :]).then_inc(S["load_c"], 16)
                sp.dma_start(amask[:, 0, :], addmask[b, :, :]).then_inc(S["load_c"], 16)
                sp.dma_start(amask[:, 1, :], addmaskT[b, :, :]).then_inc(S["load_c"], 16)

            load_a(0)
            for dst, src in ((mask_tmp[:, 0, :], mask01.rearrange("b o t -> (b o) t")), (wq0_sb[:], wq0T),
                             (wk0_sb[:], wk0T), (wv0_sb[:], wv0T), (bq0_sb[:], bq0), (bk0_sb[:], bk0),
                             (bv0_sb[:], bv0)):
                sp.dma_start(dst, src).then_inc(S["load_w0"], 16)
            load_c(0)
            sp.dma_start(gate0_sb[:], gate0T.rearrange("(k p) e -> p k e", p=P)).then_inc(S["load_gu"], 16)
            for k in range(KT):
                sp.dma_start(gu_sb[:, k, :, :],
                             gate_up[:, k * P:(k + 1) * P, :].rearrange("e p f -> p e f")).then_inc(S["load_gu"], 16)
            for dst, src in ((wq1_sb, wq1), (wk1_sb, wk1), (wv1_sb, wv1), (gate1w_sb, gate1wT)):
                sp.dma_start(dst[:], src.rearrange("(k p) o -> p k o", p=P)).then_inc(S["load_w1"], 16)
            sp.dma_start(wo1_sb[:], wo1.rearrange("r p o -> p r o")).then_inc(S["load_w1"], 16)
            sp.dma_start(gate1_sb[:], gate1.broadcast_to([P, D])).then_inc(S["load_w1"], 16)
            sp.dma_start(rope_sb[:], rope).then_inc(S["load_w1"], 16)
            wait(S["const_pool"], 1)
            for n in range(4):
                sp.dma_start(flat(KS0)[126:128, 1024 * n:1024 * n + 1024].bitcast(F32), p[0:2, 0, :]).then_inc(S["ones_row"], 16)
            ones_bf = p[:, 1, :].bitcast(BF16)
            for n in range(2):
                sp.dma_start(flat(KS1)[122:125, 2048 * n:2048 * n + 2048], ones_bf[0:3, :]).then_inc(S["ones_row"], 16)
                sp.dma_start(flat(AS1)[125:128, 2048 * n:2048 * n + 2048], ones_bf[0:3, :]).then_inc(S["ones_row"], 16)
            for n in range((SLOTS + P) // P):
                sp.dma_start(disp_dram[n * P:(n + 1) * P, :], x1[:]).then_inc(S["zeros_st"], 16)
            sp.dma_start(eout_dram[SLOTS:SLOTS + P, :], x1[:]).then_inc(S["zeros_st"], 16)
            wait(S["mask_rows_done"], 1)
            sp.dma_start(mq_dram.rearrange("b r t -> b (r t)"),
                         mask_rows[:, 0:6, :].rearrange("b r t -> b (r t)")).then_inc(S["maskrow_st"], 16)
            sp.dma_start(mk_dram.rearrange("b r t -> b (r t)"),
                         mask_rows[:, 6:12, :].rearrange("b r t -> b (r t)")).then_inc(S["maskrow_st"], 16)
            wait(S["maskrow_st"], 32)
            sp.dma_start(dn_sb[:], down.rearrange("e i h -> i e h")).then_inc(S["load_gu"], 16)

            def load_wi(e):
                sp.dma_start(wi_sb[e % 4], wi[e, :, :].rearrange("(k p) i -> p k i", p=P)).then_inc(S[f"load_wi{e % 4}"], 16)

            def load_wo(e):
                sp.dma_start(wo_sb[e % 4], wo[e, :, :].rearrange("(k p) h -> p k h", p=P)).then_inc(S[f"load_wo{e % 4}"], 16)

            def next_a(b, i, k):
                if isinstance(b, int) and b == 0:
                    return
                wait(S["norm_a"], b)
                wait(S["xres_a"], b)
                wait(S["qk0_h"], b)
                wait(S["v0_ready"], 4 * b)
                load_a(b)

            def next_c(b, i, k):
                if isinstance(b, int) and b == 0:
                    return
                wait(S["amask_l"], b)
                wait(S["qka_done"], b)
                load_c(b)

            def a1(b, i, k):
                wait(S["qk0_h"], b + 1)
                wait(S["qk0_l"], b + 1)
                flat4 = qk0_dram.rearrange("s p t -> p s t")
                src = qk0_p[:].rearrange("p l q t -> p q l t").bitcast(F32)
                wait(S["qk0_ld"], 64 * b)
                sp.dma_start(flat4[:, 0:2, :], src[:, 0, :, :]).then_inc(S["qk0_st"], 16)
                sp.dma_start(flat4[:, 2:4, :], src[:, 1, :, :]).then_inc(S["qk0_st"], 16)
                sp.dma_start(flat4[:, 4, :], src[:, 1, 0, :]).then_inc(S["qk0_st"], 16)

            def stacks_a(b, i, k):
                wait(S["pvdone_a"], 8 * b)
                if isinstance(b, int) and b == 0:
                    wait(S["const_pool"], 2)
                wait(S["qk0_st"], 48 * b + 48)
                rows = qk0_dram.rearrange("s (d h) t -> (s d) (h t)", h=H0)
                sp.dma_start(flat(QS0)[0:16, :].bitcast(F32), rows[0:16, :]).then_inc(S["qk0_ld"], 16)
                sp.dma_start(flat(QS0)[16:32, :].bitcast(F32), rows[0:16, :]).then_inc(S["qk0_ld"], 16)
                sp.dma_start(flat(KS0)[0:16, :].bitcast(F32), rows[16:32, :]).then_inc(S["qk0_ld"], 16)
                sp.dma_start(flat(KS0)[16:32, :].bitcast(F32), rows[24:40, :]).then_inc(S["qk0_ld"], 16)
                mq = mq_dram[b, :, :].unsqueeze(1).broadcast_to([6, H0, D])
                mk = mk_dram[b, :, :].unsqueeze(1).broadcast_to([6, H0, D])
                sp.dma_start(QS0[32:38, :, :].bitcast(F32), mq).then_inc(S["mask0_ld"], 16)
                sp.dma_start(KS0[32:38, :, :].bitcast(F32), mk).then_inc(S["mask0_ld"], 16)

            def experts_free(b, i, k):
                if isinstance(b, int) and b == NB - 1:
                    wait(S["x2_ready"], NB)
                    wait(S["pvdone_a"], 8 * NB)
                    for e in range(3):
                        load_wi(e)
                        load_wo(e)

            def stacks_c(b, i, k):
                wait(S["qka_done"], b + 1)
                wait(S["c_ld"], 144 * b)
                dst = c_dram.rearrange("s m p t -> p s m t")
                for x_, (at, n) in enumerate(((0, 3), (3, 3), (8, 3))):
                    sp.dma_start(dst[:, at:at + n, :, :].rearrange("p s m t -> p (s m) t"),
                                 qka_p[:, x_, :, :].rearrange("p s (m t) -> p (s m) t", m=2)).then_inc(S["c_st"], 16)
                for x_, at in ((1, 6), (2, 11)):
                    sp.dma_start(dst[:, at:at + 2, :, :].rearrange("p s m t -> p (s m) t"),
                                 qka_p[:, x_, 0:2, :].rearrange("p s (m t) -> p (s m) t", m=2)).then_inc(S["c_st"], 16)
                if isinstance(b, int) and b == NB - 1:
                    wait(S["xres_a"], NB)
                    wait(S["v0_ready"], 4 * NB)
                    load_wi(3)
                    load_wo(3)
                wait(S["pvdone_c"], 8 * b)
                wait(S["c_st"], 80 * b + 80)
                rows = c_dram.rearrange("s m (d h) t -> (s m d) (h t)", h=H1)
                for w in range(3):
                    sp.dma_start(flat(QS1)[24 * w:24 * w + 24, :], rows[0:24, :]).then_inc(S["c_ld"], 16)
                    sp.dma_start(flat(KS1)[24 * w:24 * w + 24, :], rows[24 + 8 * w:48 + 8 * w, :]).then_inc(S["c_ld"], 16)
                    sp.dma_start(flat(AS1)[24 * w:24 * w + 24, :], rows[64 + 8 * w:88 + 8 * w, :]).then_inc(S["c_ld"], 16)

            def ma(b, i, k):
                wait(S["misc_free"], before("misc", ("MA", 0), i) + 1)
                wait(S["m0_ld"], 16 * b)
                sp.dma_start(m0_dram.rearrange("s r t -> r s t"), m0_p[:].bitcast(F32)).then_inc(S["m0_st"], 16)
                wait(S["m0_st"], 16 * b + 16)
                sp.dma_start(flat(QS0)[126:128, :].bitcast(F32),
                             m0_dram.rearrange("s r t -> s (r t)")).then_inc(S["m0_ld"], 16)

            def nc_(b, i, k):
                wait(S["m1_step"], 3 * b + 3)
                wait(S["m1_ld"], 16 * b)
                for kind in range(2):
                    sp.dma_start(m1_dram[kind, :, :, :].rearrange("s h t -> h s t"),
                                 m1_p[32 * kind:32 * kind + 32, :, :]).then_inc(S["m1_st"], 16)
                wait(S["m1_st"], 32 * b + 32)
                sp.dma_start(flat(QS1)[122:128, :], m1_dram.rearrange("k s h t -> (k s) (h t)")).then_inc(S["m1_ld"], 16)

            def w_(b, i, k):
                wait(S["misc_free"], before("misc", ("W", 0), i) + 1)
                sp.dma_start(x3_dram[b, :, :], x3_now[:]).then_inc(S["x3_copy"], 16)

            iterations(sp, {"IN": next_a, "INC": next_c, "A1": a1, "LS": stacks_a, "CS": stacks_c, "MA": ma, "NC": nc_,
                            "W": w_, "X2": experts_free})

            wait(S["scat_s"], 16 * NB)
            by_tile = disp_dram.rearrange("(n p) h -> p n h", p=P)
            sp.dma_start(p[:, 0, :].rearrange("p (n h) -> p n h", n=4), by_tile[:, 0:4, :]).then_inc(S["disp_ld0"], 16)
            sp.dma_start(p[:, 1, :].rearrange("p (n h) -> p n h", n=4), by_tile[:, 4:8, :]).then_inc(S["disp_ld1"], 16)
            sp.dma_start(rows_8, by_tile[:, 8:10, :]).then_inc(S["disp_ld2"], 16)
            wait(S["x3_copy"], 16 * NB)
            sp.dma_start(x3, x3_dram.rearrange("b p h -> p b h")).then_inc(S["x3_ld"], 16)

            def store_rows(e):
                for c in range(2):
                    rows = P if c == 0 else CAP - P
                    wait(S["eo_sb"], 2 * e + c + 1)
                    sp.dma_start(eout_dram[e * CAP + c * P:e * CAP + c * P + rows, :],
                                 p[0:rows, c, (e % 2) * D:(e % 2) * D + D]).then_inc(S[f"eo_st{e % 2}"], 16)

            for e in range(E1):
                if e + 4 < E1:
                    for u in range(2):
                        wait(full(u), all_uses(f"slot{u}", NB) + 2 - u + e + 1)
                    load_wi(e + 4)
                    wait(S["eo_full"], e + 1)
                    load_wo(e + 4)
                if e >= 1:
                    store_rows(e - 1)
            store_rows(E1 - 1)
            for b in range(NB):
                wait(S["comb_s"], b + 1)
                sp.dma_start(out[b, :, :], x3[:, b, :]).then_inc(S["out_st"], 16)
            wait(S["out_st"], 16 * NB)

        @block.gpsimd
        def _(pool):
            g = nc.gpsimd
            setup = [0]

            def step(ins):
                setup[0] += 1
                ins.then_inc(S["const_step"], 1)
                return setup[0]

            step(g.memset(minus_half[:], -0.5))
            step(g.memset(ident[:], 0.0))
            step(g.memset(tri[:], 1.0))
            step(g.memset(sel[:], 0.0))
            step(g.memset(x1[:], 0.0))
            step(g.memset(p[:, 0, :], 1.0))
            step(g.memset(p[:, 1, :].bitcast(BF16), 1.0))
            step(g.memset(seen[:], 0.0))
            step(g.memset(KS0[:].bitcast(F32), 0.0))
            step(g.memset(KS1[:], 0.0))
            n = step(g.memset(AS1[:], 0.0))
            pool.wait_ge(S["const_step"], n)
            g.affine_select(out=ident[:], in_=ident[:], compare_op=ALU.not_equal, fill=1.0, base=0,
                            pattern=[[-1, P]], channel_multiplier=1).then_inc(S["const_pool"], 1)
            step(g.memset(QS0[:].bitcast(F32), 0.0))
            step(g.memset(QS1[:], 0.0))
            step(g.iota(iota16[:], pattern=[[1, 16]], base=0, channel_multiplier=0,
                        allow_small_or_imprecise_dtypes=True))
            step(g.iota(dump_row[:], pattern=[[0, 1]], base=SLOTS, channel_multiplier=1,
                        allow_small_or_imprecise_dtypes=True))
            step(g.iota(ebase[:], pattern=[[CAP, E1]], base=0, channel_multiplier=0,
                        allow_small_or_imprecise_dtypes=True))
            n = step(g.affine_select(out=tri[:], in_=tri[:], compare_op=ALU.is_ge, fill=0.0, base=0,
                                 pattern=[[1, P]], channel_multiplier=-1))
            for j in range(4):
                for r in range(2):
                    pool.wait_ge(S["const_step"], n)
                    v = sel[32 * j:32 * j + 32, r, 64 * r + 16 * j:64 * r + 16 * j + 16]
                    n = step(g.affine_select(out=v, in_=v, compare_op=ALU.not_equal, fill=1.0, base=0,
                                             pattern=[[-1, 16]], channel_multiplier=1))
            pool.wait_ge(S["const_step"], n)
            for t in (vst0[:].rearrange("p s k c -> p (s k) c"), vst_s[:], vst_x[:]):
                n = step(g.memset(t, 0.0))
            pool.wait_ge(S["const_step"], n)
            for t in (vst0[:].rearrange("p s k c -> p (s k) c"), vst_s[:], vst_x[:]):
                step(g.memset(t[:, :, 16:24], 1.0))
                n = step(g.memset(t[:, :, 56:64], 1.0))
            pool.wait_ge(S["const_step"], n)
            g.memset(ones[:], 1.0).then_inc(S["const_pool"], 1)

            def rsqrt(k, b):
                pool.wait_ge(S[f"var_{k}"], b + 1)
                g.tensor_tensor(rstd[k][:], mv[k][:, 1:2], minus_half[:], ALU.pow).then_inc(S[f"rstd_ready_{k}"], 1)

            def la(b, i, k):
                rsqrt("a", b)
                after(pool, S["qk0_h"], b)
                apart(pool, S["load_a"], 64 * b + 64)
                g.tensor_scalar(tms_b[:], tm_b[:], float(HD) ** -0.5, 1.0, ALU.mult, ALU.mult).then_inc(S["tms_s"], 1)

            def ar(b, i, k):
                after(pool, S["load_a"], 64 * b + 64)
                apart(pool, S["x1_ready"], b)
                g.tensor_copy(tm_keep[:], tm_b[:])
                g.tensor_copy(x_res[:], x_in[:]).then_inc(S["xres_a"], 1)

            def xr(b, i, k):
                after(pool, S["bn_e"], 2 * b)
                apart(pool, S["x2_ready"], b + 1)
                g.tensor_copy(x2_res[:], x2[:]).then_inc(S["x2res_s"], 1)

            def lc(b, i, k):
                rsqrt("c", b)

            def lf(b, i, k):
                rsqrt("f", b)

            def cp(b, i, k):
                after(pool, S["c_st"], 80 * b)
                apart(pool, S["slot2_free"], before("slot2", ("C1", 0), i) + 1)
                g.tensor_copy(qka_p[:, :, 0, :], by_x(qka_r)).then_inc(S["qka_p1"], 1)
                pool.wait_ge(S["qka_p1"], 2 * b + 1)
                g.tensor_tensor(by_x(qka), by_x(qka_r), qka_p[:, :, 0, :], ALU.subtract).then_inc(S["qka_p1"], 1)
                apart(pool, S["qka_p1"], 2 * b + 2)
                g.tensor_copy(qka_p[:, :, 1, :], by_x(qka)).then_inc(S["qka_p2"], 1)
                pool.wait_ge(S["qka_p2"], b + 1)
                g.tensor_tensor(qka_p[:, :, 2, :], by_x(qka), qka_p[:, :, 1, :], ALU.subtract).then_inc(S["qka_done"], 1)

            def x_(b, i, c):
                pool.wait_ge(S["comb_ready"], b + 1)
                pool.wait_ge(free(c % 2), before(f"slot{c % 2}", ("G", 2 * c), i) + 1)
                share = route[:, 7, 4 * c:4 * c + 4].unsqueeze(2).broadcast_to([P, 4, P])
                g.tensor_tensor(inter[:, c % 2, :, :], inter[:, c % 2, :, :], share,
                                ALU.mult).then_inc(S["inter_s"], 1)

            def w_(b, i, k):
                rsqrt("e", b)

            def r2(b, i, k):
                pool.wait_ge(S["norm_e"], b + 1)
                apart(pool, S["slot_ready"], b + 1)
                if isinstance(b, int) and b == 0:
                    pool.wait_ge(S["zeros_st"], 16 * (SLOTS // P + 2))
                g.indirect_dma_start(disp_dram, bass.IndirectOffsetOnAxis(ap=slot_now[:], axis=0),
                                     normed["e"][:], None).then_inc(S["scat_s"], 16)

            iterations(pool, {"LA": la, "AR": ar, "XR": xr, "LC": lc, "LF": lf, "CP": cp, "X": x_, "W": w_, "R2": r2})

            for k in range(2):
                pool.wait_ge(S[f"eo_st{k}"], 32 * E1 // 2)
            for b in range(NB):
                g.indirect_dma_start(p[:, b // 4, (b % 4) * D:(b % 4 + 1) * D], None, eout_dram,
                                     bass.IndirectOffsetOnAxis(ap=slot_u[:, b:b + 1], axis=0)).then_inc(S[f"gath{b}"], 16)

        @block.vector
        def _(dve):
            v = nc.vector

            def norm_stats(k, src, b):
                v.bn_stats(bn[k][:], src).then_inc(S[f"bn_{k}"], 1)
                apart(dve, S[f"bn_{k}"], 2 * b + 1)
                v.bn_aggr(mv[k][:], bn[k][:]).then_inc(S[f"bn_{k}"], 1)
                dve.wait_ge(S[f"bn_{k}"], 2 * b + 2)
                v.tensor_scalar_add(mv[k][:, 1:2], mv[k][:, 1:2], EPS).then_inc(S[f"var_{k}"], 1)

            def norm_apply(k, src, b):
                dve.wait_ge(S[f"rstd_ready_{k}"], b + 1)
                v.tensor_scalar(normed[k][:], src, mv[k][:, 0:1], rstd[k][:], ALU.subtract,
                                ALU.mult).then_inc(S[f"norm_{k}"], 1)

            dve.wait_ge(S["load_w0"], 16 * 7)
            steps = [0]

            def link(ins):
                steps[0] += 1
                ins.then_inc(S["const_dve"], 1)
                dve.wait_ge(S["const_dve"], steps[0])

            mh = qk0_p[0:NB, 0, 0, :]
            mask, w_, low = mask_tmp[:, 0, :], mask_tmp[:, 1, :], mask_tmp[:, 2, :]
            link(v.tensor_scalar(w_, mask, 1.0, NEG, ALU.subtract, ALU.mult))
            link(v.tensor_copy(mh, mask))
            link(v.tensor_tensor(low, mask, mh.bitcast(F32), ALU.subtract))
            for r in (0, 1):
                v.tensor_copy(mask_rows[:, r, :], mh.bitcast(F32))
                link(v.tensor_copy(mask_rows[:, 2 + r, :], low))
            link(v.tensor_copy(mh, w_))
            link(v.tensor_tensor(low, w_, mh.bitcast(F32), ALU.subtract))
            for r in (4, 6, 8):
                v.tensor_copy(mask_rows[:, r, :], mh.bitcast(F32))
                link(v.tensor_copy(mask_rows[:, r + 1, :], low))
            link(v.memset(mask_rows[:, 10, :], 1.0))
            v.memset(mask_rows[:, 11, :], 1.0).then_inc(S["mask_rows_done"], 1)
            dve.wait_ge(S["const_pool"], 1)
            v.tensor_copy(ident_r[:], ident[:]).then_inc(S["const_dve"], 1)
            identr_step = steps[0] + 1
            dve.wait_ge(S["const_pool"], 2)

            def la(b, i, k):
                dve.wait_ge(S["load_a"], 64 * b + 64)
                norm_stats("a", x_in[:], b)
                norm_apply("a", x_in[:], b)

            def a1(b, i, k):
                n = before("slot0", ("A1", 0), i)
                dve.wait_ge(full(0), n + 1)
                dve.wait_ge(S["tms_s"], b + 1)
                v.scalar_tensor_tensor(qk0[:, 0, :], slot[0][:, 0:D], bq0_sb[:], tms_b[:], ALU.add,
                                       ALU.mult).then_inc(S["qk0_ready"], 1)
                v.scalar_tensor_tensor(qk0[:, 1, :], slot[0][:, D:2 * D], bk0_sb[:], tm_b[:], ALU.add,
                                       ALU.mult).then_inc(free(0), 1)
                after(dve, S["qk0_st"], 48 * b)
                dve.wait_ge(S["qk0_ready"], b + 1)
                dve.wait_ge(free(0), n + 1)
                v.tensor_copy(qk0_p[:, 0, :, :], qk0[:]).then_inc(S["qk0_h"], 1)
                dve.wait_ge(S["qk0_h"], b + 1)
                v.tensor_tensor(qk0_p[:, 1, :, :], qk0[:], qk0_p[:, 0, :, :].bitcast(F32),
                                ALU.subtract).then_inc(S["qk0_l"], 1)

            def am(b, i, k):
                dve.wait_ge(S["load_c"], 48 * b + 48)
                after(dve, S["pvdone_c"], 8 * b)
                v.tensor_copy(amask_p[:, 0, :, :], amask[:]).then_inc(S["amask_h"], 1)
                dve.wait_ge(S["amask_h"], b + 1)
                v.tensor_tensor(amask_p[:, 1, :, :], amask[:], amask_p[:, 0, :, :].bitcast(F32),
                                ALU.subtract).then_inc(S["amask_l"], 1)

            def lc(b, i, k):
                dve.wait_ge(S["x2_ready"], b + 1)
                norm_stats("c", x2[:], b)
                norm_apply("c", x2[:], b)

            def cr(b, i, k):
                n = before("slot2", ("C1", 0), i)
                dve.wait_ge(full(2), n + 1)
                ps = slot[2][:, 0:512].rearrange("p (x m t) -> p x m t", x=2, m=2)
                cos = rope_sb[:, 0:4, :].rearrange("p (x m) t -> p x m t", x=2)
                sin = rope_sb[:, 4:8, :].rearrange("p (x m) t -> p x m t", x=2)
                r = qka_r[:, 0:4, :].rearrange("p (x m) t -> p x m t", x=2)
                s_ = qka[:, 0:4, :].rearrange("p (x m) t -> p x m t", x=2)
                after(dve, S["qka_done"], b)
                v.tensor_tensor(r, ps, cos, ALU.mult).then_inc(S["qka_step"], 1)
                v.tensor_tensor(s_[:, :, 0, :], ps[:, :, 1, :], sin[:, :, 0, :], ALU.mult).then_inc(S["qka_step"], 1)
                v.tensor_tensor(s_[:, :, 1, :], ps[:, :, 0, :], sin[:, :, 1, :], ALU.mult).then_inc(S["qka_step"], 1)
                dve.wait_ge(S["qka_step"], 3 * b + 3)
                dve.wait_ge(S["qka_a"], b + 1)
                v.tensor_tensor(qka_r[:, 0:4, :], qka_r[:, 0:4, :], qka[:, 0:4, :], ALU.add).then_inc(free(2), 1)

            def vc(b, i, k):
                dve.wait_ge(S["misc_full"], before("misc", ("VC", 0), i) + 1)
                after(dve, S["pvdone_c"], 8 * b)
                dve.wait_ge(S["vs_ready"], 2 * b + 2)
                for hh in range(2):
                    src = misc[:, D:2 * D].rearrange("p (k x) -> p k x", x=16)[:, :, 8 * hh:8 * hh + 8]
                    gt = gate1_sb[:].rearrange("p (k x) -> p k x", x=16)[:, :, 8 * hh:8 * hh + 8]
                    last = v.tensor_tensor(vst_x[:, :, 40 * hh:40 * hh + 8], src, gt, ALU.mult)
                    last.then_inc(S["vx_ready" if hh == 0 else "misc_free"], 1)

            ROUTE0 = 12

            def lf(b, i, k):
                dve.wait_ge(S["x1_ready"], b + 1)
                norm_stats("f", x1[:], b)
                norm_apply("f", x1[:], b)

            def rt(b, i, k):
                count = [0]

                def rs(ins, wait=True):
                    count[0] += 1
                    ins.then_inc(S["route_s"], 1)
                    if wait:
                        apart(dve, S["route_s"], ROUTE0 * b + count[0])

                dve.wait_ge(S["misc_free"], before("misc", ("F1", 0), i) + 1)
                after(dve, S["inter_s"], 4 * b)
                rs(v.tensor_scalar_add(route[:, 1, :], route[:, 0, :], 1.0))
                rs(v.reciprocal(route[:, 2, :], route[:, 1, :]))
                rs(v.reduce_sum(rsmall[:, 0:1], route[:, 2, :], AX.X))
                rs(v.reciprocal(rsmall[:, 1:2], rsmall[:, 0:1]))
                rs(v.tensor_scalar(route[:, 3, :], route[:, 2, :], rsmall[:, 1:2], None, ALU.mult))
                rs(v.max(top8[:], route[:, 3, :]))
                rs(v.max_index(top8i[:], top8[:], route[:, 3, :]))
                rs(v.tensor_copy(rsmall[:, 2:4], top8i[:, 0:2]))
                rs(v.tensor_tensor(rsmall[:, 4:5], top8[:, 0:1], top8[:, 1:2], ALU.add))
                rs(v.reciprocal(rsmall[:, 5:6], rsmall[:, 4:5]))
                rs(v.tensor_scalar(rsmall[:, 6:8], top8[:, 0:2], rsmall[:, 5:6], 0.5, ALU.mult, ALU.mult))
                v.tensor_scalar(route[:, 4, :], iota16[:], rsmall[:, 2:3], rsmall[:, 6:7], ALU.is_equal, ALU.mult)
                rs(v.tensor_scalar(route[:, 5, :], iota16[:], rsmall[:, 3:4], rsmall[:, 7:8], ALU.is_equal, ALU.mult))
                v.tensor_tensor(route[:, 7, :], route[:, 4, :], route[:, 5, :], ALU.add).then_inc(S["comb_ready"], 1)
                assert count[0] == ROUTE0

            def x_(b, i, c):
                k = c % 2
                ps = slot[k][:].rearrange("p (e g i) -> p e g i", e=4, g=2)
                dve.wait_ge(S["tanh_s"], 4 * b + c + 1)
                v.scalar_tensor_tensor(tanh_g[:, k, :, :], tanh_g[:, k, :, :], 1.0, ps[:, :, 0, :], ALU.add,
                                       ALU.mult).then_inc(S["actg_s"], 1)
                dve.wait_ge(S["actg_s"], 4 * b + c + 1)
                if c >= 2:
                    dve.wait_ge(S["misc_free"], before("misc", ("T", c - 2), i) + 1)
                v.tensor_tensor(inter[:, k, :, :], tanh_g[:, k, :, :], ps[:, :, 1, :],
                                ALU.mult).then_inc(free(k), 1)

            def x2_(b, i, k):
                dve.wait_ge(S["dn_chunk"], 4 * b + 4)
                after(dve, S["x2res_s"], b)
                v.tensor_tensor(x2[:], x1[:], pv0[:, 0:D], ALU.add).then_inc(S["x2_ready"], 1)

            def m_(b, i, g_):
                dve.wait_ge(full(2), before("slot2", ("M", g_), i) + 1)
                hg, tt = g_ % 4, g_ // 4
                v.reduce_max(mx0[:, 4 * hg:4 * hg + 4, tt], slot[2][:].rearrange("p (h s) -> p h s", h=4),
                             AX.X).then_inc(free(2), 1)

            def ma(b, i, k):
                n = before("misc", ("MA", 0), i)
                dve.wait_ge(S["misc_full"], n + 1)
                after(dve, S["m0_st"], 16 * b)
                v.tensor_scalar(m0_p[:, 0, :], misc[0:32, 0:P], -1.0, None, ALU.mult).then_inc(S["m0_h"], 1)
                dve.wait_ge(S["m0_h"], b + 1)
                v.scalar_tensor_tensor(m0_p[:, 1, :], misc[0:32, 0:P], -1.0, m0_p[:, 0, :].bitcast(F32), ALU.mult,
                                       ALU.subtract).then_inc(S["misc_free"], 1)

            def n_(b, i, g_):
                dve.wait_ge(full(2), before("slot2", ("N", g_), i) + 1)
                kind, r = g_ // 4, g_ % 4
                v.reduce_max(mx1[:, kind, 8 * r:8 * r + 8], slot[2][:].rearrange("p (h s) -> p h s", h=8),
                             AX.X).then_inc(free(2), 1)

            def nc_(b, i, k):
                n = before("misc", ("NC", 0), i)
                dve.wait_ge(S["misc_full"], n + 1)
                after(dve, S["m1_st"], 32 * b)
                v.tensor_scalar(m1_p[:, 0, :], misc[0:64, 0:P], -1.0, None, ALU.mult).then_inc(S["m1_step"], 1)
                dve.wait_ge(S["m1_step"], 3 * b + 1)
                v.scalar_tensor_tensor(m1_f[:, 0, :], misc[0:64, 0:P], -1.0, m1_p[:, 0, :], ALU.mult,
                                       ALU.subtract).then_inc(S["misc_free"], 1)
                dve.wait_ge(S["misc_free"], n + 1)
                v.tensor_copy(m1_p[:, 1, :], m1_f[:, 0, :]).then_inc(S["m1_step"], 1)
                dve.wait_ge(S["m1_step"], 3 * b + 2)
                v.tensor_tensor(m1_p[:, 2, :], m1_f[:, 0, :], m1_p[:, 1, :], ALU.subtract).then_inc(S["m1_step"], 1)

            to_sums = [16 + j % 16 for j in range(32)]

            def on(b, i, k):
                apart(dve, S["pvdone_a"], 8 * b + 8)
                v.stream_shuffle(den_a, pv0[:], to_sums).then_inc(S["den_a_s"], 1)
                dve.wait_ge(S["den_a_s"], b + 1)
                v.reciprocal(rec_a, den_a).then_inc(S["rec_a_s"], 1)
                dve.wait_ge(S["rec_a_s"], b + 1)
                v.tensor_tensor(o_a[:].rearrange("p r t -> p (r t)"), pv0[:], rec_a, ALU.mult).then_inc(S["o_a_s"], 1)

            def a4(b, i, k):
                n = before("misc", ("A4", 0), i)
                dve.wait_ge(S["xres_a"], b + 1)
                dve.wait_ge(S["misc_full"], n + 1)
                v.tensor_tensor(rec_a[:, 0:D], misc[:, 0:D], tm_keep[:],
                                ALU.mult).then_inc(S["misc_free"], 1)
                dve.wait_ge(S["misc_free"], n + 1)
                if isinstance(b, int) and b == 0:
                    dve.wait_ge(S["zeros_st"], 16 * (SLOTS // P + 2))
                v.tensor_tensor(x1[:], rec_a[:, 0:D], x_res[:], ALU.add).then_inc(S["x1_ready"], 1)

            ROUTE1 = 17

            def normalise(b, kind, pv):
                apart(dve, S["pvdone_c"], 8 * b + 4 * kind + 4)
                v.stream_shuffle(den[:, 0, :], pv, to_sums).then_inc(S["den_c_s"], 1)
                dve.wait_ge(S["den_c_s"], 4 * b + 2 * kind + 1)
                v.reciprocal(den[:, 1, :], den[:, 0, :]).then_inc(S["den_c_s"], 1)
                dve.wait_ge(S["den_c_s"], 4 * b + 2 * kind + 2)
                o = o_c[:].rearrange("p r t -> p (r t)")
                if kind == 0:
                    v.tensor_tensor(o, pv, den[:, 1, :], ALU.mult).then_inc(S["o_c_s"], 1)
                else:
                    v.tensor_tensor(den[:, 0, :], pv, den[:, 1, :], ALU.mult).then_inc(S["o_c_s"], 1)
                    dve.wait_ge(S["o_c_s"], 3 * b + 2)
                    v.tensor_tensor(o, o, den[:, 0, :], ALU.add).then_inc(S["o_c_s"], 1)

            def os_(b, i, k):
                normalise(b, 0, pvs)

            def ox(b, i, k):
                normalise(b, 1, pvx)

            def w_(b, i, k):
                n = before("misc", ("W", 0), i)
                dve.wait_ge(S["misc_full"], n + 1)
                dve.wait_ge(S["x2res_s"], b + 1)
                after(dve, S["x3_copy"], 16 * b)
                v.tensor_tensor(x3_now[:], misc[:, 0:D], x2_res[:],
                                ALU.add).then_inc(S["misc_free"], 1)
                dve.wait_ge(S["misc_free"], n + 1)
                norm_stats("e", x3_now[:], b)
                after(dve, S["scat_s"], 16 * b)
                norm_apply("e", x3_now[:], b)

            def steps_of_route1(b, done):
                count = [done]

                def rs(ins, wait=True):
                    count[0] += 1
                    ins.then_inc(S["route1_s"], 1)
                    if wait:
                        apart(dve, S["route1_s"], ROUTE1 * b + count[0])
                return count, rs

            def r1(b, i, k):
                count, rs = steps_of_route1(b, 0)

                n = before("misc", ("R1", 0), i)
                dve.wait_ge(S["misc_full"], n + 1)
                after(dve, S["exp_e"], b)
                v.tensor_copy(lg1[:, 0, :], misc[:, 0:E1]).then_inc(S["misc_free"], 1)
                apart(dve, S["misc_free"], n + 1)
                rs(v.max(top1[:], lg1[:, 0, :]))
                rs(v.max_index(top1i[:], top1[:], lg1[:, 0, :]))
                rs(v.tensor_scalar(small1[:, 0:1], top1[:, 0:1], -1.0, None, ALU.mult))
                rs(v.tensor_copy(small1[:, 1:2], top1i[:, 0:1]))
                v.tensor_scalar(one_hot1[:], iota16[:, 0:E1], small1[:, 1:2], None,
                                ALU.is_equal).then_inc(S["onehot_s"], 1)
                dve.wait_ge(S["exp_e"], b + 1)
                rs(v.reciprocal(small1[:, 3:4], small1[:, 2:3]))
                assert count[0] == 5

            def r2(b, i, k):
                count, rs = steps_of_route1(b, 5)
                n = before("misc", ("R2", 0), i)
                dve.wait_ge(S["onehot_s"], b + 1)
                dve.wait_ge(S["misc_full"], n + 1)
                rs(v.scalar_tensor_tensor(lg1[:, 1, :], misc[:, 0:E1], -1.0, one_hot1[:], ALU.add, ALU.mult))
                v.scalar_tensor_tensor(lg1[:, 2, :], misc[:, 0:E1], -1.0, ebase[:], ALU.add,
                                       ALU.add).then_inc(S["misc_free"], 1)
                dve.wait_ge(S["misc_free"], n + 1)
                rs(v.tensor_tensor(lg1[:, 3, :], lg1[:, 2, :], one_hot1[:], ALU.mult))
                rs(v.reduce_sum(small1[:, 4:5], lg1[:, 1, :], AX.X))
                rs(v.reduce_sum(small1[:, 5:6], lg1[:, 3, :], AX.X))
                v.tensor_tensor(seen[:], seen[:], one_hot1[:], ALU.add).then_inc(S["seen_s"], 1)
                rs(v.tensor_scalar(small1[:, 6:7], small1[:, 4:5], float(CAP), None, ALU.is_lt))
                rs(v.tensor_tensor(small1[:, 7:8], small1[:, 5:6], dump_row[:], ALU.subtract))
                rs(v.tensor_scalar(lg1[:, 4, 0:1], small1[:, 7:8], small1[:, 6:7], dump_row[:], ALU.mult, ALU.add))
                rs(v.tensor_tensor(wgt[:, bass.ds(b, 1)], small1[:, 3:4], small1[:, 6:7], ALU.mult))
                rs(v.tensor_copy(slot_u[:, bass.ds(b, 1)], lg1[:, 4, 0:1]))
                v.tensor_copy(slot_now[:], lg1[:, 4, 0:1]).then_inc(S["slot_ready"], 1)
                while count[0] < ROUTE1:
                    rs(v.tensor_copy(lg1[:, 5, 0:1], lg1[:, 4, 0:1]))
                assert count[0] == ROUTE1

            iterations(dve, {"LA": la, "A1": a1, "AM": am, "LC": lc, "CR": cr, "VC": vc, "LF": lf, "RT": rt, "X": x_,
                             "X2": x2_, "M": m_, "MA": ma, "N": n_, "NC": nc_, "ON": on, "A4": a4, "OS": os_, "OX": ox,
                             "W": w_, "R1": r1, "R2": r2})

            dve.wait_ge(full(1), all_uses("slot1", NB) + 1)
            v.tensor_copy(dispT[:, :, 4 * P:8 * P].rearrange("p k (n t) -> p n k t", n=4),
                          slot[1][:].rearrange("p (n k t) -> p n k t", n=4, k=KT)).then_inc(free(1), 1)

            def rows_out(e):
                dve.wait_ge(S["eoT_full"], e + 1)
                if e >= 2:
                    dve.wait_ge(S[f"eo_st{e % 2}"], 32 * (e // 2))
                for c in range(2):
                    rows = P if c == 0 else CAP - P
                    v.tensor_copy(p[0:rows, c, (e % 2) * D:(e % 2) * D + D],
                                  slot[2][0:rows, c * 512:c * 512 + D]).then_inc(S["eo_sb"], 1)

            for e in range(E1):
                dve.wait_ge(S["eo_full"], e + 1)
                if e >= 2:
                    dve.wait_ge(S["eoT_full"], e - 1)
                v.tensor_copy(oT[e % 2], pv0[:, 0:KT * CAP].rearrange("p (m c) -> p m c", m=KT)).then_inc(S["oT_ready"], 1)
                if e >= 1:
                    rows_out(e - 1)
            rows_out(E1 - 1)
            for b in range(NB):
                dve.wait_ge(S[f"gath{b}"], 16)
                dve.wait_ge(S["x3_ld"], 16)
                v.scalar_tensor_tensor(x3[:, b, :], p[:, b // 4, (b % 4) * D:(b % 4 + 1) * D], wgt[:, b:b + 1], x3[:, b, :],
                                       ALU.mult, ALU.add).then_inc(S["comb_s"], 1)

        @block.scalar
        def _(act):
            a = nc.scalar
            def copy_misc(dst, cols, use):
                act.wait_ge(S["misc_full"], use + 1)
                a.activation(dst, misc[:, 0:cols], ACT.Copy).then_inc(S["misc_free"], 1)

            def va(b, i, k):
                n = before("misc", ("VA", 0), i)
                after(act, S["pvdone_a"], 8 * b)
                if isinstance(b, int) and b == 0:
                    act.wait_ge(S["const_pool"], 2)
                act.wait_ge(S["load_a"], 64 * b + 64)
                act.wait_ge(S["misc_full"], n + 1)
                for st in range(2):
                    for hh in range(2):
                        src = misc[:, st * P:st * P + P].rearrange("p (k x) -> p k x", x=16)
                        ins = a.activation(vst0[:, st, :, 40 * hh:40 * hh + 8], src[:, :, 8 * hh:8 * hh + 8], ACT.Copy,
                                           scale=sm_col[:, st:st + 1])
                        ins.then_inc(S["v0_ready"], 1)
                act.wait_ge(S["v0_ready"], 4 * b + 4)
                act.sem_inc(S["misc_free"], 1)

            def c0(b, i, k):
                copy_misc(nT[:].rearrange("p k t -> p (k t)"), 512, before("misc", ("C0", 0), i))

            def c1(b, i, k):
                act.wait_ge(full(2), before("slot2", ("C1", 0), i) + 1)
                after(act, S["qka_done"], b)
                a.activation(qka_r[:, 4:6, :].rearrange("p k t -> p (k t)"), slot[2][:, 512:768],
                             ACT.Copy).then_inc(S["qka_a"], 1)

            def vc(b, i, k):
                if isinstance(b, int) and b == 0:
                    act.wait_ge(S["load_w1"], 16 * 7)
                    a.activation(gate1_sb[:], gate1_sb[:], ACT.Tanh).then_inc(S["gate1_s"], 1)
                act.wait_ge(S["misc_full"], before("misc", ("VC", 0), i) + 1)
                after(act, S["pvdone_c"], 8 * b)
                if isinstance(b, int) and b == 0:
                    act.wait_ge(S["const_pool"], 2)
                    act.wait_ge(S["gate1_s"], 1)
                for hh in range(2):
                    src = misc[:, 0:D].rearrange("p (k x) -> p k x", x=16)[:, :, 8 * hh:8 * hh + 8]
                    a.activation(vst_s[:, :, 40 * hh:40 * hh + 8], src, ACT.Copy).then_inc(S["vs_ready"], 1)

            def f0(b, i, k):
                after(act, S["dn_chunk"], 4 * b)
                copy_misc(n1T[:].rearrange("p k t -> p (k t)"), KT * P, before("misc", ("F0", 0), i))

            def f1(b, i, k):
                after(act, S["comb_ready"], b)
                act.wait_ge(S["misc_full"], before("misc", ("F1", 0), i) + 1)
                a.activation(route[:, 0, :], misc[:, 0:E0], ACT.Exp,
                             scale=-1.0).then_inc(S["misc_free"], 1)

            def x_(b, i, c):
                k = c % 2
                act.wait_ge(full(k), before(f"slot{k}", ("G", 2 * c), i) + 1)
                after(act, S["actg_s"], 4 * b + c - 1)
                ps = slot[k][:].rearrange("p (e g i) -> p e g i", e=4, g=2)
                a.activation(tanh_g[:, k, :, :], ps[:, :, 0, :], ACT.Tanh, scale=0.5).then_inc(S["tanh_s"], 1)

            def t_(b, i, c):
                after(act, S["dn_chunk"], 4 * b + c - 1)
                copy_misc(interT[:, c % 2, :, :].rearrange("p e t -> p (e t)"), 512, before("misc", ("T", c), i))

            def a3(b, i, g_):
                if g_ == 8:
                    return
                k = g_ % 2
                act.wait_ge(full(k), before(f"slot{k}", ("A3", g_), i) + 1)
                ran_c = attentions_done(2, i)
                if g_ >= 2 or (isinstance(ran_c, int) and ran_c == 0):
                    after(act, S["pvdone_a"], 8 * b + g_ - 1)
                else:
                    act.wait_ge(S["pvdone_c"], 8 * ran_c + g_ - 1)
                if isinstance(b, int) and b == 0 and g_ < 2:
                    act.wait_ge(S["ones_row"], 16 * 8)
                a.activation(p[:, k, :], slot[k][:], ACT.Exp).then_inc(free(k), 1)

            def c3(b, i, g_):
                if g_ == 8:
                    return
                k = g_ % 2
                act.wait_ge(full(k), before(f"slot{k}", ("C3", g_), i) + 1)
                if g_ >= 2 or (isinstance(i, int) and i >= NB):
                    after(act, S["pvdone_c"], 8 * b + g_ - 1)
                else:
                    act.wait_ge(S["pvdone_a"], 8 * i + g_ + 7)
                a.activation(p[:, k, :], slot[k][:], ACT.Exp).then_inc(free(k), 1)

            def r0(b, i, k):
                after(act, S["route1_s"], 17 * b)
                copy_misc(n3T[:].rearrange("p k t -> p (k t)"), KT * P, before("misc", ("R0", 0), i))

            def r1(b, i, k):
                act.wait_ge(S["route1_s"], 17 * b + 3)
                a.activation(lg1[:, 5, :], lg1[:, 0, :], ACT.Exp, bias=small1[:, 0:1],
                             accum_out=small1[:, 2:3]).then_inc(S["exp_e"], 1)

            iterations(act, {"VA": va, "C0": c0, "C1": c1, "VC": vc, "F0": f0, "F1": f1, "X": x_, "T": t_, "A3": a3,
                             "C3": c3, "R0": r0, "R1": r1})

            base = [all_uses(f"slot{k}", NB) for k in range(2)]
            for n, (at, tiles) in enumerate(((0, 4), (8, 2))):
                act.wait_ge(full(0), base[0] + n + 1)
                if n == 0:
                    act.wait_ge(S["dn_chunk"], 4 * NB)
                a.activation(dispT[:, :, at * P:(at + tiles) * P].rearrange("p k (n t) -> p n k t", n=tiles),
                             slot[0][:, 0:tiles * D].rearrange("p (n k t) -> p n k t", n=tiles, k=KT),
                             ACT.Copy).then_inc(free(0), 1)
            for e in range(E1):
                for u in range(2):
                    act.wait_ge(full(u), base[u] + 2 - u + e + 1)
                    if e >= 2:
                        act.wait_ge(S["eo_full"], e - 1)
                    src = slot[u][:].rearrange("p (k n) -> p k n", k=2)[:, :, 0:2 * CAP]
                    dst = hT[e % 2][:, 4 * u:4 * u + 4, :].rearrange("p (k i) c -> p k (i c)", k=2)
                    a.activation(dst, src, ACT.Gelu).then_inc(free(u), 1)

        @block.tensor
        def _(pe):
            t = nc.tensor

            def take(region, use):
                after(pe, S[f"{region}_free"], use)

            def take_slot2(i, use):
                after(pe, S["o_c_s"], 3 * attentions_done(2, i))
                take("slot2", use)

            def a1(b, i, k):
                take("slot0", before("slot0", ("A1", 0), i))
                if isinstance(b, int) and b == 0:
                    pe.wait_ge(S["load_w0"], 16 * 7)
                    pe.wait_ge(S["const_pool"], 2)
                pe.wait_ge(S["load_a"], 64 * b + 64)
                ps = slot[0]
                t.matmul(ps[:, D:2 * D], wk0_sb[:], ctx_a[:], start=True, stop=True)
                pe.wait_ge(S["norm_a"], b + 1)
                t.matmul(ps[:, 0:D], wq0_sb[:], normed["a"][:], start=True, stop=True).then_inc(full(0), 1)

            def va(b, i, k):
                take("misc", before("misc", ("VA", 0), i))
                for st in range(2):
                    o = misc[:, st * P:(st + 1) * P]
                    t.matmul(o, ctx_a[:, st * P:(st + 1) * P], wv0_sb[:], start=True, stop=False)
                    last = t.matmul(o, ones[0:1, :], bv0_sb[:], start=False, stop=True)
                last.then_inc(S["misc_full"], 1)

            def c0(b, i, k):
                take("misc", before("misc", ("C0", 0), i))
                pe.wait_ge(S["load_c"], 48 * b + 48)
                for k in range(KT):
                    t.transpose(misc[:, (2 + k) * P:(3 + k) * P], ctx_c[:, k * P:(k + 1) * P], ident[:])
                pe.wait_ge(S["norm_c"], b + 1)
                for k in range(KT):
                    last = t.transpose(misc[:, k * P:(k + 1) * P], normed["c"][:, k * P:(k + 1) * P], ident[:])
                last.then_inc(S["misc_full"], 1)

            def c1(b, i, k):
                take_slot2(i, before("slot2", ("C1", 0), i))
                pe.wait_ge(S["misc_free"], before("misc", ("C0", 0), i) + 1)
                if isinstance(b, int) and b == 0:
                    pe.wait_ge(S["load_w1"], 16 * 7)
                for x_, w, src in ((0, wq1_sb, 0), (1, wk1_sb, 0), (2, wk1_sb, 2)):
                    for mt in range(2):
                        at = (2 * x_ + mt) * P
                        for k in range(KT):
                            last = t.matmul(slot[2][:, at:at + P], w[:, k, mt * P:(mt + 1) * P], nT[:, src + k, :],
                                            start=(k == 0), stop=(k == KT - 1))
                last.then_inc(full(2), 1)

            def vc(b, i, k):
                take("misc", before("misc", ("VC", 0), i))
                for x_, src in ((0, 0), (1, 2)):
                    for k in range(KT):
                        last = t.matmul(misc[:, x_ * D:(x_ + 1) * D], nT[:, src + k, :], wv1_sb[:, k, :],
                                        start=(k == 0), stop=(k == KT - 1))
                last.then_inc(S["misc_full"], 1)

            def f0(b, i, k):
                take("misc", before("misc", ("F0", 0), i))
                pe.wait_ge(S["norm_f"], b + 1)
                for k in range(KT):
                    last = t.transpose(misc[:, k * P:(k + 1) * P], normed["f"][:, k * P:(k + 1) * P], ident[:])
                last.then_inc(S["misc_full"], 1)

            def f1(b, i, k):
                n = before("misc", ("F1", 0), i)
                take("misc", n)
                if isinstance(b, int) and b == 0:
                    pe.wait_ge(S["load_gu"], 16 * 4)
                for k in range(KT):
                    last = t.matmul(misc[:, 0:E0], n1T[:, k, :], gate0_sb[:, k, :], start=(k == 0), stop=(k == KT - 1))
                last.then_inc(S["misc_full"], 1)

            def g_(b, i, n):
                c, half_ = n // 2, n % 2
                s_ = c % 2
                if half_ == 0:
                    take(f"slot{s_}", before(f"slot{s_}", ("G", n), i))
                for k in range(KT):
                    rhs = gu_sb[:, k, 4 * c + 2 * half_:4 * c + 2 * half_ + 2, :].rearrange("p e f -> p (e f)")
                    last = t.matmul(slot[s_][:, 512 * half_:512 * half_ + 512], n1T[:, k, :], rhs,
                                    start=(k == 0), stop=(k == KT - 1))
                if half_ == 1:
                    last.then_inc(full(s_), 1)

            def t_(b, i, c):
                take("misc", before("misc", ("T", c), i))
                pe.wait_ge(S["inter_s"], 4 * b + c + 1)
                for e in range(4):
                    last = t.transpose(misc[:, e * P:(e + 1) * P], inter[:, c % 2, e, :], ident[:])
                last.then_inc(S["misc_full"], 1)

            def d_(b, i, c):
                if c == 0:
                    pe.wait_ge(S["o_a_s"], b + 1)
                pe.wait_ge(S["misc_free"], before("misc", ("T", c), i) + 1)
                for e in range(4):
                    last = t.matmul(pv0[:, 0:D], interT[:, c % 2, e, :], dn_sb[:, 4 * c + e, :],
                                    start=(c == 0 and e == 0), stop=(c == 3 and e == 3))
                last.then_inc(S["dn_chunk"], 1)

            def m_(b, i, g_):
                if g_ == 0:
                    pe.wait_ge(S["qk0_ld"], 64 * b + 64)
                    pe.wait_ge(S["mask0_ld"], 32 * b + 32)
                    if isinstance(b, int) and b == 0:
                        pe.wait_ge(S["ones_row"], 16 * 8)
                hg, tt = g_ % 4, g_ // 4
                take_slot2(i, before("slot2", ("M", g_), i))
                for u in range(4):
                    h = 4 * hg + u
                    last = t.matmul(slot[2][:, u * D:(u + 1) * D], QS0[0:ROWS_MAX, h, tt * P:(tt + 1) * P],
                                    KS0[0:ROWS_MAX, h, :], start=True, stop=True)
                last.then_inc(full(2), 1)

            def ma(b, i, k):
                take("misc", before("misc", ("MA", 0), i))
                apart(pe, S["slot2_free"], before("slot2", ("MA", 0), i))
                t.transpose(misc[0:32, 0:P], mx0[:].rearrange("p h s -> p (h s)"), ident[:]).then_inc(S["misc_full"], 1)

            def scores_with_mask(region, g_, which, lhs, rhs, rows):
                kind, r = g_ // 4, g_ % 4
                for hb in range(2):
                    if kind == 0:
                        for lo in range(2):
                            m = amask_p[:, lo, which, :].unsqueeze(1).broadcast_to([P, 4, P])
                            t.matmul(region[:, 512 * hb:512 * hb + 512], ident_r[:], m, start=(lo == 0), stop=(lo == 1))
                    for u in range(4):
                        h = 8 * r + 4 * hb + u
                        at = (4 * hb + u) * P
                        last = t.matmul(region[:, at:at + P], lhs[0:rows, h, :], rhs[0:rows, h, :], start=(kind == 1),
                                        stop=True, skip_group_check=True)
                return last

            def n_(b, i, g_):
                if g_ == 0:
                    pe.wait_ge(S["c_ld"], 144 * b + 144)
                    pe.wait_ge(S["amask_l"], b + 1)
                take_slot2(i, before("slot2", ("N", g_), i))
                scores_with_mask(slot[2], g_, 0, QS1, KS1 if g_ < 4 else AS1, ROWS_MAX).then_inc(full(2), 1)

            def nc_(b, i, k):
                take("misc", before("misc", ("NC", 0), i))
                apart(pe, S["slot2_free"], before("slot2", ("NC", 0), i))
                t.transpose(misc[0:64, 0:P], mx1[:].rearrange("p k h -> p (k h)"), ident[:]).then_inc(S["misc_full"], 1)

            def a3(b, i, step):
                def values(g_):
                    r, hh, st = g_ // 4, (g_ // 2) % 2, g_ % 2
                    take(f"slot{g_ % 2}", before(f"slot{g_ % 2}", ("A3", g_), i) + 1)
                    if g_ == 0:
                        after(pe, S["x2_ready"], b)
                    for j in range(4):
                        last = t.matmul(pv0[32 * j:32 * j + 32, r * D:(r + 1) * D],
                                        vst0[:, st, 4 * r + j, 32 * hh:32 * hh + 32],
                                        p[:, g_ % 2, j * D:(j + 1) * D],
                                        start=(hh == 0 and st == 0), stop=(hh == 1 and st == 1))
                    last.then_inc(S["pvdone_a"], 1)

                if step == 0:
                    pe.wait_ge(S["m0_ld"], 16 * b + 16)
                    pe.wait_ge(S["v0_ready"], 4 * b + 4)
                if step < 8:
                    s_ = step % 2
                    r, hh, st = step // 4, (step // 2) % 2, step % 2
                    take(f"slot{s_}", before(f"slot{s_}", ("A3", step), i))
                    for j in range(4):
                        h = 8 * r + 2 * j + hh
                        last = t.matmul(slot[s_][:, j * D:(j + 1) * D], KS0[:, h, st * P:(st + 1) * P], QS0[:, h, :],
                                        start=True, stop=True)
                    last.then_inc(full(s_), 1)
                if step >= 1:
                    values(step - 1)

            def a4(b, i, k):
                take("misc", before("misc", ("A4", 0), i))
                pe.wait_ge(S["o_a_s"], b + 1)
                for r in range(2):
                    last = t.matmul(misc[:, 0:D], sel[:, r, :], o_a[:, r, :], start=(r == 0), stop=(r == 1))
                last.then_inc(S["misc_full"], 1)

            def c3(b, i, step):
                def values(g_):
                    kind, r = g_ // 4, g_ % 4
                    take(f"slot{g_ % 2}", before(f"slot{g_ % 2}", ("C3", g_), i) + 1)
                    vst, pv = (vst_s, pvs) if kind == 0 else (vst_x, pvx)
                    for hh in range(2):
                        for j in range(4):
                            last = t.matmul(pv[32 * j:32 * j + 32, r * P:(r + 1) * P],
                                            vst[:, 4 * r + j, 32 * hh:32 * hh + 32],
                                            p[:, g_ % 2, (2 * j + hh) * P:(2 * j + hh + 1) * P],
                                            start=(hh == 0), stop=(hh == 1))
                    last.then_inc(S["pvdone_c"], 1)

                if step == 0:
                    pe.wait_ge(S["m1_ld"], 16 * b + 16)
                    pe.wait_ge(S["vs_ready"], 2 * b + 2)
                    pe.wait_ge(S["vx_ready"], b + 1)
                if step < 8:
                    s_ = step % 2
                    take(f"slot{s_}", before(f"slot{s_}", ("C3", step), i))
                    scores_with_mask(slot[s_], step, 1, KS1 if step < 4 else AS1, QS1, P).then_inc(full(s_), 1)
                if step == 1:
                    take_slot2(i, before("slot2", ("C3", 1), i))
                if step >= 1:
                    values(step - 1)

            def w_(b, i, k):
                take("misc", before("misc", ("W", 0), i))
                pe.wait_ge(S["o_c_s"], 3 * b + 3)
                for r in range(4):
                    last = t.matmul(misc[:, 0:D], o_c[:, r, :], wo1_sb[:, r, :], start=(r == 0), stop=(r == 3))
                last.then_inc(S["misc_full"], 1)

            def r0(b, i, k):
                take("misc", before("misc", ("R0", 0), i))
                pe.wait_ge(S["norm_e"], b + 1)
                for k in range(KT):
                    last = t.transpose(misc[:, k * P:(k + 1) * P], normed["e"][:, k * P:(k + 1) * P], ident[:])
                last.then_inc(S["misc_full"], 1)

            def r1(b, i, k):
                pe.wait_ge(S["misc_free"], before("misc", ("R0", 0), i) + 1)
                take("misc", before("misc", ("R1", 0), i))
                for k in range(KT):
                    last = t.matmul(misc[:, 0:E1], n3T[:, k, :], gate1w_sb[:, k, :], start=(k == 0), stop=(k == KT - 1))
                last.then_inc(S["misc_full"], 1)

            def r2(b, i, k):
                take("misc", before("misc", ("R2", 0), i))
                pe.wait_ge(S["onehot_s"], b + 1)
                after(pe, S["seen_s"], b)
                t.matmul(misc[:, 0:E1], tri[:], one_hot1[:], start=True, stop=False)
                t.matmul(misc[:, 0:E1], ones[:], seen[:], start=False, stop=True).then_inc(S["misc_full"], 1)

            iterations(pe, {"A1": a1, "VA": va, "C0": c0, "C1": c1, "VC": vc, "F0": f0, "F1": f1, "G": g_, "T": t_,
                            "D": d_, "M": m_, "MA": ma, "N": n_, "NC": nc_, "A3": a3, "A4": a4, "C3": c3, "W": w_,
                            "R0": r0, "R1": r1, "R2": r2})

            base = [all_uses(f"slot{k}", NB) for k in range(2)]
            for n, (s_, tiles, src) in enumerate(((0, 4, p[:, 0, :]), (1, 4, p[:, 1, :]),
                                                  (0, 2, rows_8.rearrange("p n h -> p (n h)")))):
                take(f"slot{s_}", base[s_] + n // 2)
                pe.wait_ge(S[f"disp_ld{n}"], 16)
                for k in range(tiles * KT):
                    last = t.transpose(slot[s_][:, k * P:(k + 1) * P], src[:, k * P:(k + 1) * P], ident[:])
                last.then_inc(full(s_), 1)

            def hidden(e):
                pe.wait_ge(S[f"load_wi{e % 4}"], 16 * (e // 4) + 16)
                for u in range(2):
                    take(f"slot{u}", base[u] + 2 - u + e)
                    for q in range(4):
                        at = 512 * (q // 2) + CAP * (q % 2)
                        for k in range(KT):
                            last = t.matmul(slot[u][:, at:at + CAP],
                                            wi_sb[e % 4][:, k, (4 * u + q) * P:(4 * u + q + 1) * P],
                                            dispT[:, k, e * CAP:(e + 1) * CAP], start=(k == 0), stop=(k == KT - 1))
                    last.then_inc(full(u), 1)

            def outputs(e):
                pe.wait_ge(S[f"load_wo{e % 4}"], 16 * (e // 4) + 16)
                for u in range(2):
                    take(f"slot{u}", base[u] + 2 - u + e + 1)
                after(pe, S["oT_ready"], e)
                for m in range(KT):
                    for k in range(IT1):
                        last = t.matmul(pv0[:, m * CAP:(m + 1) * CAP], wo_sb[e % 4][:, k, m * P:(m + 1) * P],
                                        hT[e % 2][:, k, :], start=(k == 0), stop=(k == IT1 - 1))
                last.then_inc(S["eo_full"], 1)

            def rows_back(e):
                pe.wait_ge(S["oT_ready"], e + 1)
                after(pe, S["eo_sb"], 2 * e)
                for c in range(2):
                    rows = P if c == 0 else CAP - P
                    for m in range(KT):
                        last = t.transpose(slot[2][0:rows, 512 * c + m * P:512 * c + (m + 1) * P],
                                           oT[e % 2][:, m, c * P:c * P + rows], ident[:])
                last.then_inc(S["eoT_full"], 1)

            for s_ in range(2):
                take(f"slot{s_}", base[s_] + 2 - s_)
            hidden(0)
            for e in range(E1):
                if e + 1 < E1:
                    hidden(e + 1)
                outputs(e)
                if e >= 1:
                    rows_back(e - 1)
            rows_back(E1 - 1)


def kernel(**inputs):
    import concourse.bacc as bacc
    from concourse.bass_utils import run_bass_kernel_spmd

    arr = {k: np.ascontiguousarray(v) for k, v in inputs.items()}
    nb, p, d = arr["x"].shape
    hd = 8

    def by_width(w):
        heads = w.shape[-1] // hd
        return np.ascontiguousarray(w.reshape(w.shape[:-1] + (heads, hd)).swapaxes(-1, -2).reshape(w.shape))

    wo_rows = np.zeros((4, 4, 32, d), np.float32)
    wo_rows[:, :, 0:16, :] = arr["L1_xattn_Wo"].reshape(4, 4, 16, d)

    inv = 1.0 / 10000.0 ** (np.arange(0, hd, 2, dtype=np.float32) / hd)
    ang = np.outer(np.arange(p, dtype=np.float32), inv)
    cos, sin = (np.repeat(f(ang).astype(np.float32).T, p // (hd // 2), axis=0) for f in (np.cos, np.sin))
    s = np.float32(1.0 / np.sqrt(hd))
    rope = np.stack([cos * s, cos * s, cos, cos, -sin * s, sin * s, -sin, sin], axis=1).astype(np.float32)

    mask = arr["mask_Bx1xSxS_fk0"][:, 0]
    feed = {
        "x": arr["x"], "ctx": arr["ctx_2048"], "mask01": arr["mask_Bx1x2048_fk1"],
        "mask01_cols": arr["mask_Bx1x2048_fk1"].reshape(nb, d // p, p).transpose(0, 2, 1),
        "addmask": mask, "addmaskT": mask.transpose(0, 2, 1),
        "wq0T": by_width(arr["L0_xattn_Wq"].T), "bq0": by_width(arr["L0_xattn_bq"]).reshape(-1, 1),
        "wk0T": by_width(arr["L0_xattn_Wk"].T), "bk0": by_width(arr["L0_xattn_bk"]).reshape(-1, 1),
        "wv0T": arr["L0_xattn_Wv"].T, "bv0": arr["L0_xattn_bv"].reshape(1, -1),
        "gate0T": arr["L0_ffn_gate_w"].T, "gate_up": arr["L0_ffn_gate_up_proj"], "down": arr["L0_ffn_down_proj"],
        "wq1": by_width(arr["L1_xattn_Wq"]), "wk1": by_width(arr["L1_xattn_Wk"]), "wv1": arr["L1_xattn_Wv"],
        "wo1": wo_rows.reshape(4, 128, d), "gate1": np.repeat(arr["L1_xattn_gate"].reshape(1, -1), hd, axis=1),
        "gate1wT": arr["L1_ffn_gate_weight"].T, "wi": arr["L1_ffn_wi"], "wo": arr["L1_ffn_wo"], "rope": rope,
    }
    nc = bacc.Bacc("TRN2", target_bir_lowering=False, num_devices=1)
    arrays, args = {}, []
    for name, a in feed.items():
        a = np.ascontiguousarray(a)
        arrays[f"in_{name}"] = a
        args.append(nc.dram_tensor(f"in_{name}", a.shape, mybir.dt.from_np(a.dtype), kind="ExternalInput").ap())
    args.append(nc.dram_tensor("out_x", (nb, p, d), mybir.dt.float32, kind="ExternalOutput").ap())
    two_layer_kernel(nc, *args)
    r = run_bass_kernel_spmd(nc, [arrays], core_ids=[0])
    return r.results[0]["out_x"]
```

```python
import concourse.bass as bass
from concourse import mybir
from contextlib import ExitStack

from functools import lru_cache

import numpy as np


LAG = {"LA": -1, "A1": -1, "VA": -1, "AR": -1, "LS": -1, "M": 0, "MA": 0, "A3": 0, "ON": 0, "A4": 0,
       "LF": 0, "F0": 0, "F1": 0, "RT": 1, "G": 1, "X": 1, "T": 1, "D": 1, "X2": 1,
       "LC": 1, "C0": 1, "C1": 1, "CR": 1, "CP": 1, "CQ": 1, "VC": 1, "AM": 1, "CS": 1,
       "N": 2, "NC": 2, "C3": 2, "OS": 2, "OX": 2, "XR": 2, "W": 3, "WN": 3, "R0": 3, "R1": 3, "R2": 3, "IN": -1, "INC": 1}
ORDER = [tuple(s.split(".")) for s in """
    IN M.0 INC G.0 RT G.1 M.1 G.2 W X.0 M.2 XR G.3 X.1 M.3 T.0 D.0 M.4 G.4 M.5 G.5 X.2 M.6 T.1 D.1 M.7 G.6 MA
    N.0 G.7 N.3 T.2 X.3 N.1 D.2 N.2 T.3 N.4 D.3 X2 N.5 N.6 N.7 A3.0 NC A3.1 LC A3.2 WN A3.3 LA A3.4 R0 A3.5 C0
    A3.6 A3.7 R1 A1 A3.8 C1 CR LS C3.0 ON C3.1 CP.0 CQ.0 C3.2 R2 C3.3 C3.4 C3.5 A4 LF AR CP.1 C3.6 C3.7 OS CQ.1
    C3.8 CS F0 VA AM OX F1 VC
""".split()]
ORDER = [(s[0], int(s[1])) if len(s) > 1 else (s[0], 0) for s in ORDER]


FIRST_LOOPED = 3


def maxima_slot(kind, k, i, batches):
    alone = isinstance(i, int) and (i == 0 if kind == "M" else i == batches + 1)
    return k % 3 if alone else 2


def uses(region, kind, k, i, batches):
    if region == "misc":
        return int(kind in ("W", "R0", "R1", "R2", "T", "MA", "NC", "C0", "A4", "F0", "F1", "VA", "VC"))
    at = int(region[-1])
    if kind in ("M", "N"):
        return int(maxima_slot(kind, k, i, batches) == at)
    if at == 2:
        return int(kind == "C1")
    return int(kind in ("A3", "C3") and k < 8 and k % 2 == at or kind == "G" and k % 4 == 2 * at
               or kind == "A1" and at == 0)


@lru_cache(maxsize=None)
def uses_before(region, step, at, batches):
    count = 0
    for i in range(-1, at + 1):
        for kind, k in ORDER:
            if i == at and (kind, k) == step:
                break
            if 0 <= i - LAG[kind] < batches:
                count += uses(region, kind, k, i, batches)
    return count


def all_uses(region, batches):
    return uses_before(region, None, batches + 4, batches)


def two_layer_kernel(nc, x, ctx_in, mask01, mask01_cols, addmask, addmaskT, wq0T, bq0, wk0T, bk0, wv0T, bv0, gate0T, gate_up, down,
                     wq1, wk1, wv1, wo1, gate1, gate1wT, wi, wo, rope, out):
    F32 = mybir.dt.float32
    F32R = mybir.dt.float32r
    BF16 = mybir.dt.bfloat16
    U32 = mybir.dt.uint32
    ALU = mybir.AluOpType
    ACT = mybir.ActivationFunctionType
    AX = mybir.AxisListType

    NB, P, D = x.shape
    H0, H1, HD = 16, 32, 8
    E0, I0 = down.shape[0], down.shape[1]
    E1, I1 = wo.shape[0], wo.shape[1]
    CAP = 160
    SLOTS = E1 * CAP
    NEG = 1000000.0
    EPS = 1e-5
    KT = D // P
    ROWS_MAX = 122
    IT1 = I1 // P

    dram = lambda name, shape, dt=F32: nc.dram_tensor(name, shape, dt, kind="Internal").ap()
    qk0_dram = dram("qk0_dram", [5, P, D])
    m0_dram = dram("m0_dram", [2, 32, P])
    mq_dram = dram("mq_dram", [NB, 6, D])
    mk_dram = dram("mk_dram", [NB, 6, D])
    c_dram = dram("c_dram", [13, 2, P, P], BF16)
    m1_dram = dram("m1_dram", [2, 3, H1, P], BF16)
    disp_dram = dram("disp_dram", [SLOTS + P, D])
    x3_dram = dram("x3_dram", [NB, P, D])
    eout_dram = dram("eout_dram", [SLOTS + P, D])

    with ExitStack() as stack:
        def sb(name, shape, dt=F32):
            return stack.enter_context(nc.sbuf_tensor(name, shape, dt))

        def pb(name, shape, dt=F32):
            return stack.enter_context(nc.psum_tensor(name, shape, dt))

        def sem(name):
            return stack.enter_context(nc.semaphore(name))

        ident = sb("ident", [P, P])
        ident_r = sb("ident_r", [P, P], F32R)
        tri = sb("tri", [P, P])
        ones = sb("ones", [P, P])
        minus_half = sb("minus_half", [P, 1])
        sel = sb("sel", [P, P])
        lower = sb("lower", [P, 1])
        upper = sb("upper", [P, 1])
        iota16 = sb("iota16", [P, 16])
        dump_row = sb("dump_row", [P, 1])
        ebase = sb("ebase", [P, E1])
        wq0_sb = sb("wq0_sb", [P, P])
        wk0_sb = sb("wk0_sb", [P, P])
        wv0_sb = sb("wv0_sb", [P, P])
        bq0_sb = sb("bq0_sb", [P, 1])
        bk0_sb = sb("bk0_sb", [P, 1])
        bv0_sb = sb("bv0_sb", [1, P])
        gate0_sb = sb("gate0_sb", [P, KT, E0])
        gu_sb = sb("gu_sb", [P, KT, E0, 2 * I0])
        dn_sb = sb("dn_sb", [P, E0, D])
        room_f = sb("room_f", [P, KT * I1 + IT1 * D])
        room_c = sb("room_c", [P, KT * I1 + IT1 * D])
        used = {"f": 0, "c": 0}

        def cut(which, shape):
            n = int(np.prod(shape))
            room = {"f": room_f, "c": room_c}[which]
            v = room[:, used[which]:used[which] + n]
            used[which] += n
            axes = "abcd"[:len(shape)]
            return v.rearrange(f"p ({' '.join(axes)}) -> p {' '.join(axes)}", **dict(zip(axes, shape)))

        wq1_sb = cut("c", (KT, D))
        wk1_sb = cut("c", (KT, D))
        wv1_sb = sb("wv1_sb", [P, KT, D])
        wo1_sb = sb("wo1_sb", [P, 4, D])
        gate1_sb = sb("gate1_sb", [P, D])
        gate1w_sb = sb("gate1w_sb", [P, KT, E1])
        rope_sb = cut("c", (8, P))
        gu_flat = gu_sb[:].rearrange("p k e f -> p (k e f)")
        dn_flat = dn_sb[:].rearrange("p e h -> p (e h)")
        dispT = dn_flat[:, 0:KT * SLOTS].rearrange("p (k c) -> p k c", k=KT)
        rows_8 = dn_flat[:, KT * SLOTS:KT * SLOTS + 2 * D].rearrange("p (n h) -> p n h", n=2)
        mask_rows = dn_flat[0:NB, 0:12 * D].rearrange("b (r t) -> b r t", r=12)
        mask_tmp = dn_flat[0:NB, 12 * D:15 * D].rearrange("b (r t) -> b r t", r=3)

        x_in = cut("c", (D,))
        x_res = sb("x_res", [P, D])
        ctx_a = cut("c", (D,))
        tm_b = sb("tm_b", [P, D])
        sm_col = sb("sm_col", [P, 2])
        tms_b = sb("tms_b", [P, D])
        qk0 = sb("qk0", [P, 2, D])
        qk0_p = sb("qk0_p", [P, 2, 2, D], F32R)
        QS0 = sb("QS0", [P, H0, D], F32R)
        KS0 = sb("KS0", [P, H0, D], F32R)
        tm_keep = sb("tm_keep", [P, D])
        half = KT * I1
        rings = [gu_flat[:, 0:2 * half], gu_flat[:, 2 * half:4 * half], room_f[:], room_c[:]]
        wi_sb = [r[:, 0:half].rearrange("p (k i) -> p k i", k=KT) for r in rings]
        wo_sb = [r[:, half:2 * half].rearrange("p (k h) -> p k h", k=IT1) for r in rings]
        vst0 = cut("f", (2, H0 // 2, 64))
        mx0 = sb("mx0", [P, H0, 2])
        m0_p = sb("m0_p", [32, 2, P], F32R)
        p = sb("p", [P, 2, 1024])
        den = sb("den", [P, 2 * D])
        sums_a, rec_a = den[:, 0:D], den[:, D:2 * D]
        swap_a, masked_a = sums_a, rec_a
        o_a = sb("o_a", [P, 2, D])
        x1 = sb("x1", [P, D])

        n1T = sb("n1T", [P, KT, P])
        route = sb("route", [P, 8, E0])
        rsmall = sb("rsmall", [P, 8])
        top8 = sb("top8", [P, 8])
        top8i = sb("top8i", [P, 8], U32)
        tanh_g = cut("f", (2, 4, P))
        inter = cut("f", (2, 4, P))
        interT = cut("f", (2, 4, P))
        x2 = sb("x2", [P, D])

        x2_res = sb("x2_res", [P, D])
        ctx_c = sb("ctx_c", [P, D])
        amask = sb("amask", [P, 2, P])
        amask_p = sb("amask_p", [P, 2, 2, P], F32R)
        nT = sb("nT", [P, 4, P])
        qka = cut("c", (6, P))
        qka_r = cut("c", (6, P))
        qka_p = sb("qka_p", [P, 3, 3, D], BF16)
        QS1 = sb("QS1", [P, H1, P], BF16)
        KS1 = sb("KS1", [P, H1, P], BF16)
        AS1 = sb("AS1", [P, H1, P], BF16)
        vst_s = sb("vst_s", [P, H1 // 2, 64])
        vst_x = sb("vst_x", [P, H1 // 2, 64])
        mx1 = sb("mx1", [P, 2, H1])
        m1_f = sb("m1_f", [64, P])
        m1_p = sb("m1_p", [64, 3, P], BF16)
        hT = [t[:].rearrange("p h t -> p (h t)").bitcast(F32)[:, 0:IT1 * CAP].rearrange("p (i c) -> p i c", i=IT1)
              for t in (QS1, KS1)]
        o_c = sb("o_c", [P, 4, P])
        den_c = sb("den_c", [P, 2 * D])

        oT = [o_a[:].rearrange("p r t -> p (r t)")[:, 0:KT * CAP].rearrange("p (m c) -> p m c", m=KT),
              o_c[:].rearrange("p r t -> p (r t)")[:, 0:KT * CAP].rearrange("p (m c) -> p m c", m=KT)]

        bn = {k: sb(f"bn_{k}", [P, 6]) for k in "afce"}
        mv = {k: sb(f"mv_{k}", [P, 2]) for k in "afce"}
        rstd = {k: sb(f"rstd_{k}", [P, 1]) for k in "afce"}
        normed = {k: sb(f"normed_{k}", [P, D]) for k in "afce"}

        x3 = AS1[:].rearrange("p h t -> p (h t)").bitcast(F32).rearrange("p (b h) -> p b h", b=NB)
        x3_now = sb("x3_now", [P, D])
        slot_now = sb("slot_now", [P, 1], U32)
        n3T = sb("n3T", [P, KT, P])
        top1 = sb("top1", [P, 8])
        top1i = sb("top1i", [P, 8], U32)
        lg1 = sb("lg1", [P, 6, E1])
        one_hot1 = sb("one_hot1", [P, E1])
        seen = sb("seen", [P, E1])
        small1 = sb("small1", [P, 8])
        wgt = sb("wgt", [P, NB])
        slot_u = sb("slot_u", [P, NB], U32)

        slot = [pb(f"slot{k}", [P, 1024]) for k in range(3)]
        misc = pb("misc", [P, 512])
        pv0 = pb("pv0", [P, 512])
        pvs, pvx = slot[2][:, 0:512], slot[2][:, 512:1024]

        names = """
        passed_SP passed_Pool passed_DVE passed_PE x3_ld gate1_s qka_a dn_chunk bn_a bn_f bn_c bn_e tms_s x3_copy load_w0 load_a load_c load_gu load_w1
        load_wi0 load_wi1 load_wi2 load_wi3 load_wo0 load_wo1 load_wo2 load_wo3 qka_p1 qka_low pva_read pvc_read os_s oT_ready eoT_full maskrow_st zeroed ones_row0 ones_row const_pool const_step const_dve mask_rows_done zeros_st slot0_full
        slot0_free slot1_full slot1_free slot2_full slot2_free misc_full misc_free bn_step rstd_ready_a rstd_ready_f rstd_ready_c
        rstd_ready_e var_a var_f var_c var_e norm_a xres_a qk0_ready qk0_h qk0_l v0_ready qk0_st qk0_ld
        mask0_ld m0_h m0_st m0_ld pvdone_a den_a_s rec_a_s o_a_s x1_ready norm_f route_s comb_ready tanh_s
        actg_s inter_s x2_ready norm_c x2res_s amask_h amask_l qka_step qka_p2 qka_done vs_ready vx_ready
        c_st c_ld m1_step m1_st m1_ld pvdone_c den_c_s o_c_s norm_e exp_e route1_s onehot_s seen_s
        slot_ready scat_s disp_ld0 disp_ld1 disp_ld2 eo_full eo_sb eo_st0 eo_st1 gath0 gath1 gath2 gath3 gath4 gath5 gath6 gath7 comb_s out_st
        """.split()
        S = {n: sem(n) for n in names}

        def full(k):
            return S[f"slot{k}_full"]

        def free(k):
            return S[f"slot{k}_free"]

        qk_flat = QS0[:].rearrange("p h t -> p (h t)")

        def flat(tile):
            return tile[:].rearrange("p h t -> p (h t)")

        def apart(eng, semaphore, value):
            after(eng, semaphore, value)
            if not isinstance(value, int):
                eng.sem_inc(S[f"passed_{eng.engine.name}"], 1)

        def head_pairs(first):
            dims = [list(d) for d in first.ap]
            return bass.AP(first.tensor, first.offset, dims[:-1] + [[40, 2]] + dims[-1:])

        def by_x(tile):
            return tile[:].rearrange("p (x m) t -> p x (m t)", x=3)

        block = stack.enter_context(nc.Block())

        LAST = NB + 2
        LOOP = (FIRST_LOOPED, NB - 1)

        def iterations(eng, steps):
            def one(i):
                for kind, k in ORDER:
                    lag = LAG[kind]
                    if kind in steps and (not isinstance(i, int) or 0 <= i - lag < NB):
                        steps[kind](i - lag if lag else i, i, k)
            for i in range(-1, LOOP[0]):
                one(i)
            with eng.Fori(*LOOP) as i:
                one(i)
            for i in range(LOOP[1], LAST + 1):
                one(i)

        def before(region, step, i):
            if isinstance(i, int):
                return uses_before(region, step, i, NB)
            first, second = (uses_before(region, step, FIRST_LOOPED + n, NB) for n in range(2))
            return i * (second - first) + (first - FIRST_LOOPED * (second - first))

        def attentions_done(lag, i):
            return min(max(i - lag, 0), NB) if isinstance(i, int) else i - lag

        def after(eng, semaphore, value):
            if not isinstance(value, int) or value > 0:
                eng.wait_ge(semaphore, value)

        @block.sync
        def _(sp):
            def wait(semaphore, value):
                if isinstance(value, int):
                    after(sp, semaphore, value)
                else:
                    apart(sp, semaphore, value)

            def load_a(b):
                sp.dma_start(x_in[:], x[b, :, :]).then_inc(S["load_a"], 16)
                sp.dma_start(ctx_a[:], ctx_in[b, :, :]).then_inc(S["load_a"], 16)
                sp.dma_start(tm_b[:], mask01[b, :, :].broadcast_to([P, D])).then_inc(S["load_a"], 16)
                sp.dma_start(sm_col[:], mask01_cols[b, :, :]).then_inc(S["load_a"], 16)

            def load_c(b):
                sp.dma_start(ctx_c[:], ctx_in[b, :, :]).then_inc(S["load_c"], 16)
                sp.dma_start(amask[:, 0, :], addmask[b, :, :]).then_inc(S["load_c"], 16)
                sp.dma_start(amask[:, 1, :], addmaskT[b, :, :]).then_inc(S["load_c"], 16)

            load_a(0)
            for dst, src in ((mask_tmp[:, 0, :], mask01.rearrange("b o t -> (b o) t")), (wq0_sb[:], wq0T),
                             (wk0_sb[:], wk0T), (wv0_sb[:], wv0T), (bq0_sb[:], bq0), (bk0_sb[:], bk0),
                             (bv0_sb[:], bv0)):
                sp.dma_start(dst, src).then_inc(S["load_w0"], 16)
            wait(S["const_pool"], 1)
            wait(S["zeroed"], 1)
            for n in range(4):
                sp.dma_start(flat(KS0)[126:128, 1024 * n:1024 * n + 1024].bitcast(F32), p[0:2, 0, :]).then_inc(S["ones_row0"], 16)

            def load_layer0_experts():
                sp.dma_start(gate0_sb[:], gate0T.rearrange("(k p) e -> p k e", p=P)).then_inc(S["load_gu"], 16)
                for k in range(KT):
                    sp.dma_start(gu_sb[:, k, :, :],
                                 gate_up[:, k * P:(k + 1) * P, :].rearrange("e p f -> p e f")).then_inc(S["load_gu"], 16)

            def rows_of_constants():
                wait(S["const_pool"], 3)
                ones_bf = p[:, 1, :].bitcast(BF16)
                for n in range(2):
                    sp.dma_start(flat(KS1)[122:125, 2048 * n:2048 * n + 2048], ones_bf[0:3, :]).then_inc(S["ones_row"], 16)
                    sp.dma_start(flat(AS1)[125:128, 2048 * n:2048 * n + 2048], ones_bf[0:3, :]).then_inc(S["ones_row"], 16)
                for n in range((SLOTS + P) // P):
                    sp.dma_start(disp_dram[n * P:(n + 1) * P, :], x1[:]).then_inc(S["zeros_st"], 16)
                sp.dma_start(eout_dram[SLOTS:SLOTS + P, :], x1[:]).then_inc(S["zeros_st"], 16)

            def load_layer1():
                sp.dma_start(dn_sb[:], down.rearrange("e i h -> i e h")).then_inc(S["load_gu"], 16)
                for dst, src in ((wq1_sb, wq1), (wk1_sb, wk1), (wv1_sb, wv1), (gate1w_sb, gate1wT)):
                    sp.dma_start(dst[:], src.rearrange("(k p) o -> p k o", p=P)).then_inc(S["load_w1"], 16)
                sp.dma_start(wo1_sb[:], wo1.rearrange("r p o -> p r o")).then_inc(S["load_w1"], 16)
                sp.dma_start(gate1_sb[:], gate1.broadcast_to([P, D])).then_inc(S["load_w1"], 16)
                sp.dma_start(rope_sb[:], rope).then_inc(S["load_w1"], 16)
                load_c(0)

            def store_mask_rows():
                wait(S["mask_rows_done"], 1)
                sp.dma_start(mq_dram.rearrange("b r t -> b (r t)"),
                             mask_rows[:, 0:6, :].rearrange("b r t -> b (r t)")).then_inc(S["maskrow_st"], 16)
                sp.dma_start(mk_dram.rearrange("b r t -> b (r t)"),
                             mask_rows[:, 6:12, :].rearrange("b r t -> b (r t)")).then_inc(S["maskrow_st"], 16)
                wait(S["maskrow_st"], 32)

            def load_wi(e):
                sp.dma_start(wi_sb[e % 4], wi[e, :, :].rearrange("(k p) i -> p k i", p=P)).then_inc(S[f"load_wi{e % 4}"], 16)

            def load_wo(e):
                sp.dma_start(wo_sb[e % 4], wo[e, :, :].rearrange("(k p) h -> p k h", p=P)).then_inc(S[f"load_wo{e % 4}"], 16)

            def next_a(b, i, k):
                if isinstance(b, int) and b == 0:
                    return
                wait(S["norm_a"], b)
                wait(S["xres_a"], b)
                wait(S["qk0_h"], b)
                wait(S["v0_ready"], 4 * b)
                load_a(b)
                if isinstance(b, int) and b == 1:
                    load_layer0_experts()
                    rows_of_constants()

            def next_c(b, i, k):
                if isinstance(b, int) and b == 0:
                    return
                wait(S["amask_l"], b)
                wait(S["qka_done"], b)
                load_c(b)

            def a1(b, i, k):
                wait(S["qk0_h"], b + 1)
                wait(S["qk0_l"], b + 1)
                flat4 = qk0_dram.rearrange("s p t -> p s t")
                src = qk0_p[:].rearrange("p l q t -> p q l t").bitcast(F32)
                wait(S["qk0_ld"], 64 * b)
                sp.dma_start(flat4[:, 0:2, :], src[:, 0, :, :]).then_inc(S["qk0_st"], 16)
                sp.dma_start(flat4[:, 2:4, :], src[:, 1, :, :]).then_inc(S["qk0_st"], 16)
                sp.dma_start(flat4[:, 4, :], src[:, 1, 0, :]).then_inc(S["qk0_st"], 16)

            def stacks_a(b, i, k):
                wait(S["pvdone_a"], 8 * b)
                wait(S["qk0_st"], 48 * b + 48)
                rows = qk0_dram.rearrange("s (d h) t -> (s d) (h t)", h=H0)
                sp.dma_start(flat(QS0)[0:16, :].bitcast(F32), rows[0:16, :]).then_inc(S["qk0_ld"], 16)
                sp.dma_start(flat(QS0)[16:32, :].bitcast(F32), rows[0:16, :]).then_inc(S["qk0_ld"], 16)
                sp.dma_start(flat(KS0)[0:16, :].bitcast(F32), rows[16:32, :]).then_inc(S["qk0_ld"], 16)
                sp.dma_start(flat(KS0)[16:32, :].bitcast(F32), rows[24:40, :]).then_inc(S["qk0_ld"], 16)
                if isinstance(b, int) and b == 0:
                    store_mask_rows()
                mq = mq_dram[b, :, :].unsqueeze(1).broadcast_to([6, H0, D])
                mk = mk_dram[b, :, :].unsqueeze(1).broadcast_to([6, H0, D])
                sp.dma_start(QS0[32:38, :, :].bitcast(F32), mq).then_inc(S["mask0_ld"], 16)
                sp.dma_start(KS0[32:38, :, :].bitcast(F32), mk).then_inc(S["mask0_ld"], 16)

            def experts_free(b, i, k):
                if isinstance(b, int) and b == NB - 1:
                    wait(S["x2_ready"], NB)
                    wait(S["pvdone_a"], 8 * NB)
                    for e in range(3):
                        load_wi(e)
                        load_wo(e)

            def stacks_c(b, i, k):
                wait(S["qka_done"], b + 1)
                wait(S["c_ld"], 144 * b)
                dst = c_dram.rearrange("s m p t -> p s m t")
                for x_, (at, n) in enumerate(((0, 3), (3, 3), (8, 3))):
                    sp.dma_start(dst[:, at:at + n, :, :].rearrange("p s m t -> p (s m) t"),
                                 qka_p[:, x_, :, :].rearrange("p s (m t) -> p (s m) t", m=2)).then_inc(S["c_st"], 16)
                for x_, at in ((1, 6), (2, 11)):
                    sp.dma_start(dst[:, at:at + 2, :, :].rearrange("p s m t -> p (s m) t"),
                                 qka_p[:, x_, 0:2, :].rearrange("p s (m t) -> p (s m) t", m=2)).then_inc(S["c_st"], 16)
                if isinstance(b, int) and b == NB - 1:
                    wait(S["xres_a"], NB)
                    wait(S["v0_ready"], 4 * NB)
                    load_wi(3)
                    load_wo(3)
                wait(S["pvdone_c"], 8 * b)
                wait(S["c_st"], 80 * b + 80)
                rows = c_dram.rearrange("s m (d h) t -> (s m d) (h t)", h=H1)
                for w in range(3):
                    sp.dma_start(flat(QS1)[24 * w:24 * w + 24, :], rows[0:24, :]).then_inc(S["c_ld"], 16)
                    sp.dma_start(flat(KS1)[24 * w:24 * w + 24, :], rows[24 + 8 * w:48 + 8 * w, :]).then_inc(S["c_ld"], 16)
                    sp.dma_start(flat(AS1)[24 * w:24 * w + 24, :], rows[64 + 8 * w:88 + 8 * w, :]).then_inc(S["c_ld"], 16)

            def ma(b, i, k):
                wait(S["misc_free"], before("misc", ("MA", 0), i) + 1)
                wait(S["m0_ld"], 16 * b)
                sp.dma_start(m0_dram.rearrange("s r t -> r s t"), m0_p[:].bitcast(F32)).then_inc(S["m0_st"], 16)
                wait(S["m0_st"], 16 * b + 16)
                sp.dma_start(flat(QS0)[126:128, :].bitcast(F32),
                             m0_dram.rearrange("s r t -> s (r t)")).then_inc(S["m0_ld"], 16)
                if isinstance(b, int) and b == 0:
                    load_layer1()

            def nc_(b, i, k):
                wait(S["m1_step"], 3 * b + 3)
                wait(S["m1_ld"], 16 * b)
                for kind in range(2):
                    sp.dma_start(m1_dram[kind, :, :, :].rearrange("s h t -> h s t"),
                                 m1_p[32 * kind:32 * kind + 32, :, :]).then_inc(S["m1_st"], 16)
                wait(S["m1_st"], 32 * b + 32)
                sp.dma_start(flat(QS1)[122:128, :], m1_dram.rearrange("k s h t -> (k s) (h t)")).then_inc(S["m1_ld"], 16)

            def w_(b, i, k):
                wait(S["misc_free"], before("misc", ("W", 0), i) + 1)
                sp.dma_start(x3_dram[b, :, :], x3_now[:]).then_inc(S["x3_copy"], 16)

            iterations(sp, {"IN": next_a, "INC": next_c, "A1": a1, "LS": stacks_a, "CS": stacks_c, "MA": ma, "NC": nc_,
                            "W": w_, "X2": experts_free})

            wait(S["scat_s"], 16 * NB)
            by_tile = disp_dram.rearrange("(n p) h -> p n h", p=P)
            sp.dma_start(p[:, 0, :].rearrange("p (n h) -> p n h", n=4), by_tile[:, 0:4, :]).then_inc(S["disp_ld0"], 16)
            sp.dma_start(p[:, 1, :].rearrange("p (n h) -> p n h", n=4), by_tile[:, 4:8, :]).then_inc(S["disp_ld1"], 16)
            sp.dma_start(rows_8, by_tile[:, 8:10, :]).then_inc(S["disp_ld2"], 16)
            wait(S["x3_copy"], 16 * NB)
            sp.dma_start(x3, x3_dram.rearrange("b p h -> p b h")).then_inc(S["x3_ld"], 16)

            def store_rows(e):
                for c in range(2):
                    rows = P if c == 0 else CAP - P
                    wait(S["eo_sb"], 2 * e + c + 1)
                    sp.dma_start(eout_dram[e * CAP + c * P:e * CAP + c * P + rows, :],
                                 p[0:rows, c, (e % 2) * D:(e % 2) * D + D]).then_inc(S[f"eo_st{e % 2}"], 16)

            for e in range(E1):
                if e + 4 < E1:
                    for u in range(2):
                        wait(full(u), all_uses(f"slot{u}", NB) + 2 - u + e + 1)
                    load_wi(e + 4)
                    wait(S["eo_full"], e + 1)
                    load_wo(e + 4)
                if e >= 1:
                    store_rows(e - 1)
            store_rows(E1 - 1)
            for b in range(NB):
                wait(S["comb_s"], b + 1)
                sp.dma_start(out[b, :, :], x3[:, b, :]).then_inc(S["out_st"], 16)
            wait(S["out_st"], 16 * NB)

        @block.gpsimd
        def _(pool):
            g = nc.gpsimd
            setup = [0]

            def step(ins):
                setup[0] += 1
                ins.then_inc(S["const_step"], 1)
                return setup[0]

            step(g.memset(minus_half[:], -0.5))
            step(g.memset(ident[:], 0.0))
            step(g.memset(p[:, 0, :], 1.0))
            n = step(g.memset(QS0[:].bitcast(F32), 0.0))
            pool.wait_ge(S["const_step"], n)
            g.affine_select(out=ident[:], in_=ident[:], compare_op=ALU.not_equal, fill=1.0, base=0,
                            pattern=[[-1, P]], channel_multiplier=1).then_inc(S["const_pool"], 1)

            def ones_in_stationaries():
                pool.wait_ge(S["zeroed"], 2)
                for t, first, second in ((vst0[:, 0, 0:4], 16, 56), (vst0[:, 1, 0:4], 16, 56), (vst_s[:], 16, 56),
                                         (vst0[:, 0, 4:8], 0, 40), (vst0[:, 1, 4:8], 0, 40), (vst_x[:], 0, 40)):
                    step(g.memset(t[:, :, first:first + 8], 1.0))
                    step(g.memset(t[:, :, second:second + 8], 1.0))
                step(g.memset(lower[:], 0.0))
                n = step(g.memset(upper[:], 1.0))
                for j in range(4):
                    pool.wait_ge(S["const_step"], n)
                    step(g.memset(lower[32 * j:32 * j + 16, :], 1.0))
                    n = step(g.memset(upper[32 * j:32 * j + 16, :], 0.0))
                pool.wait_ge(S["const_step"], n)
                g.memset(ones[:], 1.0).then_inc(S["const_pool"], 1)

            def later_constants():
                step(g.memset(p[:, 1, :].bitcast(BF16), 1.0))
                step(g.memset(tri[:], 1.0))
                step(g.memset(sel[:], 0.0))
                step(g.memset(x1[:], 0.0))
                step(g.memset(seen[:], 0.0))
                step(g.memset(KS1[:], 0.0))
                step(g.memset(AS1[:], 0.0))
                n = step(g.memset(QS1[:], 0.0))
                step(g.iota(iota16[:], pattern=[[1, 16]], base=0, channel_multiplier=0,
                            allow_small_or_imprecise_dtypes=True))
                step(g.iota(dump_row[:], pattern=[[0, 1]], base=SLOTS, channel_multiplier=1,
                            allow_small_or_imprecise_dtypes=True))
                step(g.iota(ebase[:], pattern=[[CAP, E1]], base=0, channel_multiplier=0,
                            allow_small_or_imprecise_dtypes=True))
                pool.wait_ge(S["const_step"], n)
                n = step(g.affine_select(out=tri[:], in_=tri[:], compare_op=ALU.is_ge, fill=0.0, base=0,
                                         pattern=[[1, P]], channel_multiplier=-1))
                for j in range(4):
                    for r in range(2):
                        pool.wait_ge(S["const_step"], n)
                        v = sel[32 * j:32 * j + 32, 64 * r + 16 * j:64 * r + 16 * j + 16]
                        n = step(g.affine_select(out=v, in_=v, compare_op=ALU.not_equal, fill=1.0, base=-16 * r,
                                                 pattern=[[-1, 16]], channel_multiplier=1))
                pool.wait_ge(S["const_step"], n)
                pool.sem_inc(S["const_pool"], 1)

            def rsqrt(k, b):
                pool.wait_ge(S[f"var_{k}"], b + 1)
                g.tensor_tensor(rstd[k][:], mv[k][:, 1:2], minus_half[:], ALU.pow).then_inc(S[f"rstd_ready_{k}"], 1)

            def la(b, i, k):
                rsqrt("a", b)
                after(pool, S["qk0_h"], b)
                apart(pool, S["load_a"], 64 * b + 64)
                g.tensor_scalar(tms_b[:], tm_b[:], float(HD) ** -0.5, 1.0, ALU.mult, ALU.mult).then_inc(S["tms_s"], 1)
                if isinstance(b, int) and b == 0:
                    ones_in_stationaries()

            def ar(b, i, k):
                after(pool, S["load_a"], 64 * b + 64)
                apart(pool, S["x1_ready"], b)
                g.tensor_copy(tm_keep[:], tm_b[:])
                g.tensor_copy(x_res[:], x_in[:]).then_inc(S["xres_a"], 1)
                if isinstance(b, int) and b == 0:
                    later_constants()

            def xr(b, i, k):
                if not (isinstance(b, int) and b == 0):
                    pool.wait_ge(S["misc_free"], before("misc", ("W", 0), i) + 1)
                apart(pool, S["x2_ready"], b + 1)
                g.tensor_copy(x2_res[:], x2[:]).then_inc(S["x2res_s"], 1)

            def lc(b, i, k):
                rsqrt("c", b)

            def lf(b, i, k):
                rsqrt("f", b)

            def cq(b, i, k):
                if k == 0:
                    pool.wait_ge(S["qka_p1"], b + 1)
                    g.tensor_tensor(by_x(qka), by_x(qka_r), qka_p[:, :, 0, :], ALU.subtract).then_inc(S["qka_low"], 1)
                else:
                    pool.wait_ge(S["qka_p2"], b + 1)
                    g.tensor_tensor(qka_p[:, :, 2, :], by_x(qka), qka_p[:, :, 1, :],
                                    ALU.subtract).then_inc(S["qka_done"], 1)

            def x_(b, i, c):
                pool.wait_ge(S["comb_ready"], b + 1)
                pool.wait_ge(free(c % 2), before(f"slot{c % 2}", ("G", 2 * c), i) + 1)
                share = route[:, 7, 4 * c:4 * c + 4].unsqueeze(2).broadcast_to([P, 4, P])
                g.tensor_tensor(inter[:, c % 2, :, :], inter[:, c % 2, :, :], share,
                                ALU.mult).then_inc(S["inter_s"], 1)

            def wn(b, i, k):
                rsqrt("e", b)

            def r2(b, i, k):
                pool.wait_ge(S["norm_e"], b + 1)
                apart(pool, S["slot_ready"], b + 1)
                if isinstance(b, int) and b == 0:
                    pool.wait_ge(S["zeros_st"], 16 * (SLOTS // P + 2))
                g.indirect_dma_start(disp_dram, bass.IndirectOffsetOnAxis(ap=slot_now[:], axis=0),
                                     normed["e"][:], None).then_inc(S["scat_s"], 16)

            iterations(pool, {"LA": la, "AR": ar, "XR": xr, "LC": lc, "LF": lf, "CQ": cq, "X": x_, "WN": wn, "R2": r2})

            for k in range(2):
                pool.wait_ge(S[f"eo_st{k}"], 32 * E1 // 2)
            for b in range(NB):
                g.indirect_dma_start(p[:, b // 4, (b % 4) * D:(b % 4 + 1) * D], None, eout_dram,
                                     bass.IndirectOffsetOnAxis(ap=slot_u[:, b:b + 1], axis=0)).then_inc(S[f"gath{b}"], 16)

        @block.vector
        def _(dve):
            v = nc.vector

            def norm_stats(k, src, b):
                v.bn_stats(bn[k][:], src).then_inc(S[f"bn_{k}"], 1)
                apart(dve, S[f"bn_{k}"], 2 * b + 1)
                v.bn_aggr(mv[k][:], bn[k][:]).then_inc(S[f"bn_{k}"], 1)
                dve.wait_ge(S[f"bn_{k}"], 2 * b + 2)
                v.tensor_scalar_add(mv[k][:, 1:2], mv[k][:, 1:2], EPS).then_inc(S[f"var_{k}"], 1)

            def norm_apply(k, src, b):
                dve.wait_ge(S[f"rstd_ready_{k}"], b + 1)
                v.tensor_scalar(normed[k][:], src, mv[k][:, 0:1], rstd[k][:], ALU.subtract,
                                ALU.mult).then_inc(S[f"norm_{k}"], 1)

            v.memset(KS0[:].bitcast(F32), 0.0).then_inc(S["zeroed"], 1)
            v.memset(vst0[:].rearrange("p s k c -> p (s k) c"), 0.0)
            v.memset(vst_s[:], 0.0)
            v.memset(vst_x[:], 0.0).then_inc(S["zeroed"], 1)

            def mask_products():
                dve.wait_ge(S["load_w0"], 16 * 7)
                steps = [0]

                def link(ins):
                    steps[0] += 1
                    ins.then_inc(S["const_dve"], 1)
                    dve.wait_ge(S["const_dve"], steps[0])

                mh = m0_p[0:NB, :, :].rearrange("p a t -> p (a t)")
                mask, w_, low = mask_tmp[:, 0, :], mask_tmp[:, 1, :], mask_tmp[:, 2, :]
                link(v.tensor_scalar(w_, mask, 1.0, NEG, ALU.subtract, ALU.mult))
                link(v.tensor_copy(mh, mask))
                link(v.tensor_tensor(low, mask, mh.bitcast(F32), ALU.subtract))
                for r in (0, 1):
                    v.tensor_copy(mask_rows[:, r, :], mh.bitcast(F32))
                    link(v.tensor_copy(mask_rows[:, 2 + r, :], low))
                link(v.tensor_copy(mh, w_))
                link(v.tensor_tensor(low, w_, mh.bitcast(F32), ALU.subtract))
                for r in (4, 6, 8):
                    v.tensor_copy(mask_rows[:, r, :], mh.bitcast(F32))
                    link(v.tensor_copy(mask_rows[:, r + 1, :], low))
                link(v.memset(mask_rows[:, 10, :], 1.0))
                v.memset(mask_rows[:, 11, :], 1.0).then_inc(S["mask_rows_done"], 1)
                dve.wait_ge(S["const_pool"], 1)
                v.tensor_copy(ident_r[:], ident[:]).then_inc(S["const_dve"], 1)

            def la(b, i, k):
                dve.wait_ge(S["load_a"], 64 * b + 64)
                norm_stats("a", x_in[:], b)
                norm_apply("a", x_in[:], b)

            def a1(b, i, k):
                n = before("slot0", ("A1", 0), i)
                dve.wait_ge(full(0), n + 1)
                dve.wait_ge(S["tms_s"], b + 1)
                v.scalar_tensor_tensor(qk0[:, 0, :], slot[0][:, 0:D], bq0_sb[:], tms_b[:], ALU.add,
                                       ALU.mult).then_inc(S["qk0_ready"], 1)
                v.scalar_tensor_tensor(qk0[:, 1, :], slot[0][:, D:2 * D], bk0_sb[:], tm_b[:], ALU.add,
                                       ALU.mult).then_inc(free(0), 1)
                after(dve, S["qk0_st"], 48 * b)
                dve.wait_ge(S["qk0_ready"], b + 1)
                dve.wait_ge(free(0), n + 1)
                v.tensor_copy(qk0_p[:, 0, :, :], qk0[:]).then_inc(S["qk0_h"], 1)
                dve.wait_ge(S["qk0_h"], b + 1)
                v.tensor_tensor(qk0_p[:, 1, :, :], qk0[:], qk0_p[:, 0, :, :].bitcast(F32),
                                ALU.subtract).then_inc(S["qk0_l"], 1)
                if isinstance(b, int) and b == 0:
                    mask_products()

            def am(b, i, k):
                dve.wait_ge(S["load_c"], 48 * b + 48)
                after(dve, S["pvdone_c"], 8 * b)
                v.tensor_copy(amask_p[:, 0, :, :], amask[:]).then_inc(S["amask_h"], 1)
                dve.wait_ge(S["amask_h"], b + 1)
                v.tensor_tensor(amask_p[:, 1, :, :], amask[:], amask_p[:, 0, :, :].bitcast(F32),
                                ALU.subtract).then_inc(S["amask_l"], 1)

            def lc(b, i, k):
                dve.wait_ge(S["x2_ready"], b + 1)
                norm_stats("c", x2[:], b)
                norm_apply("c", x2[:], b)

            def cr(b, i, k):
                n = before("slot2", ("C1", 0), i)
                dve.wait_ge(full(2), n + 1)
                ps = slot[2][:, 0:512].rearrange("p (x m t) -> p x m t", x=2, m=2)
                cos = rope_sb[:, 0:4, :].rearrange("p (x m) t -> p x m t", x=2)
                sin = rope_sb[:, 4:8, :].rearrange("p (x m) t -> p x m t", x=2)
                r = qka_r[:, 0:4, :].rearrange("p (x m) t -> p x m t", x=2)
                s_ = qka[:, 0:4, :].rearrange("p (x m) t -> p x m t", x=2)
                after(dve, S["qka_done"], b)
                v.tensor_tensor(r, ps, cos, ALU.mult).then_inc(S["qka_step"], 1)
                v.tensor_tensor(s_[:, :, 0, :], ps[:, :, 1, :], sin[:, :, 0, :], ALU.mult).then_inc(S["qka_step"], 1)
                v.tensor_tensor(s_[:, :, 1, :], ps[:, :, 0, :], sin[:, :, 1, :], ALU.mult).then_inc(S["qka_step"], 1)
                dve.wait_ge(S["qka_step"], 3 * b + 3)
                dve.wait_ge(S["qka_a"], b + 1)
                v.tensor_tensor(qka_r[:, 0:4, :], qka_r[:, 0:4, :], qka[:, 0:4, :], ALU.add).then_inc(free(2), 1)

            def vc(b, i, k):
                dve.wait_ge(S["misc_full"], before("misc", ("VC", 0), i) + 1)
                after(dve, S["pvdone_c"], 8 * b)
                dve.wait_ge(S["vs_ready"], 2 * b + 2)
                for hh in range(2):
                    src = misc[:, D:2 * D].rearrange("p (k x) -> p k x", x=16)[:, :, 8 * hh:8 * hh + 8]
                    gt = gate1_sb[:].rearrange("p (k x) -> p k x", x=16)[:, :, 8 * hh:8 * hh + 8]
                    last = v.tensor_tensor(vst_x[:, :, 16 + 40 * hh:24 + 40 * hh], src, gt, ALU.mult)
                    last.then_inc(S["vx_ready" if hh == 0 else "misc_free"], 1)

            ROUTE0 = 12

            def lf(b, i, k):
                dve.wait_ge(S["x1_ready"], b + 1)
                norm_stats("f", x1[:], b)
                norm_apply("f", x1[:], b)

            def rt(b, i, k):
                count = [0]

                def rs(ins, wait=True):
                    count[0] += 1
                    ins.then_inc(S["route_s"], 1)
                    if wait:
                        apart(dve, S["route_s"], ROUTE0 * b + count[0])

                dve.wait_ge(S["misc_free"], before("misc", ("F1", 0), i - LAG["RT"] + LAG["F1"]) + 1)
                after(dve, S["inter_s"], 4 * b)
                rs(v.tensor_scalar_add(route[:, 1, :], route[:, 0, :], 1.0))
                rs(v.reciprocal(route[:, 2, :], route[:, 1, :]))
                rs(v.reduce_sum(rsmall[:, 0:1], route[:, 2, :], AX.X))
                rs(v.reciprocal(rsmall[:, 1:2], rsmall[:, 0:1]))
                rs(v.tensor_scalar(route[:, 3, :], route[:, 2, :], rsmall[:, 1:2], None, ALU.mult))
                rs(v.max(top8[:], route[:, 3, :]))
                rs(v.max_index(top8i[:], top8[:], route[:, 3, :]))
                rs(v.tensor_copy(rsmall[:, 2:4], top8i[:, 0:2]))
                rs(v.tensor_tensor(rsmall[:, 4:5], top8[:, 0:1], top8[:, 1:2], ALU.add))
                rs(v.reciprocal(rsmall[:, 5:6], rsmall[:, 4:5]))
                rs(v.tensor_scalar(rsmall[:, 6:8], top8[:, 0:2], rsmall[:, 5:6], 0.5, ALU.mult, ALU.mult))
                v.tensor_scalar(route[:, 4, :], iota16[:], rsmall[:, 2:3], rsmall[:, 6:7], ALU.is_equal, ALU.mult)
                rs(v.tensor_scalar(route[:, 5, :], iota16[:], rsmall[:, 3:4], rsmall[:, 7:8], ALU.is_equal, ALU.mult))
                v.tensor_tensor(route[:, 7, :], route[:, 4, :], route[:, 5, :], ALU.add).then_inc(S["comb_ready"], 1)
                assert count[0] == ROUTE0

            def x_(b, i, c):
                k = c % 2
                ps = slot[k][:].rearrange("p (e g i) -> p e g i", e=4, g=2)
                dve.wait_ge(S["tanh_s"], 4 * b + c + 1)
                v.scalar_tensor_tensor(tanh_g[:, k, :, :], tanh_g[:, k, :, :], 1.0, ps[:, :, 0, :], ALU.add,
                                       ALU.mult).then_inc(S["actg_s"], 1)
                dve.wait_ge(S["actg_s"], 4 * b + c + 1)
                if c >= 2:
                    dve.wait_ge(S["misc_free"], before("misc", ("T", c - 2), i) + 1)
                v.tensor_tensor(inter[:, k, :, :], tanh_g[:, k, :, :], ps[:, :, 1, :],
                                ALU.mult).then_inc(free(k), 1)

            def x2_(b, i, k):
                dve.wait_ge(S["dn_chunk"], 4 * b + 4)
                after(dve, S["x2res_s"], b)
                v.tensor_tensor(x2[:], x1[:], pv0[:, 0:D], ALU.add).then_inc(S["x2_ready"], 1)

            def m_(b, i, g_):
                s_ = maxima_slot("M", g_, i, NB)
                dve.wait_ge(full(s_), before(f"slot{s_}", ("M", g_), i) + 1)
                hg, tt = g_ % 4, g_ // 4
                v.reduce_max(mx0[:, 4 * hg:4 * hg + 4, tt], slot[s_][:].rearrange("p (h s) -> p h s", h=4),
                             AX.X).then_inc(free(s_), 1)

            def ma(b, i, k):
                n = before("misc", ("MA", 0), i)
                dve.wait_ge(S["misc_full"], n + 1)
                after(dve, S["m0_st"], 16 * b)
                v.tensor_scalar(m0_p[:, 0, :], misc[0:32, 0:P], -1.0, None, ALU.mult).then_inc(S["m0_h"], 1)
                dve.wait_ge(S["m0_h"], b + 1)
                v.scalar_tensor_tensor(m0_p[:, 1, :], misc[0:32, 0:P], -1.0, m0_p[:, 0, :].bitcast(F32), ALU.mult,
                                       ALU.subtract).then_inc(S["misc_free"], 1)

            def n_(b, i, g_):
                s_ = maxima_slot("N", g_, i, NB)
                dve.wait_ge(full(s_), before(f"slot{s_}", ("N", g_), i) + 1)
                kind, r = g_ // 4, g_ % 4
                v.reduce_max(mx1[:, kind, 8 * r:8 * r + 8], slot[s_][:].rearrange("p (h s) -> p h s", h=8),
                             AX.X).then_inc(free(s_), 1)

            def nc_(b, i, k):
                n = before("misc", ("NC", 0), i)
                dve.wait_ge(S["misc_full"], n + 1)
                after(dve, S["m1_st"], 32 * b)
                v.tensor_scalar(m1_p[:, 0, :], misc[0:64, 0:P], -1.0, None, ALU.mult).then_inc(S["m1_step"], 1)
                dve.wait_ge(S["m1_step"], 3 * b + 1)
                v.scalar_tensor_tensor(m1_f[:], misc[0:64, 0:P], -1.0, m1_p[:, 0, :], ALU.mult,
                                       ALU.subtract).then_inc(S["misc_free"], 1)
                dve.wait_ge(S["misc_free"], n + 1)
                v.tensor_copy(m1_p[:, 1, :], m1_f[:]).then_inc(S["m1_step"], 1)
                dve.wait_ge(S["m1_step"], 3 * b + 2)
                v.tensor_tensor(m1_p[:, 2, :], m1_f[:], m1_p[:, 1, :], ALU.subtract).then_inc(S["m1_step"], 1)

            other_half = [(j + 16) % 32 for j in range(32)]

            def on(b, i, k):
                if isinstance(b, int) and b == 0:
                    dve.wait_ge(S["const_pool"], 3)
                dve.wait_ge(S["pvdone_a"], 8 * b + 8)
                v.tensor_scalar(sums_a, pv0[:, 0:D], upper[:], None, ALU.mult).then_inc(S["den_a_s"], 1)
                v.tensor_scalar(o_a[:, 0, :], pv0[:, 0:D], lower[:], None, ALU.mult).then_inc(S["den_a_s"], 1)
                dve.wait_ge(S["den_a_s"], 3 * b + 2)
                v.scalar_tensor_tensor(sums_a, pv0[:, D:2 * D], lower[:], sums_a, ALU.mult,
                                       ALU.add).then_inc(S["den_a_s"], 1)
                v.scalar_tensor_tensor(o_a[:, 0, :], pv0[:, D:2 * D], upper[:], o_a[:, 0, :], ALU.mult,
                                       ALU.add).then_inc(S["pva_read"], 1)
                dve.wait_ge(S["den_a_s"], 3 * b + 3)
                v.reciprocal(rec_a, sums_a).then_inc(S["rec_a_s"], 1)
                apart(dve, S["rec_a_s"], 2 * b + 1)
                v.stream_shuffle(swap_a, rec_a, other_half).then_inc(S["rec_a_s"], 1)
                dve.wait_ge(S["pva_read"], b + 1)
                dve.wait_ge(S["rec_a_s"], 2 * b + 2)
                v.tensor_tensor(o_a[:, 1, :], o_a[:, 0, :], swap_a, ALU.mult).then_inc(S["o_a_s"], 1)

            def a4(b, i, k):
                n = before("misc", ("A4", 0), i)
                dve.wait_ge(S["xres_a"], b + 1)
                dve.wait_ge(S["misc_full"], n + 1)
                v.tensor_tensor(masked_a, misc[:, 0:D], tm_keep[:],
                                ALU.mult).then_inc(S["misc_free"], 1)
                dve.wait_ge(S["misc_free"], n + 1)
                if isinstance(b, int) and b == 0:
                    dve.wait_ge(S["zeros_st"], 16 * (SLOTS // P + 2))
                v.tensor_tensor(x1[:], masked_a, x_res[:], ALU.add).then_inc(S["x1_ready"], 1)

            ROUTE1 = 14

            def ox(b, i, k):
                dve.wait_ge(S["os_s"], 2 * b + 2)
                dve.wait_ge(S["pvdone_c"], 8 * b + 8)
                o = o_c[:].rearrange("p r t -> p (r t)")
                v.scalar_tensor_tensor(den_c[:], pvx, lower[:], den_c[:], ALU.mult, ALU.add).then_inc(S["den_c_s"], 1)
                v.scalar_tensor_tensor(o, pvx, upper[:], o, ALU.mult, ALU.add).then_inc(S["pvc_read"], 1)
                dve.wait_ge(S["den_c_s"], 3 * b + 1)
                v.reciprocal(den[:], den_c[:]).then_inc(S["den_c_s"], 1)
                apart(dve, S["den_c_s"], 3 * b + 2)
                v.stream_shuffle(den_c[:], den[:], other_half).then_inc(S["den_c_s"], 1)
                dve.wait_ge(S["pvc_read"], b + 1)
                dve.wait_ge(S["den_c_s"], 3 * b + 3)
                v.tensor_tensor(o, o, den_c[:], ALU.mult).then_inc(S["o_c_s"], 1)

            def w_(b, i, k):
                n = before("misc", ("W", 0), i)
                dve.wait_ge(S["misc_full"], n + 1)
                dve.wait_ge(S["x2res_s"], b + 1)
                after(dve, S["x3_copy"], 16 * b)
                v.tensor_tensor(x3_now[:], misc[:, 0:D], x2_res[:],
                                ALU.add).then_inc(S["misc_free"], 1)

            def wn(b, i, k):
                dve.wait_ge(S["misc_free"], before("misc", ("W", 0), i) + 1)
                norm_stats("e", x3_now[:], b)
                after(dve, S["scat_s"], 16 * b)
                norm_apply("e", x3_now[:], b)

            def steps_of_route1(b, done):
                count = [done]

                def rs(ins, wait=True):
                    count[0] += 1
                    ins.then_inc(S["route1_s"], 1)
                    if wait:
                        apart(dve, S["route1_s"], ROUTE1 * b + count[0])
                return count, rs

            def r1(b, i, k):
                count, rs = steps_of_route1(b, 0)

                n = before("misc", ("R1", 0), i)
                dve.wait_ge(S["misc_full"], n + 1)
                after(dve, S["exp_e"], b)
                v.tensor_copy(lg1[:, 0, :], misc[:, 0:E1]).then_inc(S["misc_free"], 1)
                apart(dve, S["misc_free"], n + 1)
                rs(v.max(top1[:], lg1[:, 0, :]))
                rs(v.tensor_scalar(small1[:, 0:1], top1[:, 0:1], -1.0, None, ALU.mult), wait=False)
                rs(v.max_index(top1i[:], top1[:], lg1[:, 0, :]))
                rs(v.tensor_copy(small1[:, 1:2], top1i[:, 0:1]))
                v.tensor_scalar(one_hot1[:], iota16[:, 0:E1], small1[:, 1:2], None,
                                ALU.is_equal).then_inc(S["onehot_s"], 1)
                assert count[0] == 4

            def r2(b, i, k):
                count, rs = steps_of_route1(b, 4)
                n = before("misc", ("R2", 0), i)
                dve.wait_ge(S["exp_e"], b + 1)
                rs(v.reciprocal(small1[:, 3:4], small1[:, 2:3]), wait=False)
                dve.wait_ge(S["onehot_s"], b + 1)
                dve.wait_ge(S["misc_full"], n + 1)
                rs(v.scalar_tensor_tensor(lg1[:, 1, :], misc[:, 0:E1], -1.0, one_hot1[:], ALU.add, ALU.mult), wait=False)
                v.scalar_tensor_tensor(lg1[:, 2, :], misc[:, 0:E1], -1.0, ebase[:], ALU.add,
                                       ALU.add).then_inc(S["misc_free"], 1)
                v.tensor_tensor(seen[:], seen[:], one_hot1[:], ALU.add).then_inc(S["seen_s"], 1)
                dve.wait_ge(S["misc_free"], n + 1)
                rs(v.tensor_tensor(lg1[:, 3, :], lg1[:, 2, :], one_hot1[:], ALU.mult), wait=False)
                dve.wait_ge(S["route1_s"], ROUTE1 * b + 6)
                rs(v.reduce_sum(small1[:, 4:5], lg1[:, 1, :], AX.X))
                rs(v.reduce_sum(small1[:, 5:6], lg1[:, 3, :], AX.X), wait=False)
                rs(v.tensor_scalar(small1[:, 6:7], small1[:, 4:5], float(CAP), None, ALU.is_lt))
                rs(v.tensor_tensor(small1[:, 7:8], small1[:, 5:6], dump_row[:], ALU.subtract))
                rs(v.tensor_scalar(lg1[:, 4, 0:1], small1[:, 7:8], small1[:, 6:7], dump_row[:], ALU.mult, ALU.add))
                v.tensor_copy(slot_now[:], lg1[:, 4, 0:1]).then_inc(S["slot_ready"], 1)
                rs(v.tensor_copy(slot_u[:, bass.ds(b, 1)], lg1[:, 4, 0:1]), wait=False)
                rs(v.tensor_tensor(wgt[:, bass.ds(b, 1)], small1[:, 3:4], small1[:, 6:7], ALU.mult), wait=False)
                while count[0] < ROUTE1:
                    rs(v.tensor_copy(lg1[:, 5, 0:1], lg1[:, 4, 0:1]))
                assert count[0] == ROUTE1, count

            iterations(dve, {"LA": la, "A1": a1, "AM": am, "LC": lc, "CR": cr, "VC": vc, "LF": lf, "RT": rt, "X": x_,
                             "X2": x2_, "M": m_, "MA": ma, "N": n_, "NC": nc_, "ON": on, "A4": a4, "OX": ox,
                             "W": w_, "WN": wn, "R1": r1, "R2": r2})

            dve.wait_ge(full(1), all_uses("slot1", NB) + 1)
            v.tensor_copy(dispT[:, :, 4 * P:8 * P].rearrange("p k (n t) -> p n k t", n=4),
                          slot[1][:].rearrange("p (n k t) -> p n k t", n=4, k=KT)).then_inc(free(1), 1)

            def rows_out(e):
                dve.wait_ge(S["eoT_full"], e + 1)
                if e >= 2:
                    dve.wait_ge(S[f"eo_st{e % 2}"], 32 * (e // 2))
                for c in range(2):
                    rows = P if c == 0 else CAP - P
                    v.tensor_copy(p[0:rows, c, (e % 2) * D:(e % 2) * D + D],
                                  slot[2][0:rows, c * 512:c * 512 + D]).then_inc(S["eo_sb"], 1)

            for e in range(E1):
                dve.wait_ge(S["eo_full"], e + 1)
                if e >= 2:
                    dve.wait_ge(S["eoT_full"], e - 1)
                v.tensor_copy(oT[e % 2], pv0[:, 0:KT * CAP].rearrange("p (m c) -> p m c", m=KT)).then_inc(S["oT_ready"], 1)
                if e >= 1:
                    rows_out(e - 1)
            rows_out(E1 - 1)
            for b in range(NB):
                dve.wait_ge(S[f"gath{b}"], 16)
                dve.wait_ge(S["x3_ld"], 16)
                v.scalar_tensor_tensor(x3[:, b, :], p[:, b // 4, (b % 4) * D:(b % 4 + 1) * D], wgt[:, b:b + 1], x3[:, b, :],
                                       ALU.mult, ALU.add).then_inc(S["comb_s"], 1)

        @block.scalar
        def _(act):
            a = nc.scalar
            def copy_misc(dst, cols, use):
                act.wait_ge(S["misc_full"], use + 1)
                a.activation(dst, misc[:, 0:cols], ACT.Copy).then_inc(S["misc_free"], 1)

            def va(b, i, k):
                n = before("misc", ("VA", 0), i)
                after(act, S["pvdone_a"], 8 * b)
                if isinstance(b, int) and b == 0:
                    act.wait_ge(S["const_pool"], 2)
                act.wait_ge(S["load_a"], 64 * b + 64)
                act.wait_ge(S["misc_full"], n + 1)
                for st in range(2):
                    for r in range(2):
                        src = misc[:, st * P + 64 * r:st * P + 64 * r + 64].rearrange("p (k h x) -> p k h x", h=2, x=8)
                        ins = a.activation(head_pairs(vst0[:, st, 4 * r:4 * r + 4, 16 * r:16 * r + 8]), src, ACT.Copy,
                                           scale=sm_col[:, st:st + 1])
                        ins.then_inc(S["v0_ready"], 1)
                act.wait_ge(S["v0_ready"], 4 * b + 4)
                act.sem_inc(S["misc_free"], 1)

            def c0(b, i, k):
                copy_misc(nT[:].rearrange("p k t -> p (k t)"), 512, before("misc", ("C0", 0), i))

            def c1(b, i, k):
                act.wait_ge(full(2), before("slot2", ("C1", 0), i) + 1)
                after(act, S["qka_done"], b)
                a.activation(qka_r[:, 4:6, :].rearrange("p k t -> p (k t)"), slot[2][:, 512:768],
                             ACT.Copy).then_inc(S["qka_a"], 1)

            def cp(b, i, k):
                if k == 0:
                    act.wait_ge(S["slot2_free"], before("slot2", ("C1", 0), i) + 1)
                    after(act, S["c_st"], 80 * b)
                    a.activation(qka_p[:, :, 0, :], by_x(qka_r), ACT.Copy).then_inc(S["qka_p1"], 1)
                else:
                    act.wait_ge(S["qka_low"], b + 1)
                    a.activation(qka_p[:, :, 1, :], by_x(qka), ACT.Copy).then_inc(S["qka_p2"], 1)

            def os_(b, i, k):
                after(act, S["bn_e"], 2 * b)
                after(act, S["o_c_s"], b)
                act.wait_ge(S["pvdone_c"], 8 * b + 4)
                a.activation(den_c[:], pvs, ACT.Copy, scale=upper[:]).then_inc(S["os_s"], 1)
                a.activation(o_c[:].rearrange("p r t -> p (r t)"), pvs, ACT.Copy, scale=lower[:]).then_inc(S["os_s"], 1)

            def vc(b, i, k):
                if isinstance(b, int) and b == 0:
                    act.wait_ge(S["load_w1"], 16 * 7)
                    a.activation(gate1_sb[:], gate1_sb[:], ACT.Tanh).then_inc(S["gate1_s"], 1)
                act.wait_ge(S["misc_full"], before("misc", ("VC", 0), i) + 1)
                after(act, S["pvdone_c"], 8 * b)
                if isinstance(b, int) and b == 0:
                    act.wait_ge(S["const_pool"], 2)
                    act.wait_ge(S["gate1_s"], 1)
                for hh in range(2):
                    src = misc[:, 0:D].rearrange("p (k x) -> p k x", x=16)[:, :, 8 * hh:8 * hh + 8]
                    a.activation(vst_s[:, :, 40 * hh:40 * hh + 8], src, ACT.Copy).then_inc(S["vs_ready"], 1)

            def f0(b, i, k):
                after(act, S["dn_chunk"], 4 * b)
                copy_misc(n1T[:].rearrange("p k t -> p (k t)"), KT * P, before("misc", ("F0", 0), i))

            def f1(b, i, k):
                after(act, S["comb_ready"], b)
                act.wait_ge(S["misc_full"], before("misc", ("F1", 0), i) + 1)
                a.activation(route[:, 0, :], misc[:, 0:E0], ACT.Exp,
                             scale=-1.0).then_inc(S["misc_free"], 1)

            def x_(b, i, c):
                k = c % 2
                act.wait_ge(full(k), before(f"slot{k}", ("G", 2 * c), i) + 1)
                after(act, S["actg_s"], 4 * b + c - 1)
                ps = slot[k][:].rearrange("p (e g i) -> p e g i", e=4, g=2)
                a.activation(tanh_g[:, k, :, :], ps[:, :, 0, :], ACT.Tanh, scale=0.5).then_inc(S["tanh_s"], 1)

            def t_(b, i, c):
                after(act, S["dn_chunk"], 4 * b + c - 1)
                copy_misc(interT[:, c % 2, :, :].rearrange("p e t -> p (e t)"), 512, before("misc", ("T", c), i))

            def a3(b, i, g_):
                if g_ == 8:
                    return
                k = g_ % 2
                act.wait_ge(full(k), before(f"slot{k}", ("A3", g_), i) + 1)
                ran_c = attentions_done(2, i)
                if g_ >= 2 or (isinstance(ran_c, int) and ran_c == 0):
                    after(act, S["pvdone_a"], 8 * b + g_ - 1)
                else:
                    act.wait_ge(S["pvdone_c"], 8 * ran_c + g_ - 1)
                if isinstance(b, int) and b == 0 and g_ < 2:
                    act.wait_ge(S["ones_row0" if g_ == 0 else "ones_row"], 16 * 4)
                a.activation(p[:, k, :], slot[k][:], ACT.Exp).then_inc(free(k), 1)

            def c3(b, i, g_):
                if g_ == 8:
                    return
                k = g_ % 2
                act.wait_ge(full(k), before(f"slot{k}", ("C3", g_), i) + 1)
                if g_ >= 2 or (isinstance(i, int) and i >= NB):
                    after(act, S["pvdone_c"], 8 * b + g_ - 1)
                else:
                    act.wait_ge(S["pvdone_a"], 8 * i + g_ + 7)
                a.activation(p[:, k, :], slot[k][:], ACT.Exp).then_inc(free(k), 1)

            def r0(b, i, k):
                after(act, S["route1_s"], 14 * b)
                copy_misc(n3T[:].rearrange("p k t -> p (k t)"), KT * P, before("misc", ("R0", 0), i))

            def r1(b, i, k):
                act.wait_ge(S["route1_s"], 14 * b + 2)
                a.activation(lg1[:, 5, :], lg1[:, 0, :], ACT.Exp, bias=small1[:, 0:1],
                             accum_out=small1[:, 2:3]).then_inc(S["exp_e"], 1)

            iterations(act, {"CP": cp, "OS": os_, "VA": va, "C0": c0, "C1": c1, "VC": vc, "F0": f0, "F1": f1, "X": x_, "T": t_, "A3": a3,
                             "C3": c3, "R0": r0, "R1": r1})

            base = [all_uses(f"slot{k}", NB) for k in range(2)]
            for n, (at, tiles) in enumerate(((0, 4), (8, 2))):
                act.wait_ge(full(0), base[0] + n + 1)
                if n == 0:
                    act.wait_ge(S["dn_chunk"], 4 * NB)
                a.activation(dispT[:, :, at * P:(at + tiles) * P].rearrange("p k (n t) -> p n k t", n=tiles),
                             slot[0][:, 0:tiles * D].rearrange("p (n k t) -> p n k t", n=tiles, k=KT),
                             ACT.Copy).then_inc(free(0), 1)
            for e in range(E1):
                for u in range(2):
                    act.wait_ge(full(u), base[u] + 2 - u + e + 1)
                    if e >= 2:
                        act.wait_ge(S["eo_full"], e - 1)
                    src = slot[u][:].rearrange("p (k n) -> p k n", k=2)[:, :, 0:2 * CAP]
                    dst = hT[e % 2][:, 4 * u:4 * u + 4, :].rearrange("p (k i) c -> p k (i c)", k=2)
                    a.activation(dst, src, ACT.Gelu).then_inc(free(u), 1)

        @block.tensor
        def _(pe):
            t = nc.tensor

            def take(region, use):
                after(pe, S[f"{region}_free"], use)

            def take_slot(s_, i, step):
                if s_ == 2:
                    after(pe, S["pvc_read"], attentions_done(2, i))
                take(f"slot{s_}", before(f"slot{s_}", step, i))

            def all_maxima_taken(kind, i):
                for s_ in sorted({maxima_slot(kind, g_, i, NB) for g_ in range(8)}):
                    apart(pe, free(s_), before(f"slot{s_}", (kind, 7), i) + (s_ == maxima_slot(kind, 7, i, NB)))

            def a1(b, i, k):
                take("slot0", before("slot0", ("A1", 0), i))
                if isinstance(b, int) and b == 0:
                    pe.wait_ge(S["load_w0"], 16 * 7)
                pe.wait_ge(S["load_a"], 64 * b + 64)
                ps = slot[0]
                t.matmul(ps[:, D:2 * D], wk0_sb[:], ctx_a[:], start=True, stop=True)
                pe.wait_ge(S["norm_a"], b + 1)
                t.matmul(ps[:, 0:D], wq0_sb[:], normed["a"][:], start=True, stop=True).then_inc(full(0), 1)

            def va(b, i, k):
                take("misc", before("misc", ("VA", 0), i))
                if isinstance(b, int) and b == 0:
                    pe.wait_ge(S["const_pool"], 2)
                for st in range(2):
                    o = misc[:, st * P:(st + 1) * P]
                    t.matmul(o, ctx_a[:, st * P:(st + 1) * P], wv0_sb[:], start=True, stop=False)
                    last = t.matmul(o, ones[0:1, :], bv0_sb[:], start=False, stop=True)
                last.then_inc(S["misc_full"], 1)

            def c0(b, i, k):
                take("misc", before("misc", ("C0", 0), i))
                pe.wait_ge(S["load_c"], 48 * b + 48)
                for k in range(KT):
                    t.transpose(misc[:, (2 + k) * P:(3 + k) * P], ctx_c[:, k * P:(k + 1) * P], ident[:])
                pe.wait_ge(S["norm_c"], b + 1)
                for k in range(KT):
                    last = t.transpose(misc[:, k * P:(k + 1) * P], normed["c"][:, k * P:(k + 1) * P], ident[:])
                last.then_inc(S["misc_full"], 1)

            def c1(b, i, k):
                take_slot(2, i, ("C1", 0))
                pe.wait_ge(S["misc_free"], before("misc", ("C0", 0), i) + 1)
                if isinstance(b, int) and b == 0:
                    pe.wait_ge(S["load_w1"], 16 * 7)
                for x_, w, src in ((0, wq1_sb, 0), (1, wk1_sb, 0), (2, wk1_sb, 2)):
                    for mt in range(2):
                        at = (2 * x_ + mt) * P
                        for k in range(KT):
                            last = t.matmul(slot[2][:, at:at + P], w[:, k, mt * P:(mt + 1) * P], nT[:, src + k, :],
                                            start=(k == 0), stop=(k == KT - 1))
                last.then_inc(full(2), 1)

            def vc(b, i, k):
                take("misc", before("misc", ("VC", 0), i))
                for x_, src in ((0, 0), (1, 2)):
                    for k in range(KT):
                        last = t.matmul(misc[:, x_ * D:(x_ + 1) * D], nT[:, src + k, :], wv1_sb[:, k, :],
                                        start=(k == 0), stop=(k == KT - 1))
                last.then_inc(S["misc_full"], 1)

            def f0(b, i, k):
                take("misc", before("misc", ("F0", 0), i))
                pe.wait_ge(S["norm_f"], b + 1)
                for k in range(KT):
                    last = t.transpose(misc[:, k * P:(k + 1) * P], normed["f"][:, k * P:(k + 1) * P], ident[:])
                last.then_inc(S["misc_full"], 1)

            def f1(b, i, k):
                n = before("misc", ("F1", 0), i)
                take("misc", n)
                if isinstance(b, int) and b == 0:
                    pe.wait_ge(S["load_gu"], 16 * 4)
                for k in range(KT):
                    last = t.matmul(misc[:, 0:E0], n1T[:, k, :], gate0_sb[:, k, :], start=(k == 0), stop=(k == KT - 1))
                last.then_inc(S["misc_full"], 1)

            def g_(b, i, n):
                c, half_ = n // 2, n % 2
                s_ = c % 2
                if half_ == 0:
                    take(f"slot{s_}", before(f"slot{s_}", ("G", n), i))
                for k in range(KT):
                    rhs = gu_sb[:, k, 4 * c + 2 * half_:4 * c + 2 * half_ + 2, :].rearrange("p e f -> p (e f)")
                    last = t.matmul(slot[s_][:, 512 * half_:512 * half_ + 512], n1T[:, k, :], rhs,
                                    start=(k == 0), stop=(k == KT - 1))
                if half_ == 1:
                    last.then_inc(full(s_), 1)

            def t_(b, i, c):
                take("misc", before("misc", ("T", c), i))
                pe.wait_ge(S["inter_s"], 4 * b + c + 1)
                for e in range(4):
                    last = t.transpose(misc[:, e * P:(e + 1) * P], inter[:, c % 2, e, :], ident[:])
                last.then_inc(S["misc_full"], 1)

            def d_(b, i, c):
                if c == 0:
                    pe.wait_ge(S["pva_read"], b + 1)
                pe.wait_ge(S["misc_free"], before("misc", ("T", c), i) + 1)
                for e in range(4):
                    last = t.matmul(pv0[:, 0:D], interT[:, c % 2, e, :], dn_sb[:, 4 * c + e, :],
                                    start=(c == 0 and e == 0), stop=(c == 3 and e == 3))
                last.then_inc(S["dn_chunk"], 1)

            def m_(b, i, g_):
                if g_ == 0:
                    pe.wait_ge(S["qk0_ld"], 64 * b + 64)
                    pe.wait_ge(S["mask0_ld"], 32 * b + 32)
                    if isinstance(b, int) and b == 0:
                        pe.wait_ge(S["ones_row0"], 16 * 4)
                hg, tt = g_ % 4, g_ // 4
                s_ = maxima_slot("M", g_, i, NB)
                take_slot(s_, i, ("M", g_))
                for u in range(4):
                    h = 4 * hg + u
                    last = t.matmul(slot[s_][:, u * D:(u + 1) * D], QS0[0:ROWS_MAX, h, tt * P:(tt + 1) * P],
                                    KS0[0:ROWS_MAX, h, :], start=True, stop=True)
                last.then_inc(full(s_), 1)

            def ma(b, i, k):
                take("misc", before("misc", ("MA", 0), i))
                all_maxima_taken("M", i)
                t.transpose(misc[0:32, 0:P], mx0[:].rearrange("p h s -> p (h s)"), ident[:]).then_inc(S["misc_full"], 1)

            def scores_with_mask(region, g_, which, lhs, rhs, rows):
                kind, r = g_ // 4, g_ % 4
                for hb in range(2):
                    if kind == 0:
                        for lo in range(2):
                            m = amask_p[:, lo, which, :].unsqueeze(1).broadcast_to([P, 4, P])
                            t.matmul(region[:, 512 * hb:512 * hb + 512], ident_r[:], m, start=(lo == 0), stop=(lo == 1))
                    for u in range(4):
                        h = 8 * r + 4 * hb + u
                        at = (4 * hb + u) * P
                        last = t.matmul(region[:, at:at + P], lhs[0:rows, h, :], rhs[0:rows, h, :], start=(kind == 1),
                                        stop=True, skip_group_check=True)
                return last

            def n_(b, i, g_):
                if g_ == 0:
                    pe.wait_ge(S["c_ld"], 144 * b + 144)
                    pe.wait_ge(S["amask_l"], b + 1)
                s_ = maxima_slot("N", g_, i, NB)
                take_slot(s_, i, ("N", g_))
                scores_with_mask(slot[s_], g_, 0, QS1, KS1 if g_ < 4 else AS1, ROWS_MAX).then_inc(full(s_), 1)

            def nc_(b, i, k):
                take("misc", before("misc", ("NC", 0), i))
                all_maxima_taken("N", i)
                t.transpose(misc[0:64, 0:P], mx1[:].rearrange("p k h -> p (k h)"), ident[:]).then_inc(S["misc_full"], 1)

            def a3(b, i, step):
                def values(g_):
                    r, hh, st = g_ // 4, (g_ // 2) % 2, g_ % 2
                    take(f"slot{g_ % 2}", before(f"slot{g_ % 2}", ("A3", g_), i) + 1)
                    if g_ == 0:
                        after(pe, S["x2_ready"], b)
                    for j in range(4):
                        last = t.matmul(pv0[32 * j:32 * j + 32, r * D:(r + 1) * D],
                                        vst0[:, st, 4 * r + j, 32 * hh:32 * hh + 32],
                                        p[:, g_ % 2, j * D:(j + 1) * D],
                                        start=(hh == 0 and st == 0), stop=(hh == 1 and st == 1))
                    last.then_inc(S["pvdone_a"], 1)

                if step == 0:
                    pe.wait_ge(S["m0_ld"], 16 * b + 16)
                    pe.wait_ge(S["v0_ready"], 4 * b + 4)
                if step < 8:
                    s_ = step % 2
                    r, hh, st = step // 4, (step // 2) % 2, step % 2
                    take(f"slot{s_}", before(f"slot{s_}", ("A3", step), i))
                    for j in range(4):
                        h = 8 * r + 2 * j + hh
                        last = t.matmul(slot[s_][:, j * D:(j + 1) * D], KS0[:, h, st * P:(st + 1) * P], QS0[:, h, :],
                                        start=True, stop=True)
                    last.then_inc(full(s_), 1)
                if step >= 1:
                    values(step - 1)

            def a4(b, i, k):
                take("misc", before("misc", ("A4", 0), i))
                if isinstance(b, int) and b == 0:
                    pe.wait_ge(S["const_pool"], 3)
                pe.wait_ge(S["o_a_s"], b + 1)
                t.matmul(misc[:, 0:D], sel[:], o_a[:, 1, :], start=True, stop=True).then_inc(S["misc_full"], 1)

            def c3(b, i, step):
                def values(g_):
                    kind, r = g_ // 4, g_ % 4
                    take(f"slot{g_ % 2}", before(f"slot{g_ % 2}", ("C3", g_), i) + 1)
                    vst, pv = (vst_s, pvs) if kind == 0 else (vst_x, pvx)
                    for hh in range(2):
                        for j in range(4):
                            last = t.matmul(pv[32 * j:32 * j + 32, r * P:(r + 1) * P],
                                            vst[:, 4 * r + j, 32 * hh:32 * hh + 32],
                                            p[:, g_ % 2, (2 * j + hh) * P:(2 * j + hh + 1) * P],
                                            start=(hh == 0), stop=(hh == 1))
                    last.then_inc(S["pvdone_c"], 1)

                if step == 0:
                    pe.wait_ge(S["m1_ld"], 16 * b + 16)
                    pe.wait_ge(S["vs_ready"], 2 * b + 2)
                    pe.wait_ge(S["vx_ready"], b + 1)
                if step < 8:
                    s_ = step % 2
                    take(f"slot{s_}", before(f"slot{s_}", ("C3", step), i))
                    scores_with_mask(slot[s_], step, 1, KS1 if step < 4 else AS1, QS1, P).then_inc(full(s_), 1)
                if step == 1:
                    take_slot(2, i, ("C3", 1))
                if step >= 1:
                    values(step - 1)

            def w_(b, i, k):
                take("misc", before("misc", ("W", 0), i))
                pe.wait_ge(S["o_c_s"], b + 1)
                for r in range(4):
                    last = t.matmul(misc[:, 0:D], o_c[:, r, :], wo1_sb[:, r, :], start=(r == 0), stop=(r == 3))
                last.then_inc(S["misc_full"], 1)

            def r0(b, i, k):
                take("misc", before("misc", ("R0", 0), i))
                pe.wait_ge(S["norm_e"], b + 1)
                for k in range(KT):
                    last = t.transpose(misc[:, k * P:(k + 1) * P], normed["e"][:, k * P:(k + 1) * P], ident[:])
                last.then_inc(S["misc_full"], 1)

            def r1(b, i, k):
                pe.wait_ge(S["misc_free"], before("misc", ("R0", 0), i) + 1)
                take("misc", before("misc", ("R1", 0), i))
                for k in range(KT):
                    last = t.matmul(misc[:, 0:E1], n3T[:, k, :], gate1w_sb[:, k, :], start=(k == 0), stop=(k == KT - 1))
                last.then_inc(S["misc_full"], 1)

            def r2(b, i, k):
                take("misc", before("misc", ("R2", 0), i))
                pe.wait_ge(S["onehot_s"], b + 1)
                after(pe, S["seen_s"], b)
                t.matmul(misc[:, 0:E1], tri[:], one_hot1[:], start=True, stop=False)
                t.matmul(misc[:, 0:E1], ones[:], seen[:], start=False, stop=True).then_inc(S["misc_full"], 1)

            iterations(pe, {"A1": a1, "VA": va, "C0": c0, "C1": c1, "VC": vc, "F0": f0, "F1": f1, "G": g_, "T": t_,
                            "D": d_, "M": m_, "MA": ma, "N": n_, "NC": nc_, "A3": a3, "A4": a4, "C3": c3, "W": w_,
                            "R0": r0, "R1": r1, "R2": r2})

            base = [all_uses(f"slot{k}", NB) for k in range(2)]
            for n, (s_, tiles, src) in enumerate(((0, 4, p[:, 0, :]), (1, 4, p[:, 1, :]),
                                                  (0, 2, rows_8.rearrange("p n h -> p (n h)")))):
                take(f"slot{s_}", base[s_] + n // 2)
                pe.wait_ge(S[f"disp_ld{n}"], 16)
                for k in range(tiles * KT):
                    last = t.transpose(slot[s_][:, k * P:(k + 1) * P], src[:, k * P:(k + 1) * P], ident[:])
                last.then_inc(full(s_), 1)

            def hidden(e):
                pe.wait_ge(S[f"load_wi{e % 4}"], 16 * (e // 4) + 16)
                for u in range(2):
                    take(f"slot{u}", base[u] + 2 - u + e)
                    for q in range(4):
                        at = 512 * (q // 2) + CAP * (q % 2)
                        for k in range(KT):
                            last = t.matmul(slot[u][:, at:at + CAP],
                                            wi_sb[e % 4][:, k, (4 * u + q) * P:(4 * u + q + 1) * P],
                                            dispT[:, k, e * CAP:(e + 1) * CAP], start=(k == 0), stop=(k == KT - 1))
                    last.then_inc(full(u), 1)

            def outputs(e):
                pe.wait_ge(S[f"load_wo{e % 4}"], 16 * (e // 4) + 16)
                for u in range(2):
                    take(f"slot{u}", base[u] + 2 - u + e + 1)
                after(pe, S["oT_ready"], e)
                for m in range(KT):
                    for k in range(IT1):
                        last = t.matmul(pv0[:, m * CAP:(m + 1) * CAP], wo_sb[e % 4][:, k, m * P:(m + 1) * P],
                                        hT[e % 2][:, k, :], start=(k == 0), stop=(k == IT1 - 1))
                last.then_inc(S["eo_full"], 1)

            def rows_back(e):
                pe.wait_ge(S["oT_ready"], e + 1)
                after(pe, S["eo_sb"], 2 * e)
                for c in range(2):
                    rows = P if c == 0 else CAP - P
                    for m in range(KT):
                        last = t.transpose(slot[2][0:rows, 512 * c + m * P:512 * c + (m + 1) * P],
                                           oT[e % 2][:, m, c * P:c * P + rows], ident[:])
                last.then_inc(S["eoT_full"], 1)

            for s_ in range(2):
                take(f"slot{s_}", base[s_] + 2 - s_)
            hidden(0)
            for e in range(E1):
                if e + 1 < E1:
                    hidden(e + 1)
                outputs(e)
                if e >= 1:
                    rows_back(e - 1)
            rows_back(E1 - 1)


def kernel(**inputs):
    import concourse.bacc as bacc
    from concourse.bass_utils import run_bass_kernel_spmd

    arr = {k: np.ascontiguousarray(v) for k, v in inputs.items()}
    nb, p, d = arr["x"].shape
    hd = 8

    def by_width(w):
        heads = w.shape[-1] // hd
        return np.ascontiguousarray(w.reshape(w.shape[:-1] + (heads, hd)).swapaxes(-1, -2).reshape(w.shape))

    wo_rows = np.empty((4, 4, 2, 16, d), np.float32)
    wo_rows[:] = arr["L1_xattn_Wo"].reshape(4, 4, 1, 16, d)

    inv = 1.0 / 10000.0 ** (np.arange(0, hd, 2, dtype=np.float32) / hd)
    ang = np.outer(np.arange(p, dtype=np.float32), inv)
    cos, sin = (np.repeat(f(ang).astype(np.float32).T, p // (hd // 2), axis=0) for f in (np.cos, np.sin))
    s = np.float32(1.0 / np.sqrt(hd))
    rope = np.stack([cos * s, cos * s, cos, cos, -sin * s, sin * s, -sin, sin], axis=1).astype(np.float32)

    mask = arr["mask_Bx1xSxS_fk0"][:, 0]
    feed = {
        "x": arr["x"], "ctx": arr["ctx_2048"], "mask01": arr["mask_Bx1x2048_fk1"],
        "mask01_cols": arr["mask_Bx1x2048_fk1"].reshape(nb, d // p, p).transpose(0, 2, 1),
        "addmask": mask, "addmaskT": mask.transpose(0, 2, 1),
        "wq0T": by_width(arr["L0_xattn_Wq"].T), "bq0": by_width(arr["L0_xattn_bq"]).reshape(-1, 1),
        "wk0T": by_width(arr["L0_xattn_Wk"].T), "bk0": by_width(arr["L0_xattn_bk"]).reshape(-1, 1),
        "wv0T": arr["L0_xattn_Wv"].T, "bv0": arr["L0_xattn_bv"].reshape(1, -1),
        "gate0T": arr["L0_ffn_gate_w"].T, "gate_up": arr["L0_ffn_gate_up_proj"], "down": arr["L0_ffn_down_proj"],
        "wq1": by_width(arr["L1_xattn_Wq"]), "wk1": by_width(arr["L1_xattn_Wk"]), "wv1": arr["L1_xattn_Wv"],
        "wo1": wo_rows.reshape(4, 128, d), "gate1": np.repeat(arr["L1_xattn_gate"].reshape(1, -1), hd, axis=1),
        "gate1wT": arr["L1_ffn_gate_weight"].T, "wi": arr["L1_ffn_wi"], "wo": arr["L1_ffn_wo"], "rope": rope,
    }
    nc = bacc.Bacc("TRN2", target_bir_lowering=False, num_devices=1)
    arrays, args = {}, []
    for name, a in feed.items():
        a = np.ascontiguousarray(a)
        arrays[f"in_{name}"] = a
        args.append(nc.dram_tensor(f"in_{name}", a.shape, mybir.dt.from_np(a.dtype), kind="ExternalInput").ap())
    args.append(nc.dram_tensor("out_x", (nb, p, d), mybir.dt.float32, kind="ExternalOutput").ap())
    two_layer_kernel(nc, *args)
    r = run_bass_kernel_spmd(nc, [arrays], core_ids=[0])
    return r.results[0]["out_x"]
```
